# Optimizing a Trainium2 kernel written in Bass

```python
import numpy as np
import jax
import jax.numpy as jnp

def _softmax(x, axis=-1):
    return jax.nn.softmax(x, axis=axis)

def _gelu(x):
    return jax.nn.gelu(x, approximate=True)

def _silu(x):
    return jax.nn.silu(x)

def _sigmoid(x):
    return jax.nn.sigmoid(x)

def _layernorm(x, axis=-1, eps=1e-05):
    m = jnp.mean(x, axis=axis, keepdims=True)
    v = jnp.var(x, axis=axis, keepdims=True)
    return (x - m) / jnp.sqrt(v + eps)

def _scatter_add(tgt, idx, src, axis=0):
    return tgt.at[idx].add(src)

def _segment_sum(src, seg, n):
    return jax.ops.segment_sum(src, seg, n)
kernel_name = 'mk_recurrent_d2_jaxref_r8_f5b4fe'

def setup_inputs(seed: int=0):
    np.random.seed(seed)
    _w = jnp.asarray

    def _L0_attn_setup():
        import jax, jax.numpy as jnp
        import numpy as np
        import math
        H = 16
        DN = 128
        DR = 64
        DV = 128
        ROPE_BASE = 10000.0

        def _rope_cos_sin(seq_len, dim, dtype):
            inv_freq = 1.0 / ROPE_BASE ** (jnp.arange(0, dim, 2, dtype=jnp.float32) / dim)
            t = jnp.arange(seq_len, dtype=jnp.float32)
            freqs = t[:, None] * inv_freq[None, :]
            return (jnp.cos(freqs).astype(dtype), jnp.sin(freqs).astype(dtype))

        def _apply_rope(x, cos, sin):
            half = x.shape[-1] // 2
            x1, x2 = (x[..., :half], x[..., half:])
            c = cos[None, :, None, :]
            s = sin[None, :, None, :]
            return jnp.concatenate([x1 * c - x2 * s, x1 * s + x2 * c], axis=-1)
        key = jax.random.key(seed)
        ks = jax.random.split(key, 5)
        hidden = 256
        B, S = (1, 256)
        q_size = H * (DN + DR)
        v_size = H * DV
        std = 0.02
        return {'hidden_states': jax.random.normal(ks[0], (B, S, hidden), jnp.float32), 'Wq': jax.random.normal(ks[1], (q_size, hidden), jnp.float32) * std, 'Wk': jax.random.normal(ks[2], (q_size, hidden), jnp.float32) * std, 'Wv': jax.random.normal(ks[3], (v_size, hidden), jnp.float32) * std, 'Wo': jax.random.normal(ks[4], (hidden, v_size), jnp.float32) * std}
    _L0_attn_in = _L0_attn_setup()

    def _L0_ffn_setup():
        import jax, jax.numpy as jnp
        import numpy as np
        DIM = 256
        HID = 704
        ZERO_POINT = 128.0

        def _qlinear(x, wq, scale):
            W = (wq.astype(jnp.float32) - ZERO_POINT) * scale[:, None]
            return jnp.einsum('bsd,hd->bsh', x, W)
        key = jax.random.key(seed)
        ks = jax.random.split(key, 7)
        B, S = (4, 256)
        sg = jax.random.uniform(ks[1], (HID,)) * (0.02 / np.sqrt(DIM)) + 0.0001
        su = jax.random.uniform(ks[3], (HID,)) * (0.02 / np.sqrt(DIM)) + 0.0001
        sd = jax.random.uniform(ks[5], (DIM,)) * (0.02 / np.sqrt(HID)) + 0.0001
        return {'x': jax.random.normal(ks[0], (B, S, DIM), dtype=jnp.float32), 'wq_gate': jax.random.randint(ks[2], (HID, DIM), 0, 32, dtype=jnp.int32), 's_gate': sg, 'wq_up': jax.random.randint(ks[4], (HID, DIM), 0, 32, dtype=jnp.int32), 's_up': su, 'wq_down': jax.random.randint(ks[6], (DIM, HID), 0, 32, dtype=jnp.int32), 's_down': sd}
    _L0_ffn_in = _L0_ffn_setup()

    def _L1_attn_setup():
        import jax, jax.numpy as jnp
        import numpy as np
        EPS = 1e-06

        def rmsnorm(t, w):
            var = jnp.mean(t * t, axis=-1, keepdims=True)
            return t * jax.lax.rsqrt(var + EPS) * w
        key = jax.random.key(seed)
        ks = jax.random.split(key, 6)
        B, L, dim, H = (2, 256, 256, 16)
        D = dim // H
        x = jax.random.normal(ks[0], (B, L, dim), dtype=jnp.float32)
        w_qkv = jax.random.normal(ks[1], (3 * dim, dim), dtype=jnp.float32) * dim ** (-0.5)
        q_norm_w = jnp.ones((D,), dtype=jnp.float32)
        k_norm_w = jnp.ones((D,), dtype=jnp.float32)
        w_proj = jax.random.normal(ks[2], (dim, dim), dtype=jnp.float32) * dim ** (-0.5)
        b_proj = jnp.zeros((dim,), dtype=jnp.float32)
        return {'x': x, 'w_qkv': w_qkv, 'q_norm_w': q_norm_w, 'k_norm_w': k_norm_w, 'w_proj': w_proj, 'b_proj': b_proj}
    _L1_attn_in = _L1_attn_setup()

    def _L1_ffn_setup():
        import jax, jax.numpy as jnp
        import numpy as np
        B, S, H, I, E, TOP_K, NS = (2, 256, 256, 176, 8, 2, 2)
        SI = I * NS
        INIT = 0.02
        key = jax.random.key(seed)
        ks = jax.random.split(key, 9)
        f32 = jnp.float32
        return {'hidden_states': jax.random.normal(ks[0], (B, S, H), f32), 'router_w': jax.random.normal(ks[1], (E, H), f32) * INIT, 'gate_w': jax.random.normal(ks[2], (E, H, I), f32) * INIT, 'up_w': jax.random.normal(ks[3], (E, H, I), f32) * INIT, 'down_w': jax.random.normal(ks[4], (E, I, H), f32) * INIT, 's_gate_w': jax.random.normal(ks[5], (H, SI), f32) * INIT, 's_gate_b': jnp.zeros((SI,), f32), 's_up_w': jax.random.normal(ks[6], (H, SI), f32) * INIT, 's_up_b': jnp.zeros((SI,), f32), 's_down_w': jax.random.normal(ks[7], (SI, H), f32) * INIT, 's_down_b': jnp.zeros((H,), f32)}
    _L1_ffn_in = _L1_ffn_setup()
    _d = {'L0_attn_hidden_states': _L0_attn_in['hidden_states'], 'L0_attn_Wq': _L0_attn_in['Wq'], 'L0_attn_Wk': _L0_attn_in['Wk'], 'L0_attn_Wv': _L0_attn_in['Wv'], 'L0_attn_Wo': _L0_attn_in['Wo'], 'L0_ffn_wq_gate': _L0_ffn_in['wq_gate'], 'L0_ffn_s_gate': _L0_ffn_in['s_gate'], 'L0_ffn_wq_up': _L0_ffn_in['wq_up'], 'L0_ffn_s_up': _L0_ffn_in['s_up'], 'L0_ffn_wq_down': _L0_ffn_in['wq_down'], 'L0_ffn_s_down': _L0_ffn_in['s_down'], 'L1_attn_w_qkv': _L1_attn_in['w_qkv'], 'L1_attn_q_norm_w': _L1_attn_in['q_norm_w'], 'L1_attn_k_norm_w': _L1_attn_in['k_norm_w'], 'L1_attn_w_proj': _L1_attn_in['w_proj'], 'L1_attn_b_proj': _L1_attn_in['b_proj'], 'L1_ffn_router_w': _L1_ffn_in['router_w'], 'L1_ffn_gate_w': _L1_ffn_in['gate_w'], 'L1_ffn_up_w': _L1_ffn_in['up_w'], 'L1_ffn_down_w': _L1_ffn_in['down_w'], 'L1_ffn_s_gate_w': _L1_ffn_in['s_gate_w'], 'L1_ffn_s_gate_b': _L1_ffn_in['s_gate_b'], 'L1_ffn_s_up_w': _L1_ffn_in['s_up_w'], 'L1_ffn_s_up_b': _L1_ffn_in['s_up_b'], 'L1_ffn_s_down_w': _L1_ffn_in['s_down_w'], 'L1_ffn_s_down_b': _L1_ffn_in['s_down_b']}
    _x0 = _d['L0_attn_hidden_states']
    _d['L0_attn_hidden_states'] = jax.random.normal(jax.random.fold_in(jax.random.key(seed), 1), (8, 256, 256), dtype=_x0.dtype)
    del _x0
    return _d

def reference(L0_attn_hidden_states, L0_attn_Wq, L0_attn_Wk, L0_attn_Wv, L0_attn_Wo, L0_ffn_wq_gate, L0_ffn_s_gate, L0_ffn_wq_up, L0_ffn_s_up, L0_ffn_wq_down, L0_ffn_s_down, L1_attn_w_qkv, L1_attn_q_norm_w, L1_attn_k_norm_w, L1_attn_w_proj, L1_attn_b_proj, L1_ffn_router_w, L1_ffn_gate_w, L1_ffn_up_w, L1_ffn_down_w, L1_ffn_s_gate_w, L1_ffn_s_gate_b, L1_ffn_s_up_w, L1_ffn_s_up_b, L1_ffn_s_down_w, L1_ffn_s_down_b):

    def _L0_attn_ref(hidden_states, Wq, Wk, Wv, Wo):
        import jax, jax.numpy as jnp
        import numpy as np
        import math
        H = 16
        DN = 128
        DR = 64
        DV = 128
        ROPE_BASE = 10000.0

        def _rope_cos_sin(seq_len, dim, dtype):
            inv_freq = 1.0 / ROPE_BASE ** (jnp.arange(0, dim, 2, dtype=jnp.float32) / dim)
            t = jnp.arange(seq_len, dtype=jnp.float32)
            freqs = t[:, None] * inv_freq[None, :]
            return (jnp.cos(freqs).astype(dtype), jnp.sin(freqs).astype(dtype))

        def _apply_rope(x, cos, sin):
            half = x.shape[-1] // 2
            x1, x2 = (x[..., :half], x[..., half:])
            c = cos[None, :, None, :]
            s = sin[None, :, None, :]
            return jnp.concatenate([x1 * c - x2 * s, x1 * s + x2 * c], axis=-1)
        B, S, _ = hidden_states.shape
        q = hidden_states @ Wq.T
        k = hidden_states @ Wk.T
        v = hidden_states @ Wv.T
        q_nope = q[:, :, :H * DN].reshape(B, S, H, DN)
        q_rope = q[:, :, H * DN:].reshape(B, S, H, DR)
        k_nope = k[:, :, :H * DN].reshape(B, S, H, DN)
        k_rope = k[:, :, H * DN:].reshape(B, S, H, DR)
        v = v.reshape(B, S, H, DV)
        cos, sin = _rope_cos_sin(S, DR, hidden_states.dtype)
        q_rope = _apply_rope(q_rope, cos, sin)
        k_rope = _apply_rope(k_rope, cos, sin)
        scores = jnp.einsum('bqhd,bkhd->bhqk', q_nope, k_nope) / math.sqrt(DN) + jnp.einsum('bqhd,bkhd->bhqk', q_rope, k_rope) / math.sqrt(DR)
        attn = jax.nn.softmax(scores, axis=-1)
        out = jnp.einsum('bhqk,bkhd->bqhd', attn, v)
        out = out.reshape(B, S, H * DV)
        return out @ Wo.T

    def _L0_ffn_ref(x, wq_gate, s_gate, wq_up, s_up, wq_down, s_down):
        import jax, jax.numpy as jnp
        import numpy as np
        DIM = 256
        HID = 704
        ZERO_POINT = 128.0

        def _qlinear(x, wq, scale):
            W = (wq.astype(jnp.float32) - ZERO_POINT) * scale[:, None]
            return jnp.einsum('bsd,hd->bsh', x, W)
        gate = _qlinear(x, wq_gate, s_gate)
        gate = jax.nn.silu(gate)
        up = _qlinear(x, wq_up, s_up)
        return _qlinear(gate * up, wq_down, s_down)

    def _L1_attn_ref(x, w_qkv, q_norm_w, k_norm_w, w_proj, b_proj):
        import jax, jax.numpy as jnp
        import numpy as np
        EPS = 1e-06

        def rmsnorm(t, w):
            var = jnp.mean(t * t, axis=-1, keepdims=True)
            return t * jax.lax.rsqrt(var + EPS) * w
        B, L, dim = x.shape
        H = 16
        D = dim // H
        qkv = jnp.einsum('bld,ed->ble', x, w_qkv)
        qkv = qkv.reshape(B, L, 3, H, D).transpose(2, 0, 3, 1, 4)
        q, k, v = (qkv[0], qkv[1], qkv[2])
        q = rmsnorm(q, q_norm_w)
        k = rmsnorm(k, k_norm_w)
        scale = D ** (-0.5)
        scores = jnp.einsum('bhqd,bhkd->bhqk', q, k) * scale
        attn = jax.nn.softmax(scores, axis=-1)
        out = jnp.einsum('bhqk,bhkd->bhqd', attn, v)
        out = out.transpose(0, 2, 1, 3).reshape(B, L, dim)
        return jnp.einsum('bld,ed->ble', out, w_proj) + b_proj

    def _L1_ffn_ref(hidden_states, router_w, gate_w, up_w, down_w, s_gate_w, s_gate_b, s_up_w, s_up_b, s_down_w, s_down_b):
        import jax, jax.numpy as jnp
        import numpy as np
        B, S, H, I, E, TOP_K, NS = (2, 256, 256, 176, 8, 2, 2)
        SI = I * NS
        INIT = 0.02
        b, s, h = hidden_states.shape
        x = hidden_states.reshape(-1, h)
        T = x.shape[0]
        num_experts = router_w.shape[0]
        logits = x @ router_w.T
        probs = jax.nn.softmax(logits.astype(jnp.float32), axis=-1)
        topk_w, topk_idx = jax.lax.top_k(probs, TOP_K)
        topk_w = topk_w / jnp.sum(topk_w, axis=-1, keepdims=True)
        combine = jnp.zeros((T, num_experts), probs.dtype)
        combine = combine.at[jnp.arange(T)[:, None], topk_idx].add(topk_w)

        def expert_step(acc, ws):
            gw, uw, dw, ce = ws
            out = jax.nn.silu(x @ gw) * (x @ uw) @ dw
            return (acc + ce[:, None].astype(out.dtype) * out, None)
        moe_out, _ = jax.lax.scan(expert_step, jnp.zeros_like(x), (gate_w, up_w, down_w, combine.T))
        shared = jax.nn.silu(x @ s_gate_w + s_gate_b) * (x @ s_up_w + s_up_b) @ s_down_w + s_down_b
        return (moe_out + shared).reshape(b, s, h)
    x = L0_attn_hidden_states
    xn = _layernorm(x, axis=-1)
    s = _L0_attn_ref(xn, L0_attn_Wq, L0_attn_Wk, L0_attn_Wv, L0_attn_Wo)
    g = _silu(_L0_ffn_ref(xn, L0_ffn_wq_gate, L0_ffn_s_gate, L0_ffn_wq_up, L0_ffn_s_up, L0_ffn_wq_down, L0_ffn_s_down))
    x = x + s * g
    xn = _layernorm(x, axis=-1)
    s = _L1_attn_ref(xn, L1_attn_w_qkv, L1_attn_q_norm_w, L1_attn_k_norm_w, L1_attn_w_proj, L1_attn_b_proj)
    g = _silu(_L1_ffn_ref(xn, L1_ffn_router_w, L1_ffn_gate_w, L1_ffn_up_w, L1_ffn_down_w, L1_ffn_s_gate_w, L1_ffn_s_gate_b, L1_ffn_s_up_w, L1_ffn_s_up_b, L1_ffn_s_down_w, L1_ffn_s_down_b))
    x = x + s * g
    return x

_drawn_inputs = setup_inputs


def setup_inputs(seed=0):
    import zlib

    import numpy as np

    out = dict(_drawn_inputs(seed))
    spreads = {'L1_attn_q_norm_w': (1.0, 0.6),
     'L1_attn_k_norm_w': (1.0, 0.6),
     'L1_attn_b_proj': (0.0, 0.8),
     'L1_ffn_s_gate_b': (0.0, 0.8),
     'L1_ffn_s_up_b': (0.0, 0.8),
     'L1_ffn_s_down_b': (0.0, 0.8)}
    factors = {'L0_attn_Wq': 8.0,
     'L0_attn_Wk': 8.0,
     'L0_attn_Wv': 8.0,
     'L0_attn_Wo': 8.0,
     'L0_ffn_s_gate': 8.0,
     'L0_ffn_s_up': 8.0,
     'L0_ffn_s_down': 8.0,
     'L1_attn_w_qkv': 8.0,
     'L1_attn_w_proj': 8.0,
     'L1_ffn_router_w': 8.0,
     'L1_ffn_gate_w': 8.0,
     'L1_ffn_up_w': 8.0,
     'L1_ffn_down_w': 8.0,
     'L1_ffn_s_gate_w': 8.0,
     'L1_ffn_s_up_w': 8.0,
     'L1_ffn_s_down_w': 8.0}
    for name, (base, spread) in spreads.items():
        noise = np.random.default_rng([zlib.crc32(name.encode()), seed]).standard_normal(out[name].shape)
        drawn = base * np.exp(spread * noise) if base else spread * noise
        out[name] = jnp.asarray(drawn.astype(out[name].dtype))
    for name, factor in factors.items():
        out[name] = (out[name] * factor).astype(out[name].dtype)
    return out
```

```python
from contextlib import ExitStack
import math

import concourse.bass as bass
from concourse import mybir

F32 = mybir.dt.float32
F32R = mybir.dt.float32r
I32 = mybir.dt.int32
ALU = mybir.AluOpType
ACT = mybir.ActivationFunctionType
AX = mybir.AxisListType

P = 128
D = 256
KC = D // P
NTOK, SEQ, BATCH = 2048, 256, 8
NT = NTOK // P
STEP = 512
NSTEP = NTOK // STEP
TT = STEP // P
H, DN, DR, DV = 16, 128, 64, 128
HG = 4
NG = H // HG
HALF = DR // 2
HID = 704
HT = 6
HREST = HID - (HT - 1) * P
H1, D1 = 16, 16
E, I1 = 8, 176
SI = 2 * I1
MW = E * I1 + SI
MT = 14
ME = E * I1 // P
MREST = MW - (MT - 1) * P
LN_EPS, RMS_EPS = 1e-5, 1e-6
SCALE0 = 1.0 / math.sqrt(DN)
SCALE1 = D1 ** -0.5
CREDIT = 2

W_Q, W_K, W_V, W_R, W_O, W_END = 0, 1024, 2048, 3072, 4096, 5120


def product(pe, out, lhs, rhs, first, last):
    (lh, ll), (rh, rl) = lhs, rhs
    pe.matmul(out, lh, rh, start=first, stop=False)
    pe.matmul(out, lh, rl, start=False, stop=False)
    return pe.matmul(out, ll, rh, start=False, stop=last)


class Names:

    def __init__(self, nc, ctx, prefix):
        self.nc, self.ctx, self.prefix = nc, ctx, prefix

    def sb(self, name, shape, dt=F32):
        return self.ctx.enter_context(self.nc.sbuf_tensor(self.prefix + name, shape, dt))

    def ps(self, name, shape=(P, 512)):
        return self.ctx.enter_context(self.nc.psum_tensor(self.prefix + name, list(shape), F32))

    def sem(self, name):
        return self.ctx.enter_context(self.nc.semaphore(self.prefix + name))


def norm_stats(dve, own, seen, k, xt, stats, mv, var_eps, tiles, eps):
    for t in range(tiles):
        dve.bn_stats(stats[:, t, :], xt[:, t, :]).then_inc(own, 1)
    dve.wait_ge(own, k + tiles)
    dve.sem_inc(seen, 1)
    for t in range(tiles):
        dve.bn_aggr(mv[:, t, :], stats[:, t, :]).then_inc(own, 1)
    dve.wait_ge(own, k + 2 * tiles)
    dve.tensor_scalar(var_eps, mv[:, 0:tiles, 1], eps, None, ALU.add).then_inc(own, 1)
    return k + 2 * tiles + 1


def polish_rsqrt(dve, own, k, r, v, tmp):
    dve.tensor_tensor(tmp, r, r, ALU.mult).then_inc(own, 1)
    dve.wait_ge(own, k + 1)
    dve.tensor_tensor(tmp, tmp, v, ALU.mult).then_inc(own, 1)
    dve.wait_ge(own, k + 2)
    dve.tensor_scalar(tmp, tmp, -0.5, 1.5, ALU.mult, ALU.add).then_inc(own, 1)
    dve.wait_ge(own, k + 3)
    dve.tensor_tensor(r, r, tmp, ALU.mult).then_inc(own, 1)
    dve.wait_ge(own, k + 4)
    return k + 4


def stage_norm0(nc, x, ident_in, xn_dram):
    with ExitStack() as ctx:
        n = Names(nc, ctx, "n0_")
        xt = n.sb("x", [P, NT, D])
        xn = n.sb("xn", [P, 2, TT, D])
        ident = n.sb("ident", [P, P])
        stats = n.sb("stats", [P, TT, 6])
        mv = n.sb("mv", [P, TT, 2])
        ve = n.sb("ve", [P, 2, TT])
        rs = n.sb("rs", [P, 2, TT])
        tmp = n.sb("tmp", [P, TT])
        mhalf = n.sb("mhalf", [P, TT])
        xs = n.sb("xs", [P, 2, 2, KC, STEP], F32R)
        bank = [n.ps(f"bank{i}") for i in range(2)]
        x_in = [n.sem(f"x_in{s}") for s in range(NSTEP)]
        id_in, own, stats_seen, ve_ready, rs_ready, mhalf_ready = (n.sem(s) for s in ("id_in", "own", "stats_seen", "ve_ready", "rs_ready", "mhalf_ready"))
        xn_ready, turned, hi_ready, lo_ready = (n.sem(s) for s in ("xn_ready", "turned", "hi_ready", "lo_ready"))
        stored = [n.sem(f"stored{i}") for i in range(2)]

        with nc.Block() as block:
            @block.sync
            def _(sp):
                sp.dma_start(ident[:, :], ident_in).then_inc(id_in, 16)
                for s in range(NSTEP):
                    sp.dma_start(xt[:, TT * s:TT * (s + 1), :],
                                 x[STEP * s:STEP * (s + 1), :].rearrange("(t p) d -> p t d", p=P)).then_inc(x_in[s], 16)
                for s in range(NSTEP):
                    sp.wait_ge(lo_ready, 2 * s + 2)
                    sp.dma_start(xn_dram[s], xs[:, s % 2].bitcast(F32)).then_inc(stored[s % 2], 16)
                for i in range(2):
                    sp.wait_ge(stored[i], 16 * NSTEP // 2)

            @block.gpsimd
            def _(pool):
                pool.memset(mhalf[:, :], -0.5).then_inc(mhalf_ready, 1)
                pool.wait_ge(mhalf_ready, 1)
                for s in range(NSTEP):
                    pool.wait_ge(ve_ready, s + 1)
                    pool.tensor_tensor(rs[:, s % 2, :], ve[:, s % 2, :], mhalf[:, :], ALU.pow).then_inc(rs_ready, 1)

            @block.vector
            def _(dve):
                k = 0
                for s in range(NSTEP):
                    dve.wait_ge(x_in[s], 16)
                    k = norm_stats(dve, own, stats_seen, k, xt[:, TT * s:TT * (s + 1), :], stats, mv, ve[:, s % 2, :], TT, LN_EPS)
                    dve.wait_ge(own, k)
                    dve.sem_inc(ve_ready, 1)
                    dve.wait_ge(rs_ready, s + 1)
                    k = polish_rsqrt(dve, own, k, rs[:, s % 2, :], ve[:, s % 2, :], tmp[:, :])
                    if s >= 2:
                        dve.wait_ge(turned, 2 * (s - 1))
                    for t in range(TT):
                        i = dve.tensor_scalar(xn[:, s % 2, t, :], xt[:, TT * s + t, :], mv[:, t, 0:1],
                                              rs[:, s % 2, t:t + 1], ALU.subtract, ALU.mult)
                    i.then_inc(xn_ready, 1)
                    for c in range(KC):
                        dve.wait_ge(hi_ready, 2 * s + c + 1)
                        dve.tensor_tensor(xs[:, s % 2, 1, c, :], bank[c][:, :], xs[:, s % 2, 0, c, :], ALU.subtract)\
                           .then_inc(lo_ready, 1)

            @block.tensor
            def _(pe):
                pe.wait_ge(id_in, 16)
                for s in range(NSTEP):
                    pe.wait_ge(xn_ready, s + 1)
                    for c in range(KC):
                        if s >= 1:
                            pe.wait_ge(lo_ready, 2 * (s - 1) + c + 1)
                        for t in range(TT):
                            i = pe.transpose(bank[c][:, t * P:(t + 1) * P], xn[:, s % 2, t, c * P:(c + 1) * P], ident[:, :])
                        i.then_inc(turned, 1)

            @block.scalar
            def _(act):
                for s in range(NSTEP):
                    if s >= 2:
                        act.wait_ge(stored[s % 2], 16 * (s // 2))
                    for c in range(KC):
                        act.wait_ge(turned, 2 * s + c + 1)
                        act.activation(xs[:, s % 2, 0, c, :], bank[c][:, :], ACT.Copy).then_inc(hi_ready, 1)


def stage_attention0(nc, weights, tables, ident_in, xn_dram, sacc):
    UN = 2 * HG
    JR, JV, JO, JN0, JS, JP = 6, 10, 14, 16, 18, 10
    HI, HP = 12, 6
    with ExitStack() as ctx:
        n = Names(nc, ctx, "a0_")
        ident = n.sb("ident", [P, P])
        tab = n.sb("tab", [P, 4, STEP])
        raw = n.sb("raw", [P, W_END])
        wh, wl = n.sb("wh", [P, W_END], F32R), n.sb("wl", [P, W_END], F32R)
        xs = n.sb("xs", [P, 2, KC, STEP], F32R)
        rot = [n.sb("rotq", [P, 4, STEP]), n.sb("rotk", [P, 4, STEP])]
        sq = n.sb("sq", [P, HG, STEP], F32R)
        sk = n.sb("sk", [P, 2, HG, STEP], F32R)
        qn = n.sb("qn", [P, 2, 2, STEP], F32R)
        kn = n.sb("kn", [P, 2, 2, STEP], F32R)
        v = n.sb("v", [P, 2, TT, HG * DV], F32R)
        pr = n.sb("pr", [P, 2, 2, SEQ])
        pt = n.sb("pt", [P, 2, 2, 512], F32R)
        ot = n.sb("ot", [P, 2, HG, STEP], F32R)
        mx = n.sb("mx", [P, 2, 2])
        nb = n.sb("nb", [P, 2, 2])
        sm = n.sb("sm", [P, 2, 2])
        ri = n.sb("ri", [P, 2, 2])
        PJ = [n.ps(f"job{i}") for i in range(2)]
        PS = [n.ps(f"score{i}") for i in range(2)]
        PT = [n.ps(f"turn{i}") for i in range(2)]
        PO = [n.ps(f"out{i}") for i in range(2)]
        STACKS = 16 * 10
        stack_in = [n.sem(f"stack_in{j}") for j in range(HG)]
        S = {s: n.sem(s) for s in (
            "const_in", "w_in", "w_hi", "w_lo_d", "w_lo_p", "x_in", "job_full", "job_free", "job_hi", "rot_mul",
            "rot_add", "rot_hi", "rot_lo", "score_full", "score_free", "max_raw", "max_ready", "exp_ready",
            "sum_inv", "norm_ready", "turn_full", "turn_free", "turn_hi", "pv_done", "out_hi", "out_free", "zeroed", "wl_p")}

        def w(part, a, b):
            return (wh, wl)[part][:, a:b]

        def w2(a, b):
            return w(0, a, b), w(1, a, b)

        def x2(c, a, b):
            return xs[:, 0, c, a:b], xs[:, 1, c, a:b]

        with nc.Block() as block:
            @block.sync
            def _(sp):
                sp.dma_start(ident[:, :], ident_in).then_inc(S["const_in"], 16)
                sp.dma_start(tab[:, :, :], tables).then_inc(S["const_in"], 16)
                def load_x(b):
                    sp.dma_start(xs[:, :, :, :].bitcast(F32).rearrange("p s c n -> p (s c n)"),
                                 xn_dram[bass.ds(b, 1)].rearrange("o p s c n -> p (o s c n)")).then_inc(S["x_in"], 16)

                def load_weights(g):
                    sp.dma_start(raw[:, :], weights[bass.ds(g, 1)].rearrange("o p n -> p (o n)")).then_inc(S["w_in"], 16)

                def stack(st):
                    sp.wait_ge(S["score_full"], st * UN)
                    sp.wait_ge(S["rot_lo"], st * 2 + 2)
                    for j in range(HG):
                        rows = slice(HALF * j, HALF * (j + 1))
                        for r in range(2):
                            for part in range(2):
                                slot = 2 + r if part == 0 else r
                                at = HALF * (2 * part + r)
                                sp.dma_start(sq[at:at + HALF, j, :].bitcast(F32), rot[0][rows, slot, :]).then_inc(stack_in[j], 16)
                                for dup in range(2 - part):
                                    at = HALF * (2 * dup + r)
                                    sp.dma_start(sk[at:at + HALF, part, j, :].bitcast(F32), rot[1][rows, slot, :])\
                                      .then_inc(stack_in[j], 16)

                def step(g, b, next_b):
                    st = g * NSTEP + b
                    sp.wait_ge(S["job_full"], JP + st * JS + JR)
                    load_x(next_b)
                    stack(st + 1)

                load_x(0)
                load_weights(0)
                stack(0)
                with sp.Fori(0, NG) as g:
                    sp.wait_ge(S["w_lo_d"], (g + 1) * 3)
                    load_weights((g + 1) % NG)
                    with sp.Fori(0, NSTEP - 1) as b:
                        step(g, b, b + 1)
                    step(g, NSTEP - 1, 0)
                for j in range(HG):
                    sp.wait_ge(stack_in[j], STACKS * (NG * NSTEP + 1))
                sp.wait_ge(S["x_in"], 16 * (NG * NSTEP + 1))
                sp.wait_ge(S["w_in"], 16 * (NG + 1))

            @block.gpsimd
            def _(pool):
                def split_weights(g):
                    for i in (1, 3):
                        pool.wait_ge(S["w_hi"], 5 * g + i + 1)
                        pool.tensor_tensor(w(1, 1024 * i, 1024 * i + 1024), raw[:, 1024 * i:1024 * i + 1024],
                                           w(0, 1024 * i, 1024 * i + 1024), ALU.subtract).then_inc(S["w_lo_p"], 1)

                def rotate(st):
                    for q in range(2):
                        r = rot[q]
                        pool.wait_ge(S["rot_mul"], st * 2 + q + 1)
                        pool.tensor_tensor(r[:, 0, :], r[:, 0, :], r[:, 2, :], ALU.subtract).then_inc(S["rot_add"], 1)
                        pool.tensor_tensor(r[:, 1, :], r[:, 1, :], r[:, 3, :], ALU.add).then_inc(S["rot_add"], 1)
                        pool.wait_ge(S["rot_hi"], st * 2 + q + 1)
                        pool.tensor_tensor(r[:, 0:2, :].bitcast(F32R), r[:, 0:2, :], r[:, 2:4, :],
                                           ALU.subtract).then_inc(S["rot_lo"], 1)

                split_weights(0)
                rotate(0)
                with pool.Fori(0, NG) as g:
                    with pool.Fori(0, NSTEP - 1) as b:
                        rotate(g * NSTEP + b + 1)
                    split_weights(g + 1)
                    rotate((g + 1) * NSTEP)

            @block.scalar
            def _(act):
                def split_weights(g, chunks):
                    for i in chunks:
                        act.activation(w(0, 1024 * i, 1024 * i + 1024), raw[:, 1024 * i:1024 * i + 1024], ACT.Copy)\
                           .then_inc(S["w_hi"], 1)

                def job_hi(count, j, out):
                    act.wait_ge(S["job_full"], count)
                    act.activation(out, PJ[j % 2][:, :], ACT.Copy).then_inc(S["job_hi"], 1)

                def rot_hi(st, q):
                    act.wait_ge(S["rot_add"], st * 4 + 2 * q + 2)
                    act.activation(rot[q][:, 2:4, :].bitcast(F32R), rot[q][:, 0:2, :], ACT.Copy).then_inc(S["rot_hi"], 1)

                def values_and_rope(st, job0):
                    for i in range(4):
                        job_hi(job0 + i + 1, i, v[:, 0, i, :])
                        if i % 2 == 1:
                            rot_hi(st, i // 2)

                def nope_hi(job0, h):
                    job_hi(job0 + 1, 0, qn[:, h % 2, 0, :])
                    job_hi(job0 + 2, 1, kn[:, h % 2, 0, :])

                def step(g, b, last):
                    st = g * NSTEP + b
                    job0 = JP + st * JS

                    def out_hi(h):
                        act.wait_ge(S["pv_done"], st * UN + 2 * h + 2 + CREDIT)
                        act.activation(ot[:, 0, h, :], PO[h % 2][:, :], ACT.Copy).then_inc(S["out_hi"], 1)

                    def turn_hi(u):
                        act.wait_ge(S["turn_full"], st * UN + u + 1 + CREDIT)
                        act.wait_ge(S["pv_done"], st * UN + u - 1 + CREDIT)
                        act.activation(pt[:, u % 2, 0, :], PT[u % 2][:, :], ACT.Copy).then_inc(S["turn_hi"], 1)

                    for u in range(UN):
                        h = u // 2
                        act.wait_ge(S["max_ready"], st * UN + u + 1)
                        act.wait_ge(S["turn_full"], st * UN + u - 1 + CREDIT)
                        for t in range(2):
                            i = act.activation(pr[:, u % 2, t, :], PS[u % 2][:, t * SEQ:(t + 1) * SEQ], ACT.Exp,
                                               bias=nb[:, u % 2, t:t + 1], scale=SCALE0,
                                               accum_out=sm[:, u % 2, t:t + 1])
                        i.then_inc(S["exp_ready"], 1)
                        if u % 2 == 0 and h + 1 < HG:
                            nope_hi(job0 + 2 * h, h + 1)
                        if u >= 1:
                            turn_hi(u - 1)
                        if u >= 3 and u % 2 == 1:
                            out_hi((u - 3) // 2)
                        if last and u == 4:
                            act.wait_ge(S["w_in"], 16 * (g + 2))
                            act.wait_ge(S["job_full"], job0 + JR)
                        if last and u >= 4:
                            split_weights(g + 1, (u - 4,))
                    turn_hi(UN - 1)
                    out_hi(HG - 1)
                    values_and_rope(st + 1, job0 + JV)
                    if last:
                        act.wait_ge(S["job_full"], job0 + JO + 2)
                        split_weights(g + 1, (4,))
                    nope_hi(job0 + JN0, 0)

                act.wait_ge(S["w_in"], 16)
                split_weights(0, range(5))
                values_and_rope(0, 4)
                nope_hi(8, 0)
                with act.Fori(0, NG) as g:
                    with act.Fori(0, NSTEP - 1) as b:
                        step(g, b, False)
                    step(g, NSTEP - 1, True)

            @block.vector
            def _(dve):
                dve.memset(sk[DR:P, 1, :, :].bitcast(F32), 0.0)
                dve.memset(sacc[:, :, :], 0.0).then_inc(S["zeroed"], 1)
                dve.wait_ge(S["zeroed"], 1)
                dve.wait_ge(S["const_in"], 32)
                dve.sem_inc(S["job_free"], CREDIT)
                dve.sem_inc(S["turn_free"], CREDIT)
                dve.sem_inc(S["out_free"], CREDIT)
                def split_weights(g, i):
                    dve.wait_ge(S["w_hi"], 5 * g + i + 1)
                    dve.tensor_tensor(w(1, 1024 * i, 1024 * i + 1024), raw[:, 1024 * i:1024 * i + 1024],
                                      w(0, 1024 * i, 1024 * i + 1024), ALU.subtract).then_inc(S["w_lo_d"], 1)

                def job_lo(count, j, hi, lo):
                    dve.wait_ge(S["job_hi"], count)
                    dve.tensor_tensor(lo, PJ[j % 2][:, :], hi, ALU.subtract).then_inc(S["job_free"], 1)

                def nope_lo(hi0, h):
                    job_lo(hi0 + 1, 0, qn[:, h % 2, 0, :], qn[:, h % 2, 1, :])
                    job_lo(hi0 + 2, 1, kn[:, h % 2, 0, :], kn[:, h % 2, 1, :])

                def values_lo(hi0):
                    for i in range(4):
                        job_lo(hi0 + i + 1, i, v[:, 0, i, :], v[:, 1, i, :])

                def rope_half(st, job0, q, half):
                    if half == 0:
                        for j in range(HG):
                            dve.wait_ge(stack_in[j], st * STACKS)
                    dve.wait_ge(S["job_full"], job0 + 2 * q + half + 1)
                    for s_ in range(2):
                        slot = 2 * half + s_
                        i = dve.tensor_tensor(rot[q][:, slot, :], PJ[half][:, :],
                                              tab[:, 2 * q + (s_ if half == 0 else 1 - s_), :], ALU.mult)
                    i.then_inc(S["job_free"], 1)
                    if half == 1:
                        dve.wait_ge(S["job_free"], job0 + 2 * q + 2 + CREDIT)
                        dve.sem_inc(S["rot_mul"], 1)

                def step(g, b, last):
                    st = g * NSTEP + b
                    job0, hi0 = JP + st * JS, HP + st * HI

                    def normalise(u):
                        dve.wait_ge(S["exp_ready"], st * UN + u + 1 + CREDIT)
                        dve.reciprocal(ri[:, u % 2, :], sm[:, u % 2, :]).then_inc(S["sum_inv"], 1)
                        dve.wait_ge(S["sum_inv"], st * UN + u + 1)
                        for t in range(2):
                            i = dve.tensor_scalar(pr[:, u % 2, t, :], pr[:, u % 2, t, :], ri[:, u % 2, t:t + 1],
                                                  None, ALU.mult)
                        i.then_inc(S["norm_ready"], 1)

                    def turn_lo(u):
                        dve.wait_ge(S["turn_hi"], st * UN + u + 1)
                        dve.tensor_tensor(pt[:, u % 2, 1, :], PT[u % 2][:, :], pt[:, u % 2, 0, :], ALU.subtract)\
                           .then_inc(S["turn_free"], 1)

                    def out_lo(h):
                        dve.wait_ge(S["out_hi"], st * HG + h + 1)
                        dve.tensor_tensor(ot[:, 1, h, :], PO[h % 2][:, :], ot[:, 0, h, :], ALU.subtract)\
                           .then_inc(S["out_free"], 1)

                    for u in range(UN):
                        h = u // 2
                        if u >= 1:
                            normalise(u - 1)
                        dve.wait_ge(S["score_full"], st * UN + u + 1)
                        dve.tensor_reduce(mx[:, u % 2, :], PS[u % 2][:, :].rearrange("p (t k) -> p t k", t=2),
                                          AX.X, ALU.max).then_inc(S["max_raw"], 1)
                        dve.wait_ge(S["max_raw"], st * UN + u + 1)
                        dve.tensor_scalar(nb[:, u % 2, :], mx[:, u % 2, :], -SCALE0, None, ALU.mult)\
                           .then_inc(S["max_ready"], 1)
                        if u % 2 == 0 and h + 1 < HG:
                            nope_lo(hi0 + 2 * h, h + 1)
                        if u >= 1:
                            turn_lo(u - 1)
                        if u >= 3 and u % 2 == 1:
                            out_lo((u - 3) // 2)
                        if last and u in (5, 7):
                            split_weights(g + 1, u - 5)
                    rope_half(st + 1, job0 + JR, 0, 0)
                    normalise(UN - 1)
                    rope_half(st + 1, job0 + JR, 0, 1)
                    turn_lo(UN - 1)
                    rope_half(st + 1, job0 + JR, 1, 0)
                    rope_half(st + 1, job0 + JR, 1, 1)
                    out_lo(HG - 1)
                    values_lo(hi0 + 6)
                    for i in range(2):
                        dve.wait_ge(S["job_full"], job0 + JO + i + 1)
                        acc = sacc[:, bass.ds(b * TT + 2 * i, 2), :]
                        dve.tensor_tensor(acc, acc, PJ[i][:, :].rearrange("p (t d) -> p t d", t=2), ALU.add)\
                           .then_inc(S["job_free"], 1)
                    if last:
                        split_weights(g + 1, 4)
                    nope_lo(hi0 + 10, 0)

                for i in (0, 2, 4):
                    split_weights(0, i)
                for i in range(4):
                    rope_half(0, 0, i // 2, i % 2)
                values_lo(0)
                nope_lo(4, 0)
                with dve.Fori(0, NG) as g:
                    with dve.Fori(0, NSTEP - 1) as b:
                        step(g, b, False)
                    step(g, NSTEP - 1, True)

            @block.tensor
            def _(pe):
                pe.wait_ge(S["const_in"], 32)
                pe.sem_inc(S["exp_ready"], CREDIT)
                pe.sem_inc(S["turn_full"], CREDIT)
                pe.sem_inc(S["pv_done"], CREDIT)
                def open_job(job0, j):
                    pe.wait_ge(S["job_free"], job0 + j - 1 + CREDIT)
                    return PJ[j % 2]

                def feature_job(job0, j, wcol, rows):
                    bank = open_job(job0, j)
                    for c in range(KC):
                        i = product(pe, bank[:, :], w2(wcol + c * rows, wcol + c * rows + P), x2(c, 0, STEP),
                                    c == 0, c == KC - 1)
                    i.then_inc(S["job_full"], 1)

                def nope(job0, j, h):
                    feature_job(job0, j, W_Q + h * DN, HG * DN)
                    feature_job(job0, j + 1, W_K + h * DN, HG * DN)

                def rope(job0, j, q):
                    for half in range(2):
                        feature_job(job0, j + half, W_R + 512 * q + half * P, 2 * P)

                def value_rows(job0, j):
                    for i in range(TT):
                        bank = open_job(job0, j + i)
                        for c in range(KC):
                            m = product(pe, bank[:, :], x2(c, i * P, (i + 1) * P),
                                        w2(W_V + c * 512, W_V + (c + 1) * 512), c == 0, c == KC - 1)
                        m.then_inc(S["job_full"], 1)

                def step(g, b, last):
                    st = g * NSTEP + b
                    job0 = JP + st * JS

                    def scores(u):
                        h, bb = u // 2, u % 2
                        pe.wait_ge(S["exp_ready"], st * UN + u - 1 + CREDIT)
                        pe.wait_ge(S["job_free"], job0 + 2 * h + CREDIT)
                        if bb == 0:
                            pe.wait_ge(stack_in[h], (st + 1) * STACKS)
                        for t in range(2):
                            out = PS[u % 2][:, t * SEQ:(t + 1) * SEQ]
                            a, z = bb * SEQ + t * P, bb * SEQ
                            product(pe, out, (qn[:, h % 2, 0, a:a + P], qn[:, h % 2, 1, a:a + P]),
                                    (kn[:, h % 2, 0, z:z + SEQ], kn[:, h % 2, 1, z:z + SEQ]), True, False)
                            pe.matmul(out, sq[:, h, a:a + P], sk[:, 0, h, z:z + SEQ], start=False, stop=False)
                            i = pe.matmul(out, sq[:, h, a:a + P], sk[:, 1, h, z:z + SEQ], start=False, stop=True)
                        i.then_inc(S["score_full"], 1)

                    def turn(u):
                        pe.wait_ge(S["norm_ready"], st * UN + u + 1)
                        pe.wait_ge(S["turn_free"], st * UN + u - 1 + CREDIT)
                        for kc in range(2):
                            for t in range(2):
                                i = pe.transpose(PT[u % 2][:, kc * SEQ + t * P:kc * SEQ + (t + 1) * P],
                                                 pr[:, u % 2, t, kc * P:(kc + 1) * P], ident[:, :])
                        i.then_inc(S["turn_full"], 1)

                    def values(u):
                        h, bb = u // 2, u % 2
                        pe.wait_ge(S["turn_free"], st * UN + u + 1 + CREDIT)
                        if bb == 0:
                            pe.wait_ge(S["out_free"], st * HG + h - 1 + CREDIT)
                        for kc in range(2):
                            vv = [v[:, s_, 2 * bb + kc, h * DV:(h + 1) * DV] for s_ in range(2)]
                            pp = [pt[:, u % 2, s_, kc * SEQ:(kc + 1) * SEQ] for s_ in range(2)]
                            i = product(pe, PO[h % 2][:, bb * SEQ:(bb + 1) * SEQ], vv, pp, kc == 0, kc == 1)
                        i.then_inc(S["pv_done"], 1)

                    for u in range(UN):
                        scores(u)
                        if u % 2 == 0 and u // 2 + 1 < HG:
                            nope(job0, u, u // 2 + 1)
                        if u >= 1:
                            turn(u - 1)
                        if u >= 2:
                            values(u - 2)
                    pe.wait_ge(S["x_in"], 16 * (st + 2))
                    if last:
                        pe.wait_ge(S["w_lo_d"], 3 * (g + 1) + 2)
                        pe.wait_ge(S["w_lo_p"], 2 * (g + 1) + 2)
                    rope(job0, JR, 0)
                    values(UN - 2)
                    turn(UN - 1)
                    rope(job0, JR + 2, 1)
                    values(UN - 1)
                    value_rows(job0, JV)
                    pe.wait_ge(S["w_lo_d"], 3 * (g + 1))
                    pe.wait_ge(S["out_free"], (st + 1) * HG + CREDIT)
                    for i in range(2):
                        bank = open_job(job0, JO + i)
                        for t in range(2):
                            a = (2 * i + t) * P
                            for h in range(HG):
                                m = product(pe, bank[:, t * D:(t + 1) * D],
                                            (ot[:, 0, h, a:a + P], ot[:, 1, h, a:a + P]),
                                            w2(W_O + h * D, W_O + (h + 1) * D), h == 0, h == HG - 1)
                        m.then_inc(S["job_full"], 1)
                    nope(job0, JN0, 0)

                pe.wait_ge(S["w_lo_d"], 3)
                pe.wait_ge(S["w_lo_p"], 2)
                pe.wait_ge(S["x_in"], 16)
                rope(0, 0, 0)
                rope(0, 2, 1)
                value_rows(0, 4)
                nope(0, 8, 0)
                with pe.Fori(0, NG) as g:
                    with pe.Fori(0, NSTEP - 1) as b:
                        step(g, b, False)
                    step(g, NSTEP - 1, True)


def stage_ffn0(nc, x, wg_in, wu_in, wd_in, scale_in, scale_rest_in, sd_in, xn_dram, sacc):
    with ExitStack() as ctx:
        n = Names(nc, ctx, "f0_")
        ri = [n.sb(f"raw{i}", [P, KC, HT * P], I32) for i in range(2)] + [n.sb("raw2", [P, HT, D], I32)]
        rf = [n.sb(f"rawf{i}", [P, HT * D]) for i in range(2)]
        w = [n.sb(f"w{i}", [P, 2, HT * D], F32R) for i in range(3)]
        scale = n.sb("scale", [P, HT, 2])
        sd = n.sb("sd", [P, D])
        xs = n.sb("xs", [P, 2, 2, KC, STEP], F32R)
        xt = n.sb("x", [P, 2, TT, D])
        act_g = n.sb("act_g", [P, 2, STEP])
        hid = n.sb("hid", [P, 2, HT, STEP], F32R)
        y = n.sb("y", [P, 2, 2 * D])
        G = [n.ps(f"gate{i}") for i in range(2)]
        U = [n.ps(f"up{i}") for i in range(2)]
        Y = [n.ps(f"down{i}") for i in range(2)]
        S = {s: n.sem(s) for s in ("scale_in", "padded", "ws", "w_hi", "w_lo", "own", "up_full", "act_ready", "prod",
                                   "hid_hi", "hid_lo", "down_full", "y_ready", "y_act", "merged")}
        w_in = [n.sem(f"w_in{i}") for i in range(3)]
        x_in = [n.sem(f"x_in{i}") for i in range(NSTEP)]

        with nc.Block() as block:
            @block.sync
            def _(sp):
                for i, src in ((0, wg_in), (1, wu_in)):
                    sp.dma_start(ri[i][:, :, 0:HID], src.rearrange("(c p) n -> p c n", p=P)).then_inc(w_in[i], 16)
                sp.dma_start(ri[2][:, 0:HT - 1, :], wd_in[0:(HT - 1) * P, :].rearrange("(t p) n -> p t n", p=P)).then_inc(w_in[2], 16)
                sp.dma_start(ri[2][0:HREST, HT - 1, :], wd_in[(HT - 1) * P:HID, :]).then_inc(w_in[2], 16)
                sp.dma_start(scale[:, 0:HT - 1, :], scale_in).then_inc(S["scale_in"], 16)
                sp.dma_start(scale[0:HREST, HT - 1, :], scale_rest_in).then_inc(S["scale_in"], 16)
                sp.dma_start(sd[:, :], sd_in.rearrange("(o n) -> o n", o=1).broadcast_to([P, D])).then_inc(S["scale_in"], 16)
                for s in range(NSTEP):
                    if s >= 2:
                        sp.wait_ge(S["merged"], 2 * (s - 1))
                    sp.dma_start(xs[:, s % 2].bitcast(F32), xn_dram[s]).then_inc(x_in[s], 16)
                    sp.dma_start(xt[:, s % 2], x[STEP * s:STEP * (s + 1), :].rearrange("(t p) d -> p t d", p=P)).then_inc(x_in[s], 16)

            @block.gpsimd
            def _(pool):
                for s in range(NSTEP):
                    for t in range(HT):
                        k = HT * s + t
                        pool.wait_ge(S["hid_hi"], k + 1)
                        pool.tensor_tensor(hid[:, 1, t, :], act_g[:, k % 2, :], hid[:, 0, t, :], ALU.subtract)\
                            .then_inc(S["hid_lo"], 1)

            @block.scalar
            def _(act):
                for i in range(3):
                    act.wait_ge(S["ws"], i + 1)
                    act.activation(w[i][:, 0, :], rf[i % 2][:, :], ACT.Copy).then_inc(S["w_hi"], 1)
                act.wait_ge(S["scale_in"], 48)
                for s in range(NSTEP):
                    for t in range(HT):
                        k = HT * s + t
                        act.wait_ge(S["up_full"], k + 1)
                        if k >= 2:
                            act.wait_ge(S["hid_lo"], k - 1)
                        act.activation(act_g[:, k % 2, :], G[k % 2][:, :], ACT.Silu, scale=scale[:, t, 0:1])\
                           .then_inc(S["act_ready"], 1)
                        act.wait_ge(S["prod"], k + 1)
                        if t == 0 and s >= 1:
                            act.wait_ge(S["down_full"], 2 * s)
                        act.activation(hid[:, 0, t, :], act_g[:, k % 2, :], ACT.Copy).then_inc(S["hid_hi"], 1)
                    for i in range(2):
                        act.wait_ge(S["y_ready"], 2 * s + i + 1)
                        act.activation(y[:, i, :], y[:, i, :], ACT.Silu).then_inc(S["y_act"], 1)

            @block.vector
            def _(dve):
                dve.memset(ri[0][:, :, HID:], 128)
                dve.memset(ri[1][:, :, HID:], 128)
                dve.memset(ri[2][HREST:, HT - 1, :], 128)
                dve.memset(scale[HREST:, HT - 1, :], 0.0).then_inc(S["padded"], 1)
                dve.wait_ge(S["padded"], 1)
                for i in range(3):
                    dve.wait_ge(w_in[i], 16 if i < 2 else 32)
                    if i >= 2:
                        dve.wait_ge(S["w_lo"], i - 1)
                    dve.tensor_scalar(rf[i % 2][:, :], ri[i][:, :, :].rearrange("p a b -> p (a b)"), -128.0, None, ALU.add)\
                       .then_inc(S["ws"], 1)
                    dve.wait_ge(S["w_hi"], i + 1)
                    dve.tensor_tensor(w[i][:, 1, :], rf[i % 2][:, :], w[i][:, 0, :], ALU.subtract).then_inc(S["w_lo"], 1)
                dve.wait_ge(S["scale_in"], 48)
                for s in range(NSTEP):
                    for t in range(HT):
                        k = HT * s + t
                        dve.wait_ge(S["act_ready"], k + 1)
                        dve.scalar_tensor_tensor(out=act_g[:, k % 2, :], in0=U[k % 2][:, :], scalar=scale[:, t, 1:2],
                                                 in1=act_g[:, k % 2, :], op0=ALU.mult, op1=ALU.mult).then_inc(S["prod"], 1)
                    for i in range(2):
                        dve.wait_ge(S["down_full"], 2 * s + i + 1)
                        if s >= 1:
                            dve.wait_ge(S["merged"], 2 * (s - 1) + i + 1)
                        dve.tensor_tensor(y[:, i, :].rearrange("p (t d) -> p t d", t=2), Y[i][:, :].rearrange("p (t d) -> p t d", t=2),
                                          sd[:, :].unsqueeze(1).broadcast_to([P, 2, D]), ALU.mult).then_inc(S["y_ready"], 1)
                    dve.wait_ge(x_in[s], 32)
                    for i in range(2):
                        part = sacc[:, TT * s + 2 * i:TT * s + 2 * i + 2, :]
                        dve.wait_ge(S["y_act"], 2 * s + i + 1)
                        dve.tensor_tensor(part, part, y[:, i, :].rearrange("p (t d) -> p t d", t=2), ALU.mult).then_inc(S["own"], 1)
                        dve.wait_ge(S["own"], 2 * s + i + 1)
                        dve.tensor_tensor(part, part, xt[:, s % 2, 2 * i:2 * i + 2, :], ALU.add).then_inc(S["merged"], 1)

            @block.tensor
            def _(pe):
                pe.wait_ge(S["w_lo"], 3)
                for s in range(NSTEP):
                    pe.wait_ge(x_in[s], 32)
                    for t in range(HT):
                        k = HT * s + t
                        if k >= 2:
                            pe.wait_ge(S["prod"], k - 1)
                        for i, bank in ((0, G[k % 2]), (1, U[k % 2])):
                            for c in range(KC):
                                a = c * HT * P + t * P
                                m = product(pe, bank[:, :], (w[i][:, 0, a:a + P], w[i][:, 1, a:a + P]),
                                            (xs[:, s % 2, 0, c, :], xs[:, s % 2, 1, c, :]), c == 0, c == KC - 1)
                        m.then_inc(S["up_full"], 1)
                    pe.wait_ge(S["hid_lo"], HT * (s + 1))
                    for i in range(2):
                        if s >= 1:
                            pe.wait_ge(S["y_ready"], 2 * (s - 1) + i + 1)
                        for tt in range(2):
                            a = (2 * i + tt) * P
                            for t in range(HT):
                                m = product(pe, Y[i][:, tt * D:(tt + 1) * D], (hid[:, 0, t, a:a + P], hid[:, 1, t, a:a + P]),
                                            (w[2][:, 0, t * D:(t + 1) * D], w[2][:, 1, t * D:(t + 1) * D]),
                                            t == 0, t == HT - 1)
                        m.then_inc(S["down_full"], 1)


def stage_attention1(nc, wqkv_in, wproj_in, norm_in, bproj_in, ident_in, xn_dram, x1, s1):
    JT, JQ, JV, JS, JP, JN = 0, 2, 4, 5, 13, 14
    TB = SEQ // P
    QK = 2 * D
    NPAIR = H1 // 2
    OWN = 1 + 2 * TB + 1 + 4 + 1 + 4
    with ExitStack() as ctx:
        n = Names(nc, ctx, "a1_")
        ident = n.sb("ident", [P, P])
        raw = n.sb("raw", [P, KC, 3 * D])
        rawp = n.sb("rawp", [P, KC, D])
        w = n.sb("w", [P, 2, KC, 3 * D], F32R)
        wp = n.sb("wp", [P, 2, KC, D], F32R)
        nw = n.sb("nw", [P, QK])
        bp = n.sb("bp", [P, D])
        mhalf = n.sb("mhalf", [P, 64])
        xt = n.sb("x", [P, TB, D])
        stats, mv = n.sb("stats", [P, TB, 6]), n.sb("mv", [P, TB, 2])
        ve, rs, tmp = n.sb("ve", [P, TB]), n.sb("rs", [P, TB]), n.sb("tmp", [P, TB])
        xs = n.sb("xs", [P, 2, KC, SEQ], F32R)
        qk = n.sb("qk", [P, TB, QK])
        sqr = n.sb("sqr", [P, TB, QK])
        ss, rq, tq = n.sb("ss", [P, 64]), n.sb("rq", [P, 64]), n.sb("tq", [P, 64])
        stq = n.sb("stq", [P, TB, H1, 4, D1])
        stk = n.sb("stk", [P, TB, H1, 4, D1])
        stack = n.sb("stack", [P, NPAIR, 2 * SEQ], F32R)
        BLK = 8 * 144
        vp = n.sb("vp", [P, 2, TB, 2, BLK], F32R)
        pr = n.sb("pr", [P, 2, 2, SEQ])
        pt = n.sb("pt", [P, 2, 2, 512], F32R)
        ot = n.sb("ot", [P, 2, 2, SEQ], F32R)
        mx, nb, sm, ri = (n.sb(s, [P, 2, 2]) for s in ("mx", "nb", "sm", "ri"))
        PJ = [n.ps(f"job{i}") for i in range(2)]
        PS = [n.ps(f"score{i}") for i in range(2)]
        PT = [n.ps(f"turn{i}") for i in range(2)]
        PO = [n.ps(f"out{i}") for i in range(2)]
        S = {s: n.sem(s) for s in (
            "const_in", "w_in", "w_hi", "w_lo", "mhalf_ready", "zeroed", "own", "stats_seen", "ve_ready", "rs_ready", "xn_ready",
            "job_full", "job_free", "job_hi", "qk_ready", "sq_ready", "ms_ready", "rq_ready", "scaled", "normed", "st_hi",
            "st_lo", "stored", "score_full", "max_raw", "max_ready", "exp_ready", "sum_inv", "norm_ready", "turn_full",
            "turn_free", "turn_hi", "pv_done", "out_hi", "out_free")}

        def bc(ap, shape):
            return ap.broadcast_to(shape)

        def heads(buf, t, part):
            return bc(buf[:, t, part * D:(part + 1) * D].rearrange("p (h d) -> p h d", d=D1).unsqueeze(2), [P, H1, 2, D1])

        with nc.Block() as block:
            @block.sync
            def _(sp):
                sp.dma_start(raw[:, :, :], wqkv_in.rearrange("(c p) n -> p c n", p=P)).then_inc(S["w_in"], 16)
                sp.dma_start(rawp[:, :, :], wproj_in.rearrange("(c p) n -> p c n", p=P)).then_inc(S["w_in"], 16)
                sp.dma_start(ident[:, :], ident_in).then_inc(S["const_in"], 16)
                sp.dma_start(nw[:, :], norm_in.broadcast_to([P, QK])).then_inc(S["const_in"], 16)
                sp.dma_start(bp[:, :], bproj_in.broadcast_to([P, D])).then_inc(S["const_in"], 16)
                with sp.Fori(0, BATCH) as b:
                    sp.wait_ge(S["job_free"], b * JN + JT + 2 + CREDIT)
                    sp.dma_start(xn_dram[bass.ds(b, 1)].rearrange("o p s c n -> p (o s c n)"),
                                 xs[:, :, :, :].bitcast(F32).rearrange("p s c n -> p (s c n)")).then_inc(S["stored"], 16)
                sp.wait_ge(S["stored"], 16 * BATCH)

            @block.gpsimd
            def _(pool):
                pool.memset(mhalf[:, :], -0.5).then_inc(S["mhalf_ready"], 1)
                pool.wait_ge(S["mhalf_ready"], 1)
                pool.wait_ge(S["const_in"], 48)
                with pool.Fori(0, BATCH) as b:
                    pool.wait_ge(S["ve_ready"], b + 1)
                    pool.tensor_tensor(rs[:, :], ve[:, :], mhalf[:, 0:TB], ALU.pow).then_inc(S["rs_ready"], 1)
                    pool.wait_ge(S["qk_ready"], b + 1)
                    pool.tensor_tensor(sqr[:, :, :], qk[:, :, :], qk[:, :, :], ALU.mult).then_inc(S["sq_ready"], 1)
                    pool.wait_ge(S["ms_ready"], b + 1)
                    pool.tensor_tensor(rq[:, :], ss[:, :], mhalf[:, :], ALU.pow).then_inc(S["rq_ready"], 1)
                    pool.wait_ge(S["scaled"], b + 1)
                    pool.tensor_tensor(qk[:, :, :], qk[:, :, :], bc(nw[:, :].unsqueeze(1), [P, TB, QK]), ALU.mult)\
                        .then_inc(S["normed"], 1)
                    for t in range(TB):
                        pool.wait_ge(S["st_hi"], b * 2 * TB + 2 * t + 2)
                        pool.tensor_tensor(stq[:, t, :, 1::2, :].bitcast(F32R), heads(qk, t, 0), stq[:, t, :, 0::2, :], ALU.subtract)
                        pool.tensor_tensor(stk[:, t, :, 2:4, :].bitcast(F32R), heads(qk, t, 1), stk[:, t, :, 0:2, :], ALU.subtract)\
                            .then_inc(S["st_lo"], 1)

            @block.scalar
            def _(act):
                act.wait_ge(S["w_in"], 32)
                act.activation(w[:, 0, :, :], raw[:, :, :], ACT.Copy).then_inc(S["w_hi"], 1)
                act.activation(wp[:, 0, :, :], rawp[:, :, :], ACT.Copy).then_inc(S["w_hi"], 1)
                act.wait_ge(S["zeroed"], 1)
                with act.Fori(0, BATCH) as b:
                    act.wait_ge(S["stored"], b * 16)
                    for c in range(KC):
                        act.wait_ge(S["job_full"], b * JN + JT + c + 1)
                        act.activation(xs[:, 0, c, :], PJ[c][:, 0:SEQ], ACT.Copy).then_inc(S["job_hi"], 1)
                    act.wait_ge(S["job_full"], b * JN + JV + 1)
                    act.activation(vp[:, 0].rearrange("p t a (e w) -> p (t a) e w", w=144)[:, :, :, 0:D1],
                                   PJ[JV % 2][:, :].rearrange("p (q e d) -> p q e d", e=8, d=D1), ACT.Copy).then_inc(S["job_hi"], 1)
                    act.wait_ge(S["normed"], b + 1)
                    for t in range(TB):
                        act.activation(stq[:, t, :, 0::2, :].bitcast(F32R), heads(qk, t, 0), ACT.Copy).then_inc(S["st_hi"], 1)
                        act.activation(stk[:, t, :, 0:2, :].bitcast(F32R), heads(qk, t, 1), ACT.Copy).then_inc(S["st_hi"], 1)

                    def turn_hi(u):
                        act.wait_ge(S["turn_full"], b * H1 + u + 1 + CREDIT)
                        act.wait_ge(S["pv_done"], b * H1 + u - 1 + CREDIT)
                        act.activation(pt[:, u % 2, 0, :], PT[u % 2][:, :], ACT.Copy).then_inc(S["turn_hi"], 1)

                    def out_hi(a):
                        act.wait_ge(S["pv_done"], b * H1 + 8 * a + 8 + CREDIT)
                        act.activation(ot[:, 0, a, :], PO[a][:, 0:SEQ], ACT.Copy).then_inc(S["out_hi"], 1)

                    for u in range(H1):
                        act.wait_ge(S["max_ready"], b * H1 + u + 1)
                        act.wait_ge(S["turn_full"], b * H1 + u - 1 + CREDIT)
                        for t in range(2):
                            i = act.activation(pr[:, u % 2, t, :], PS[u % 2][:, t * SEQ:(t + 1) * SEQ], ACT.Exp,
                                               bias=nb[:, u % 2, t:t + 1], scale=SCALE1, accum_out=sm[:, u % 2, t:t + 1])
                        i.then_inc(S["exp_ready"], 1)
                        if u >= 1:
                            turn_hi(u - 1)
                        if u == 10:
                            out_hi(0)
                    turn_hi(H1 - 1)
                    out_hi(1)

            @block.vector
            def _(dve):
                dve.memset(vp[:, :, :, :, :].bitcast(F32), 0.0).then_inc(S["zeroed"], 1)
                dve.wait_ge(S["w_hi"], 2)
                dve.tensor_tensor(w[:, 1, :, :], raw[:, :, :], w[:, 0, :, :], ALU.subtract).then_inc(S["w_lo"], 1)
                dve.tensor_tensor(wp[:, 1, :, :], rawp[:, :, :], wp[:, 0, :, :], ALU.subtract).then_inc(S["w_lo"], 1)
                dve.wait_ge(S["const_in"], 48)
                dve.wait_ge(S["zeroed"], 1)
                for s in ("job_free", "turn_free", "out_free"):
                    dve.sem_inc(S[s], CREDIT)
                with dve.Fori(0, BATCH) as b:
                    k0 = b * OWN
                    dve.tensor_copy(xt[:, :, :], x1[:, bass.ds(b * TB, TB), :]).then_inc(S["own"], 1)
                    dve.wait_ge(S["own"], k0 + 1)
                    k = norm_stats(dve, S["own"], S["stats_seen"], k0 + 1, xt, stats, mv, ve[:, :], TB, LN_EPS)
                    dve.wait_ge(S["own"], k0 + 2 + 2 * TB)
                    dve.sem_inc(S["ve_ready"], 1)
                    dve.wait_ge(S["rs_ready"], b + 1)
                    polish_rsqrt(dve, S["own"], k0 + 2 + 2 * TB, rs[:, :], ve[:, :], tmp[:, :])
                    for t in range(TB):
                        i = dve.tensor_scalar(xt[:, t, :], xt[:, t, :], mv[:, t, 0:1], rs[:, t:t + 1], ALU.subtract, ALU.mult)
                    i.then_inc(S["xn_ready"], 1)
                    for c in range(KC):
                        dve.wait_ge(S["job_hi"], b * 3 + c + 1)
                        dve.tensor_tensor(xs[:, 1, c, :], PJ[c][:, 0:SEQ], xs[:, 0, c, :], ALU.subtract).then_inc(S["job_free"], 1)
                    for t in range(TB):
                        j = JQ + t
                        dve.wait_ge(S["job_full"], b * JN + j + 1)
                        dve.tensor_copy(qk[:, t, :], PJ[j % 2][:, :]).then_inc(S["job_free"], 1)
                    dve.wait_ge(S["job_free"], b * JN + JQ + TB + CREDIT)
                    dve.sem_inc(S["qk_ready"], 1)
                    dve.wait_ge(S["job_hi"], b * 3 + 3)
                    dve.tensor_tensor(vp[:, 1].rearrange("p t a (e w) -> p (t a) e w", w=144)[:, :, :, 0:D1],
                                      PJ[JV % 2][:, :].rearrange("p (q e d) -> p q e d", e=8, d=D1),
                                      vp[:, 0].rearrange("p t a (e w) -> p (t a) e w", w=144)[:, :, :, 0:D1],
                                      ALU.subtract).then_inc(S["job_free"], 1)
                    k = k0 + 6 + 2 * TB
                    dve.wait_ge(S["sq_ready"], b + 1)
                    dve.tensor_reduce(ss[:, :], sqr[:, :, :].rearrange("p t (g d) -> p (t g) d", d=D1), AX.X, ALU.add)\
                       .then_inc(S["own"], 1)
                    dve.wait_ge(S["own"], k + 1)
                    dve.tensor_scalar(ss[:, :], ss[:, :], 1.0 / D1, RMS_EPS, ALU.mult, ALU.add).then_inc(S["ms_ready"], 1)
                    dve.wait_ge(S["rq_ready"], b + 1)
                    polish_rsqrt(dve, S["own"], k + 1, rq[:, :], ss[:, :], tq[:, :])
                    dve.tensor_tensor(qk[:, :, :].rearrange("p t (g d) -> p (t g) d", d=D1),
                                      qk[:, :, :].rearrange("p t (g d) -> p (t g) d", d=D1),
                                      bc(rq[:, :].unsqueeze(2), [P, 64, D1]), ALU.mult).then_inc(S["scaled"], 1)
                    for p in range(NPAIR):
                        j = JS + p
                        dve.wait_ge(S["job_full"], b * JN + j + 1)
                        dve.tensor_copy(stack[:, p, :], PJ[j % 2][:, :]).then_inc(S["job_free"], 1)

                    def normalise(u):
                        dve.wait_ge(S["exp_ready"], b * H1 + u + 1 + CREDIT)
                        dve.reciprocal(ri[:, u % 2, :], sm[:, u % 2, :]).then_inc(S["sum_inv"], 1)
                        dve.wait_ge(S["sum_inv"], b * H1 + u + 1)
                        for t in range(2):
                            i = dve.tensor_scalar(pr[:, u % 2, t, :], pr[:, u % 2, t, :], ri[:, u % 2, t:t + 1], None, ALU.mult)
                        i.then_inc(S["norm_ready"], 1)

                    def turn_lo(u):
                        dve.wait_ge(S["turn_hi"], b * H1 + u + 1)
                        dve.tensor_tensor(pt[:, u % 2, 1, :], PT[u % 2][:, :], pt[:, u % 2, 0, :], ALU.subtract)\
                           .then_inc(S["turn_free"], 1)

                    def out_lo(a):
                        dve.wait_ge(S["out_hi"], b * 2 + a + 1)
                        dve.tensor_tensor(ot[:, 1, a, :], PO[a][:, 0:SEQ], ot[:, 0, a, :], ALU.subtract).then_inc(S["out_free"], 1)

                    for u in range(H1):
                        if u >= 1:
                            normalise(u - 1)
                        dve.wait_ge(S["score_full"], b * H1 + u + 1)
                        dve.tensor_reduce(mx[:, u % 2, :], PS[u % 2][:, :].rearrange("p (t k) -> p t k", t=2), AX.X, ALU.max)\
                           .then_inc(S["max_raw"], 1)
                        dve.wait_ge(S["max_raw"], b * H1 + u + 1)
                        dve.tensor_scalar(nb[:, u % 2, :], mx[:, u % 2, :], -SCALE1, None, ALU.mult).then_inc(S["max_ready"], 1)
                        if u >= 1:
                            turn_lo(u - 1)
                        if u == 10:
                            out_lo(0)
                    normalise(H1 - 1)
                    turn_lo(H1 - 1)
                    out_lo(1)
                    dve.wait_ge(S["job_full"], b * JN + JP + 1)
                    dve.tensor_tensor(s1[:, bass.ds(b * TB, TB), :], PJ[JP % 2][:, :].rearrange("p (t d) -> p t d", t=TB),
                                      bc(bp[:, :].unsqueeze(1), [P, TB, D]), ALU.add).then_inc(S["job_free"], 1)

            @block.tensor
            def _(pe):
                pe.wait_ge(S["const_in"], 48)
                pe.wait_ge(S["w_lo"], 2)
                for s in ("exp_ready", "turn_full", "pv_done"):
                    pe.sem_inc(S[s], CREDIT)
                with pe.Fori(0, BATCH) as b:
                    def open_job(j):
                        pe.wait_ge(S["job_free"], b * JN + j - 1 + CREDIT)
                        return PJ[j % 2]

                    pe.wait_ge(S["xn_ready"], b + 1)
                    for c in range(KC):
                        bank = open_job(JT + c)
                        for t in range(TB):
                            m = pe.transpose(bank[:, t * P:(t + 1) * P], xt[:, t, c * P:(c + 1) * P], ident[:, :])
                        m.then_inc(S["job_full"], 1)
                    pe.wait_ge(S["job_free"], b * JN + JT + 2 + CREDIT)
                    for t in range(TB):
                        bank = open_job(JQ + t)
                        for c in range(KC):
                            m = product(pe, bank[:, :], [xs[:, s, c, t * P:(t + 1) * P] for s in range(2)],
                                        [w[:, s, c, 0:QK] for s in range(2)], c == 0, c == KC - 1)
                        m.then_inc(S["job_full"], 1)
                    bank = open_job(JV)
                    for t in range(TB):
                        for c in range(KC):
                            m = product(pe, bank[:, t * D:(t + 1) * D], [xs[:, s, c, t * P:(t + 1) * P] for s in range(2)],
                                        [w[:, s, c, QK:QK + D] for s in range(2)], c == 0, c == KC - 1)
                    m.then_inc(S["job_full"], 1)
                    pe.wait_ge(S["st_lo"], TB * (b + 1))
                    for p in range(NPAIR):
                        bank = open_job(JS + p)
                        for i, st in enumerate((stq, stk)):
                            for t in range(TB):
                                m = pe.transpose(bank[:, i * SEQ + t * P:i * SEQ + (t + 1) * P],
                                                 st[:, t, 2 * p:2 * p + 2, :, :].rearrange("p h r d -> p (h r d)"), ident[:, :])
                        m.then_inc(S["job_full"], 1)

                    def scores(u):
                        p, at = u // 2, 64 * (u % 2)
                        pe.wait_ge(S["exp_ready"], b * H1 + u - 1 + CREDIT)
                        pe.wait_ge(S["job_free"], b * JN + JS + p + 1 + CREDIT)
                        for t in range(2):
                            m = pe.matmul(PS[u % 2][:, t * SEQ:(t + 1) * SEQ], stack[at:at + 64, p, t * P:(t + 1) * P],
                                          stack[at:at + 64, p, SEQ:2 * SEQ], start=True, stop=True)
                        m.then_inc(S["score_full"], 1)

                    def turn(u):
                        pe.wait_ge(S["norm_ready"], b * H1 + u + 1)
                        pe.wait_ge(S["turn_free"], b * H1 + u - 1 + CREDIT)
                        for kc in range(2):
                            for t in range(2):
                                m = pe.transpose(PT[u % 2][:, kc * SEQ + t * P:kc * SEQ + (t + 1) * P],
                                                 pr[:, u % 2, t, kc * P:(kc + 1) * P], ident[:, :])
                        m.then_inc(S["turn_full"], 1)

                    def values(u):
                        a, e = u // 8, u % 8
                        pe.wait_ge(S["turn_free"], b * H1 + u + 1 + CREDIT)
                        if e == 0:
                            pe.wait_ge(S["out_free"], b * 2 + a - 1 + CREDIT)
                        for kc in range(2):
                            m = product(pe, PO[a][:, 0:SEQ], [vp[:, s, kc, a, e * P:(e + 1) * P] for s in range(2)],
                                        [pt[:, u % 2, s, kc * SEQ:(kc + 1) * SEQ] for s in range(2)],
                                        e == 0 and kc == 0, e == 7 and kc == 1)
                        m.then_inc(S["pv_done"], 1)

                    for u in range(H1):
                        scores(u)
                        if u >= 1:
                            turn(u - 1)
                        if u >= 2:
                            values(u - 2)
                    turn(H1 - 1)
                    values(H1 - 2)
                    values(H1 - 1)
                    pe.wait_ge(S["out_free"], 2 * (b + 1) + CREDIT)
                    bank = open_job(JP)
                    for t in range(TB):
                        for a in range(2):
                            m = product(pe, bank[:, t * D:(t + 1) * D], [ot[:, s, a, t * P:(t + 1) * P] for s in range(2)],
                                        [wp[:, s, a, :] for s in range(2)], a == 0, a == 1)
                    m.then_inc(S["job_full"], 1)


def stage_moe(nc, a, xn_dram, x1, s1, out):
    ROUT = ME * P
    OWN = 19
    with ExitStack() as ctx:
        n = Names(nc, ctx, "m_")
        ident = n.sb("ident", [P, P])
        raw = n.sb("raw", [P, MT * D])
        w = [n.sb(f"w{i}", [P, 2, MT * D], F32R) for i in range(3)]
        rr, rw = n.sb("rr", [P, KC, E]), n.sb("rw", [P, 2, KC, E], F32R)
        sel_raw, sel = n.sb("sel_raw", [2 * E, ROUT]), n.sb("sel", [2 * E, ROUT], F32R)
        rank = n.sb("rank", [P, E])
        bias = n.sb("bias", [P, MT, 2])
        db = n.sb("db", [P, D])
        xs = n.sb("xs", [P, 2, KC, STEP], F32R)
        lg, eq, oh, oh2 = (n.sb(s, [P, TT, E]) for s in ("lg", "eq", "oh", "oh2"))
        m1 = n.sb("m1", [P, TT])
        cm = n.sb("cm", [P, TT, 2, E])
        ct = n.sb("ct", [2 * E, STEP], F32R)
        g = n.sb("g", [P, 2, STEP])
        hid = n.sb("hid", [P, 2, 2, STEP], F32R)
        y = n.sb("y", [P, 2, 2 * D])
        G = [n.ps(f"gate{i}") for i in range(2)]
        U = [n.ps(f"up{i}") for i in range(2)]
        C = [n.ps(f"comb{i}") for i in range(2)]
        Y = [n.ps(f"down{i}") for i in range(2)]
        S = {s: n.sem(s) for s in ("const_in", "w_hi", "w_lo", "raw_used", "zeroed", "own", "x_in", "x_used", "logits",
                                   "lg_ready", "exp_ready", "cm_hi", "cm_ready", "ct_turned", "ct_ready", "up_full", "act_ready",
                                   "prod", "comb_read", "hid_hi", "hid_lo", "down_done", "y_ready", "y_act", "merged", "stored")}
        w_in = [n.sem(f"w_in{i}") for i in range(3)]

        def split(i):
            return w[i][:, 0, :], w[i][:, 1, :]

        with nc.Block() as block:
            @block.sync
            def _(sp):
                sp.dma_start(ident[:, :], a["ident"]).then_inc(S["const_in"], 16)
                sp.dma_start(rr[:, :, :], a["router"].rearrange("(c p) e -> p c e", p=P)).then_inc(S["const_in"], 16)
                sp.dma_start(sel_raw[:, :], a["select"]).then_inc(S["const_in"], 16)
                sp.dma_start(rank[:, :], a["rank"].broadcast_to([P, E])).then_inc(S["const_in"], 16)
                sp.dma_start(db[:, :], a["down_b"].broadcast_to([P, D])).then_inc(S["const_in"], 16)
                sp.wait_ge(S["zeroed"], 1)
                sp.dma_start(bias[:, ME:MT - 1, :], a["bias"]).then_inc(S["const_in"], 16)
                sp.dma_start(bias[0:MREST, MT - 1, :], a["bias_rest"]).then_inc(S["const_in"], 16)
                for i, name in enumerate(("gate", "up")):
                    if i:
                        sp.wait_ge(S["w_lo"], i)
                    dst = raw[:, :].rearrange("p (c n) -> p c n", c=KC)
                    sp.dma_start(dst[:, :, 0:ROUT], a[name].rearrange("(c p) n -> p c n", p=P)).then_inc(w_in[i], 16)
                    sp.dma_start(dst[:, :, ROUT:MW], a["s_" + name].rearrange("(c p) n -> p c n", p=P)).then_inc(w_in[i], 16)
                sp.wait_ge(S["raw_used"], 1)
                dst = raw[:, :].rearrange("p (t n) -> p t n", t=MT)
                sp.dma_start(dst[:, 0:ME, :], a["down"].rearrange("(t p) n -> p t n", p=P)).then_inc(w_in[2], 16)
                sp.dma_start(dst[:, ME:MT - 1, :], a["s_down"][0:(MT - 1 - ME) * P, :].rearrange("(t p) n -> p t n", p=P))\
                  .then_inc(w_in[2], 16)
                sp.dma_start(dst[0:MREST, MT - 1, :], a["s_down"][(MT - 1 - ME) * P:SI, :]).then_inc(w_in[2], 16)
                with sp.Fori(0, NSTEP) as s:
                    sp.wait_ge(S["x_used"], s)
                    for half in range(2):
                        sp.dma_start(xs[:, :, :, half * SEQ:(half + 1) * SEQ].bitcast(F32),
                                     xn_dram[bass.ds(2 * s + half, 1)].rearrange("o p s c n -> p (o s) c n")).then_inc(S["x_in"], 16)
                    sp.wait_ge(S["merged"], 2 * s + 2)
                    sp.dma_start(out[bass.ds(s, 1)].rearrange("o (t p) d -> p (o t) d", p=P),
                                 x1[:, bass.ds(s * TT, TT), :]).then_inc(S["stored"], 16)
                sp.wait_ge(S["stored"], 16 * NSTEP)

            @block.gpsimd
            def _(pool):
                with pool.Fori(0, NSTEP) as s:
                    for t in range(MT):
                        pool.wait_ge(S["hid_hi"], s * MT + t + 1)
                        pool.tensor_tensor(hid[:, t % 2, 1, :], g[:, t % 2, :], hid[:, t % 2, 0, :], ALU.subtract)\
                            .then_inc(S["hid_lo"], 1)

            @block.scalar
            def _(act):
                act.wait_ge(S["const_in"], 112)
                act.activation(rw[:, 0, :, :], rr[:, :, :], ACT.Copy).then_inc(S["w_hi"], 1)
                act.activation(sel[:, :], sel_raw[:, :], ACT.Copy).then_inc(S["w_hi"], 1)
                for i in range(3):
                    act.wait_ge(w_in[i], 32 if i < 2 else 48)
                    act.activation(w[i][:, 0, :], raw[:, :], ACT.Copy).then_inc(S["w_hi"], 1)
                with act.Fori(0, NSTEP) as s:
                    act.wait_ge(S["lg_ready"], s + 1)
                    act.activation(lg[:, :, :], lg[:, :, :], ACT.Exp).then_inc(S["exp_ready"], 1)
                    act.wait_ge(S["cm_hi"], s + 1)
                    act.activation(cm[:, :, 0, :].bitcast(F32R), oh[:, :, :], ACT.Copy).then_inc(S["cm_ready"], 1)
                    act.wait_ge(S["ct_turned"], s + 1)
                    act.activation(ct[:, :], C[1][0:2 * E, :], ACT.Copy).then_inc(S["ct_ready"], 1)
                    for t in range(MT):
                        act.wait_ge(S["up_full"], s * MT + t + 1)
                        act.wait_ge(S["hid_lo"], s * MT + t - 1 + CREDIT)
                        act.activation(g[:, t % 2, :], G[t % 2][:, :], ACT.Silu, bias=bias[:, t, 0:1]).then_inc(S["act_ready"], 1)
                        act.wait_ge(S["comb_read"], s * MT + t + 1 + CREDIT)
                        act.wait_ge(S["down_done"], s * MT + t - 1 + CREDIT)
                        act.activation(hid[:, t % 2, 0, :], g[:, t % 2, :], ACT.Copy).then_inc(S["hid_hi"], 1)
                    for i in range(2):
                        act.wait_ge(S["y_ready"], 2 * s + i + 1 + CREDIT)
                        act.activation(y[:, i, :], y[:, i, :], ACT.Silu).then_inc(S["y_act"], 1)

            @block.vector
            def _(dve):
                pad = raw[:, :].rearrange("p (c n) -> p c n", c=KC)
                dve.memset(pad[:, :, MW:], 0.0)
                dve.memset(bias[:, :, :], 0.0).then_inc(S["zeroed"], 1)
                dve.wait_ge(S["w_hi"], 1)
                dve.tensor_tensor(rw[:, 1, :, :], rr[:, :, :], rw[:, 0, :, :], ALU.subtract).then_inc(S["own"], 1)
                for i in range(3):
                    dve.wait_ge(S["w_hi"], i + 3)
                    dve.tensor_tensor(w[i][:, 1, :], raw[:, :], w[i][:, 0, :], ALU.subtract).then_inc(S["w_lo"], 1)
                    if i == 1:
                        dve.wait_ge(S["w_lo"], 2)
                        dve.memset(raw[96:P, (MT - 1) * D:], 0.0).then_inc(S["raw_used"], 1)
                dve.wait_ge(S["const_in"], 112)
                for s_ in ("hid_lo", "comb_read", "y_ready"):
                    dve.sem_inc(S[s_], CREDIT)
                with dve.Fori(0, NSTEP) as s:
                    k0 = s * OWN + 1

                    def own(k, i):
                        i.then_inc(S["own"], 1)
                        dve.wait_ge(S["own"], k0 + k)

                    def rows(ap):
                        return ap.unsqueeze(2).broadcast_to([P, TT, E])

                    ranks = rank[:, :].unsqueeze(1).broadcast_to([P, TT, E])
                    dve.wait_ge(S["logits"], s + 1)
                    own(1, dve.tensor_reduce(m1[:, :], C[0][:, 0:TT * E].rearrange("p (t e) -> p t e", e=E), AX.X, ALU.max))
                    dve.tensor_tensor(lg[:, :, :], C[0][:, 0:TT * E].rearrange("p (t e) -> p t e", e=E), rows(m1[:, :]), ALU.subtract)\
                       .then_inc(S["lg_ready"], 1)
                    dve.wait_ge(S["exp_ready"], s + 1)
                    own(2, dve.tensor_reduce(m1[:, :], lg[:, :, :], AX.X, ALU.max))
                    own(3, dve.tensor_tensor(eq[:, :, :], lg[:, :, :], rows(m1[:, :]), ALU.is_equal))
                    own(4, dve.tensor_tensor(eq[:, :, :], eq[:, :, :], ranks, ALU.mult))
                    own(5, dve.tensor_reduce(m1[:, :], eq[:, :, :], AX.X, ALU.max))
                    own(6, dve.tensor_tensor(oh[:, :, :], eq[:, :, :], rows(m1[:, :]), ALU.is_equal))
                    own(7, dve.scalar_tensor_tensor(out=eq[:, :, :], in0=oh[:, :, :], scalar=-2.0, in1=lg[:, :, :],
                                                    op0=ALU.mult, op1=ALU.add))
                    own(8, dve.tensor_reduce(m1[:, :], eq[:, :, :], AX.X, ALU.max))
                    own(9, dve.tensor_tensor(eq[:, :, :], eq[:, :, :], rows(m1[:, :]), ALU.is_equal))
                    own(10, dve.tensor_tensor(eq[:, :, :], eq[:, :, :], ranks, ALU.mult))
                    own(11, dve.tensor_reduce(m1[:, :], eq[:, :, :], AX.X, ALU.max))
                    own(12, dve.tensor_tensor(oh2[:, :, :], eq[:, :, :], rows(m1[:, :]), ALU.is_equal))
                    own(13, dve.tensor_tensor(oh2[:, :, :], oh2[:, :, :], oh[:, :, :], ALU.add))
                    own(14, dve.tensor_tensor(oh2[:, :, :], oh2[:, :, :], lg[:, :, :], ALU.mult))
                    own(15, dve.tensor_reduce(m1[:, :], oh2[:, :, :], AX.X, ALU.add))
                    own(16, dve.reciprocal(m1[:, :], m1[:, :]))
                    dve.tensor_tensor(oh[:, :, :], oh2[:, :, :], rows(m1[:, :]), ALU.mult).then_inc(S["cm_hi"], 1)
                    dve.wait_ge(S["cm_ready"], s + 1)
                    own(17, dve.tensor_tensor(cm[:, :, 1, :].bitcast(F32R), oh[:, :, :], cm[:, :, 0, :], ALU.subtract))
                    dve.sem_inc(S["raw_used"], 1)
                    for t in range(MT):
                        dve.wait_ge(S["act_ready"], s * MT + t + 1)
                        i = dve.scalar_tensor_tensor(out=g[:, t % 2, :], in0=U[t % 2][:, :], scalar=bias[:, t, 1:2],
                                                     in1=g[:, t % 2, :], op0=ALU.add, op1=ALU.mult)
                        if t < ME:
                            i.then_inc(S["prod"], 1)
                            dve.wait_ge(S["prod"], s * ME + t + 1)
                            i = dve.tensor_tensor(g[:, t % 2, :], g[:, t % 2, :], C[t % 2][:, :], ALU.mult)
                        i.then_inc(S["comb_read"], 1)
                    for i in range(2):
                        dve.wait_ge(S["down_done"], (s + 1) * MT + CREDIT)
                        dve.tensor_tensor(y[:, i, :].rearrange("p (t d) -> p t d", t=2), Y[i][:, :].rearrange("p (t d) -> p t d", t=2),
                                          db[:, :].unsqueeze(1).broadcast_to([P, 2, D]), ALU.add).then_inc(S["y_ready"], 1)
                    for i in range(2):
                        dve.wait_ge(S["y_act"], 2 * s + i + 1)
                        yy = y[:, i, :].rearrange("p (t d) -> p t d", t=2)
                        own(18 + i, dve.tensor_tensor(yy, yy, s1[:, bass.ds(s * TT + 2 * i, 2), :], ALU.mult))
                        part = x1[:, bass.ds(s * TT + 2 * i, 2), :]
                        dve.tensor_tensor(part, part, yy, ALU.add).then_inc(S["merged"], 1)

            @block.tensor
            def _(pe):
                pe.wait_ge(S["const_in"], 112)
                pe.wait_ge(S["w_lo"], 3)
                pe.wait_ge(S["own"], 1)
                pe.wait_ge(S["w_hi"], 5)
                pe.sem_inc(S["down_done"], CREDIT)
                with pe.Fori(0, NSTEP) as s:
                    pe.wait_ge(S["x_in"], 32 * (s + 1))
                    pe.wait_ge(S["comb_read"], s * MT + CREDIT)
                    for t in range(TT):
                        for c in range(KC):
                            m = product(pe, C[0][:, t * E:(t + 1) * E], [xs[:, i, c, t * P:(t + 1) * P] for i in range(2)],
                                        [rw[:, i, c, :] for i in range(2)], c == 0, c == KC - 1)
                    m.then_inc(S["logits"], 1)

                    def up(t):
                        pe.wait_ge(S["comb_read"], s * MT + t - 1 + CREDIT)
                        for i, bank in ((0, G[t % 2]), (1, U[t % 2])):
                            for c in range(KC):
                                a_ = c * (MT * P) + t * P
                                m = product(pe, bank[:, :], [w[i][:, q, a_:a_ + P] for q in range(2)],
                                            [xs[:, q, c, :] for q in range(2)], c == 0, c == KC - 1)
                        return m

                    def combine(t):
                        return pe.matmul(C[t % 2][:, :], sel[:, t * P:(t + 1) * P], ct[:, :], start=True, stop=True)

                    def down(t):
                        pe.wait_ge(S["hid_lo"], s * MT + t + 1 + CREDIT)
                        if t == 0:
                            pe.wait_ge(S["y_ready"], 2 * s + CREDIT)
                        for tt in range(TT):
                            o = Y[tt // 2][:, (tt % 2) * D:(tt % 2 + 1) * D]
                            hh, hl = (hid[:, t % 2, q, tt * P:(tt + 1) * P] for q in range(2))
                            wh, wl = (w[2][:, q, t * D:(t + 1) * D] for q in range(2))
                            pe.matmul(o, hh, wh, start=(t == 0 and tt % 2 == 0), stop=False, skip_group_check=True)
                            pe.matmul(o, hh, wl, start=False, stop=False, skip_group_check=True)
                            m = pe.matmul(o, hl, wh, start=False, stop=(t == MT - 1), skip_group_check=True)
                        m.then_inc(S["down_done"], 1)

                    up(0)
                    pe.wait_ge(S["raw_used"], s + 2)
                    for t in range(TT):
                        m = pe.transpose(C[1][0:2 * E, t * P:(t + 1) * P], cm[:, t, :, :].rearrange("p s e -> p (s e)"), ident[:, :])
                    m.then_inc(S["ct_turned"], 1)
                    pe.wait_ge(S["ct_ready"], s + 1)
                    combine(0).then_inc(S["up_full"], 1)
                    for t in range(1, MT):
                        m = up(t)
                        if t == MT - 1:
                            m.then_inc(S["x_used"], 1)
                            pe.wait_ge(S["x_used"], s + 1)
                            pe.sem_inc(S["up_full"], 1)
                        else:
                            (combine(t) if t < ME else m).then_inc(S["up_full"], 1)
                        down(t - 1)
                    down(MT - 1)


def program(nc, a, out):
    xn0 = nc.dram_tensor("xn0_scratch", [NSTEP, P, 2, KC, STEP], F32, kind="Internal").ap()
    xn1 = nc.dram_tensor("xn1_scratch", [BATCH, P, 2, KC, SEQ], F32, kind="Internal").ap()
    stage_norm0(nc, a["x"], a["ident"], xn0)
    with nc.sbuf_tensor("x1", [P, NT, D], F32) as x1:
        stage_attention0(nc, a["w0"], a["rope"], a["ident"], xn0, x1)
        stage_ffn0(nc, a["x"], a["wg"], a["wu"], a["wd"], a["scale"], a["scale_rest"], a["sd"], xn0, x1)
        with nc.sbuf_tensor("s1", [P, NT, D], F32) as s1:
            stage_attention1(nc, a["w_qkv"], a["w_proj"], a["norm_w"], a["b_proj"], a["ident"], xn1, x1, s1)
            stage_moe(nc, a, xn1, x1, s1, out)


def rope_tables():
    import numpy as np
    freq = (np.float32(1.0) / np.float32(10000.0) ** (np.arange(0, DR, 2, dtype=np.float32) / np.float32(DR))).astype(np.float32)
    angle = (np.arange(SEQ, dtype=np.float32)[None, :] * freq[:, None]).astype(np.float32)
    cos, sin = (np.tile(f(angle.astype(np.float64)), (HG, 2)) for f in (np.cos, np.sin))
    more = math.sqrt(DN / DR)
    return np.ascontiguousarray(np.stack([cos * more, sin * more, cos, sin], axis=1).astype(np.float32))


def group_weights(wq, wk, wv, wo):
    import numpy as np
    groups = []
    for g in range(NG):
        cols = []
        for w in (wq, wk, wv):
            rows = w[g * HG * DN:(g + 1) * HG * DN]
            cols.append(rows.T.reshape(KC, P, HG * DN).transpose(1, 0, 2).reshape(P, -1))
        for w in (wq, wk):
            rows = w[H * DN + g * HG * DR:H * DN + (g + 1) * HG * DR].reshape(HG, 2, HALF, D)
            rows = rows.transpose(1, 0, 2, 3).reshape(2 * HG * HALF, D)
            cols.append(rows.T.reshape(KC, P, 2 * P).transpose(1, 0, 2).reshape(P, -1))
        cols.append(wo[:, g * HG * DV:(g + 1) * HG * DV].T.reshape(HG, DV, D).transpose(1, 0, 2).reshape(P, -1))
        groups.append(np.concatenate(cols, axis=1))
    return np.ascontiguousarray(np.stack(groups))


def kernel(**inputs):
    import numpy as _np
    import concourse.bacc as _bacc
    from concourse import mybir as _mybir
    from concourse.bass_utils import run_bass_kernel_spmd as _run

    i = {k: _np.asarray(v) for k, v in inputs.items()}
    scales = _np.stack([i["L0_ffn_s_gate"], i["L0_ffn_s_up"]], axis=1)
    shared = _np.stack([i["L1_ffn_s_gate_b"], i["L1_ffn_s_up_b"]], axis=1)
    data = {
        "x": i["L0_attn_hidden_states"].reshape(NTOK, D),
        "ident": _np.eye(P, dtype=_np.float32),
        "rope": rope_tables(),
        "w0": group_weights(i["L0_attn_Wq"], i["L0_attn_Wk"], i["L0_attn_Wv"], i["L0_attn_Wo"]),
        "wg": i["L0_ffn_wq_gate"].T, "wu": i["L0_ffn_wq_up"].T, "wd": i["L0_ffn_wq_down"].T,
        "scale": scales[0:(HT - 1) * P].reshape(HT - 1, P, 2).transpose(1, 0, 2), "scale_rest": scales[(HT - 1) * P:],
        "sd": i["L0_ffn_s_down"],
        "w_qkv": i["L1_attn_w_qkv"].T, "w_proj": i["L1_attn_w_proj"].T,
        "norm_w": _np.concatenate([_np.tile(i["L1_attn_q_norm_w"], H1), _np.tile(i["L1_attn_k_norm_w"], H1)])[None],
        "b_proj": i["L1_attn_b_proj"][None],
        "router": i["L1_ffn_router_w"].T,
        "gate": i["L1_ffn_gate_w"].transpose(1, 0, 2).reshape(D, E * I1),
        "up": i["L1_ffn_up_w"].transpose(1, 0, 2).reshape(D, E * I1),
        "down": i["L1_ffn_down_w"].reshape(E * I1, D),
        "s_gate": i["L1_ffn_s_gate_w"], "s_up": i["L1_ffn_s_up_w"], "s_down": i["L1_ffn_s_down_w"],
        "bias": shared[0:2 * P].reshape(2, P, 2).transpose(1, 0, 2), "bias_rest": shared[2 * P:],
        "down_b": i["L1_ffn_s_down_b"][None],
        "rank": (E - _np.arange(E, dtype=_np.float32))[None],
        "select": _np.tile(_np.repeat(_np.eye(E, dtype=_np.float32), I1, axis=1), (2, 1)),
    }
    nc = _bacc.Bacc("TRN2", target_bir_lowering=False, num_devices=1)
    arrays, args = {}, {}
    for name, value in data.items():
        arrays["in_" + name] = _np.ascontiguousarray(value)
        args[name] = nc.dram_tensor("in_" + name, value.shape, _mybir.dt.from_np(value.dtype), kind="ExternalInput").ap()
    out = nc.dram_tensor("out_x", (NSTEP, STEP, D), F32, kind="ExternalOutput").ap()
    program(nc, args, out)
    r = _run(nc, [arrays], core_ids=[0])
    return r.results[0]["out_x"].reshape(BATCH, SEQ, D)
```

```python
from contextlib import ExitStack
import math

import concourse.bass as bass
from concourse import mybir

F32 = mybir.dt.float32
F32R = mybir.dt.float32r
I32 = mybir.dt.int32
ALU = mybir.AluOpType
ACT = mybir.ActivationFunctionType
AX = mybir.AxisListType

P = 128
D = 256
KC = D // P
NTOK, SEQ, BATCH = 2048, 256, 8
NT = NTOK // P
STEP = 512
NSTEP = NTOK // STEP
TT = STEP // P
H, DN, DR, DV = 16, 128, 64, 128
HG = 4
NG = H // HG
HALF = DR // 2
HID = 704
HT = 6
HREST = HID - (HT - 1) * P
H1, D1 = 16, 16
E, I1 = 8, 176
SI = 2 * I1
MW = E * I1 + SI
MT = 14
ME = E * I1 // P
MREST = MW - (MT - 1) * P
LN_EPS, RMS_EPS = 1e-5, 1e-6
SCALE0 = 1.0 / math.sqrt(DN)
SCALE1 = D1 ** -0.5
CREDIT = 2

W_Q, W_K, W_V, W_R, W_O, W_END = 0, 1024, 2048, 3072, 4096, 5120


def product(pe, out, lhs, rhs, first, last):
    (lh, ll), (rh, rl) = lhs, rhs
    pe.matmul(out, lh, rh, start=first, stop=False)
    pe.matmul(out, lh, rl, start=False, stop=False)
    return pe.matmul(out, ll, rh, start=False, stop=last)


class Names:

    def __init__(self, nc, ctx, prefix):
        self.nc, self.ctx, self.prefix = nc, ctx, prefix

    def sb(self, name, shape, dt=F32):
        return self.ctx.enter_context(self.nc.sbuf_tensor(self.prefix + name, shape, dt))

    def ps(self, name, shape=(P, 512)):
        return self.ctx.enter_context(self.nc.psum_tensor(self.prefix + name, list(shape), F32))

    def sem(self, name):
        return self.ctx.enter_context(self.nc.semaphore(self.prefix + name))


def norm_stats(dve, own, seen, k, xt, stats, mv, var_eps, tiles, eps):
    for t in range(tiles):
        dve.bn_stats(stats[:, t, :], xt[:, t, :]).then_inc(own, 1)
    dve.wait_ge(own, k + tiles)
    dve.sem_inc(seen, 1)
    for t in range(tiles):
        dve.bn_aggr(mv[:, t, :], stats[:, t, :]).then_inc(own, 1)
    dve.wait_ge(own, k + 2 * tiles)
    dve.tensor_scalar(var_eps, mv[:, 0:tiles, 1], eps, None, ALU.add).then_inc(own, 1)
    return k + 2 * tiles + 1


def polish_rsqrt(dve, own, k, r, v, tmp):
    dve.tensor_tensor(tmp, r, r, ALU.mult).then_inc(own, 1)
    dve.wait_ge(own, k + 1)
    dve.tensor_tensor(tmp, tmp, v, ALU.mult).then_inc(own, 1)
    dve.wait_ge(own, k + 2)
    dve.tensor_scalar(tmp, tmp, -0.5, 1.5, ALU.mult, ALU.add).then_inc(own, 1)
    dve.wait_ge(own, k + 3)
    dve.tensor_tensor(r, r, tmp, ALU.mult).then_inc(own, 1)
    dve.wait_ge(own, k + 4)
    return k + 4


def stage_norm0(nc, x, ident_in, xn_dram):
    with ExitStack() as ctx:
        n = Names(nc, ctx, "n0_")
        xt = n.sb("x", [P, NT, D])
        xn = n.sb("xn", [P, 2, TT, D])
        ident = n.sb("ident", [P, P])
        stats = n.sb("stats", [P, TT, 6])
        mv = n.sb("mv", [P, TT, 2])
        ve = n.sb("ve", [P, 2, TT])
        rs = n.sb("rs", [P, 2, TT])
        tmp = n.sb("tmp", [P, TT])
        mhalf = n.sb("mhalf", [P, TT])
        xs = n.sb("xs", [P, 2, 2, KC, STEP], F32R)
        bank = [n.ps(f"bank{i}") for i in range(2)]
        x_in = [n.sem(f"x_in{s}") for s in range(NSTEP)]
        id_in, own, stats_seen, ve_ready, rs_ready, mhalf_ready = (n.sem(s) for s in ("id_in", "own", "stats_seen", "ve_ready", "rs_ready", "mhalf_ready"))
        xn_ready, turned, hi_ready, lo_ready = (n.sem(s) for s in ("xn_ready", "turned", "hi_ready", "lo_ready"))
        stored = [n.sem(f"stored{i}") for i in range(2)]

        with nc.Block() as block:
            @block.sync
            def _(sp):
                sp.dma_start(ident[:, :], ident_in).then_inc(id_in, 16)
                for s in range(NSTEP):
                    sp.dma_start(xt[:, TT * s:TT * (s + 1), :],
                                 x[STEP * s:STEP * (s + 1), :].rearrange("(t p) d -> p t d", p=P)).then_inc(x_in[s], 16)
                for s in range(NSTEP):
                    sp.wait_ge(lo_ready, 2 * s + 2)
                    sp.dma_start(xn_dram[s], xs[:, s % 2].bitcast(F32)).then_inc(stored[s % 2], 16)
                for i in range(2):
                    sp.wait_ge(stored[i], 16 * NSTEP // 2)

            @block.gpsimd
            def _(pool):
                pool.memset(mhalf[:, :], -0.5).then_inc(mhalf_ready, 1)
                pool.wait_ge(mhalf_ready, 1)
                for s in range(NSTEP):
                    pool.wait_ge(ve_ready, s + 1)
                    pool.tensor_tensor(rs[:, s % 2, :], ve[:, s % 2, :], mhalf[:, :], ALU.pow).then_inc(rs_ready, 1)

            @block.vector
            def _(dve):
                k = 0
                for s in range(NSTEP):
                    dve.wait_ge(x_in[s], 16)
                    k = norm_stats(dve, own, stats_seen, k, xt[:, TT * s:TT * (s + 1), :], stats, mv, ve[:, s % 2, :], TT, LN_EPS)
                    dve.wait_ge(own, k)
                    dve.sem_inc(ve_ready, 1)
                    dve.wait_ge(rs_ready, s + 1)
                    k = polish_rsqrt(dve, own, k, rs[:, s % 2, :], ve[:, s % 2, :], tmp[:, :])
                    if s >= 2:
                        dve.wait_ge(turned, 2 * (s - 1))
                    for t in range(TT):
                        i = dve.tensor_scalar(xn[:, s % 2, t, :], xt[:, TT * s + t, :], mv[:, t, 0:1],
                                              rs[:, s % 2, t:t + 1], ALU.subtract, ALU.mult)
                    i.then_inc(xn_ready, 1)
                    for c in range(KC):
                        dve.wait_ge(hi_ready, 2 * s + c + 1)
                        dve.tensor_tensor(xs[:, s % 2, 1, c, :], bank[c][:, :], xs[:, s % 2, 0, c, :], ALU.subtract)\
                           .then_inc(lo_ready, 1)

            @block.tensor
            def _(pe):
                pe.wait_ge(id_in, 16)
                for s in range(NSTEP):
                    pe.wait_ge(xn_ready, s + 1)
                    for c in range(KC):
                        if s >= 1:
                            pe.wait_ge(lo_ready, 2 * (s - 1) + c + 1)
                        for t in range(TT):
                            i = pe.transpose(bank[c][:, t * P:(t + 1) * P], xn[:, s % 2, t, c * P:(c + 1) * P], ident[:, :])
                        i.then_inc(turned, 1)

            @block.scalar
            def _(act):
                for s in range(NSTEP):
                    if s >= 2:
                        act.wait_ge(stored[s % 2], 16 * (s // 2))
                    for c in range(KC):
                        act.wait_ge(turned, 2 * s + c + 1)
                        act.activation(xs[:, s % 2, 0, c, :], bank[c][:, :], ACT.Copy).then_inc(hi_ready, 1)


def stage_attention0(nc, weights, tables, ident_in, xn_dram, sacc):
    UN = 2 * HG
    UNIT_JOBS = [[], ["k1"], ["q2"], ["k2", "rope0"], ["q3", "rope1"], ["k3", "rope2"], ["q0+", "rope3"], []]
    JOB = {name: i for i, name in enumerate(sum(UNIT_JOBS, []))}
    JN, JV, JO, JS, JP = 10, 12, 16, 18, 12
    HI, HP = 12, 7
    SPLIT = {name: i for i, name in enumerate(x for x in JOB if not x.startswith("rope"))}
    SN, SV = 6, 8
    QK_DONE = [-2] + [JOB[f"k{h}"] + 1 for h in range(1, HG)]
    W_ORDER = [3, 2, 0, 1, 4]
    with ExitStack() as ctx:
        n = Names(nc, ctx, "a0_")
        ident = n.sb("ident", [P, P])
        tab = n.sb("tab", [P, 4, STEP])
        raw = n.sb("raw", [P, W_END])
        wh, wl = n.sb("wh", [P, W_END], F32R), n.sb("wl", [P, W_END], F32R)
        xs = n.sb("xs", [P, 2, KC, STEP], F32R)
        xr = n.sb("xr", [P, 2, KC, STEP], F32R)
        rot = [n.sb("rotq", [P, 4, STEP]), n.sb("rotk", [P, 4, STEP])]
        sq = n.sb("sq", [P, HG, STEP], F32R)
        sk = n.sb("sk", [P, 2, HG, STEP], F32R)
        qn = n.sb("qn", [P, 2, 2, STEP], F32R)
        kn = n.sb("kn", [P, 2, 2, STEP], F32R)
        v = n.sb("v", [P, 2, TT, HG * DV], F32R)
        pr = n.sb("pr", [P, 2, 2, SEQ])
        pt = n.sb("pt", [P, 2, 2, 512], F32R)
        ot = n.sb("ot", [P, 2, HG, STEP], F32R)
        mx = n.sb("mx", [P, 2, 2])
        nb = n.sb("nb", [P, 2, 2])
        sm = n.sb("sm", [P, 2, 2])
        ri = n.sb("ri", [P, 2, 2])
        PJ = [n.ps(f"job{i}") for i in range(2)]
        PS = [n.ps(f"score{i}") for i in range(2)]
        PT = [n.ps(f"turn{i}") for i in range(2)]
        PO = [n.ps(f"out{i}") for i in range(2)]
        QSTACKS, KSTACKS = 16 * 4 * HG, 16 * 6
        kstack_in = [n.sem(f"kstack_in{j}") for j in range(HG)]
        S = {s: n.sem(s) for s in (
            "const_in", "w_in", "w_hi", "w_lo_d", "w_lo_p", "x_in", "xr_in", "qstack_in", "job_full", "job_free", "job_hi", "rot_mul",
            "rot_add", "rot_hi", "rot_lo", "score_full", "score_free", "max_raw", "max_ready", "exp_ready",
            "sum_inv", "norm_ready", "turn_full", "turn_free", "turn_hi", "pv_done", "out_hi", "out_free", "zeroed", "wl_p")}

        def w(part, a, b):
            return (wh, wl)[part][:, a:b]

        def w2(a, b):
            return w(0, a, b), w(1, a, b)

        def x2(x, c, a, b):
            return x[:, 0, c, a:b], x[:, 1, c, a:b]

        with nc.Block() as block:
            @block.sync
            def _(sp):
                sp.dma_start(ident[:, :], ident_in).then_inc(S["const_in"], 16)
                sp.dma_start(tab[:, :, :], tables).then_inc(S["const_in"], 16)
                def load_x(x, b, loaded):
                    sp.dma_start(x[:, :, :, :].bitcast(F32).rearrange("p s c n -> p (s c n)"),
                                 xn_dram[bass.ds(b, 1)].rearrange("o p s c n -> p (o s c n)")).then_inc(S[loaded], 16)

                def load_weights(g):
                    sp.dma_start(raw[:, :], weights[bass.ds(g, 1)].rearrange("o p n -> p (o n)")).then_inc(S["w_in"], 16)

                def stack_q(st, before):
                    sp.wait_ge(S["rot_lo"], st * 2 + 1)
                    for j in range(HG):
                        if before is not None:
                            sp.wait_ge(S["score_full"], before * UN + 2 * j + 2)
                        for part in range(2):
                            for r in range(2):
                                at = HALF * (2 * part + r)
                                sp.dma_start(sq[at:at + HALF, j, :].bitcast(F32),
                                             rot[0][HALF * j:HALF * (j + 1), 2 * (1 - part) + r, :]).then_inc(S["qstack_in"], 16)

                def stack_k(st):
                    sp.wait_ge(S["rot_lo"], st * 2 + 2)
                    for j in range(HG):
                        for part, copies in ((0, 2), (1, 1)):
                            for r in range(2):
                                for copy in range(copies):
                                    at = HALF * (2 * copy + r)
                                    sp.dma_start(sk[at:at + HALF, part, j, :].bitcast(F32),
                                                 rot[1][HALF * j:HALF * (j + 1), 2 * (1 - part) + r, :]).then_inc(kstack_in[j], 16)

                def step(g, b, next_b):
                    st = g * NSTEP + b
                    job0 = JP + st * JS
                    sp.wait_ge(S["job_full"], job0 + JOB["k3"] + 1)
                    load_x(xs, next_b, "x_in")
                    stack_q(st + 1, st)
                    sp.wait_ge(S["job_full"], job0 + JN + 2)
                    load_x(xr, (b + 2) % NSTEP, "xr_in")
                    stack_k(st + 1)

                load_x(xr, 0, "xr_in")
                load_weights(0)
                load_x(xs, 0, "x_in")
                sp.wait_ge(S["job_full"], 8)
                load_x(xr, 1, "xr_in")
                stack_q(0, None)
                stack_k(0)
                with sp.Fori(0, NG) as g:
                    sp.wait_ge(S["w_lo_d"], (g + 1) * 3)
                    load_weights((g + 1) % NG)
                    with sp.Fori(0, NSTEP - 1) as b:
                        step(g, b, b + 1)
                    step(g, NSTEP - 1, 0)
                sp.wait_ge(S["qstack_in"], QSTACKS * (NG * NSTEP + 1))
                for j in range(HG):
                    sp.wait_ge(kstack_in[j], KSTACKS * (NG * NSTEP + 1))
                sp.wait_ge(S["x_in"], 16 * (NG * NSTEP + 1))
                sp.wait_ge(S["xr_in"], 16 * (NG * NSTEP + 2))
                sp.wait_ge(S["w_in"], 16 * (NG + 1))

            @block.gpsimd
            def _(pool):
                def split_weights(g, i):
                    pool.wait_ge(S["w_hi"], 5 * g + W_ORDER.index(i) + 1)
                    pool.tensor_tensor(w(1, 1024 * i, 1024 * i + 1024), raw[:, 1024 * i:1024 * i + 1024],
                                       w(0, 1024 * i, 1024 * i + 1024), ALU.subtract).then_inc(S["w_lo_p"], 1)

                def rotate(st, q):
                    r = rot[q]
                    pool.wait_ge(S["rot_mul"], st * 2 + q + 1)
                    pool.tensor_tensor(r[:, 0, :], r[:, 0, :], r[:, 2, :], ALU.subtract).then_inc(S["rot_add"], 1)
                    pool.tensor_tensor(r[:, 1, :], r[:, 1, :], r[:, 3, :], ALU.add).then_inc(S["rot_add"], 1)
                    pool.wait_ge(S["rot_hi"], st * 2 + q + 1)
                    pool.tensor_tensor(r[:, 0:2, :].bitcast(F32R), r[:, 0:2, :], r[:, 2:4, :],
                                       ALU.subtract).then_inc(S["rot_lo"], 1)

                split_weights(0, 3)
                split_weights(0, 1)
                rotate(0, 0)
                rotate(0, 1)
                with pool.Fori(0, NG) as g:
                    with pool.Fori(0, NSTEP - 1) as b:
                        rotate(g * NSTEP + b + 1, 0)
                        rotate(g * NSTEP + b + 1, 1)
                    split_weights(g + 1, 3)
                    rotate((g + 1) * NSTEP, 0)
                    split_weights(g + 1, 1)
                    rotate((g + 1) * NSTEP, 1)

            @block.scalar
            def _(act):
                def split_weights(i):
                    act.activation(w(0, 1024 * i, 1024 * i + 1024), raw[:, 1024 * i:1024 * i + 1024], ACT.Copy)\
                       .then_inc(S["w_hi"], 1)

                def job_hi(count, out):
                    act.wait_ge(S["job_full"], count[0] + count[1] + 1)
                    act.activation(out, PJ[count[1] % 2][:, :], ACT.Copy).then_inc(S["job_hi"], 1)

                def rot_hi(st, q):
                    act.wait_ge(S["rot_add"], st * 4 + 2 * q + 2)
                    act.activation(rot[q][:, 2:4, :].bitcast(F32R), rot[q][:, 0:2, :], ACT.Copy).then_inc(S["rot_hi"], 1)

                def step(g, b, last):
                    st = g * NSTEP + b
                    job0 = JP + st * JS

                    def out_hi(h):
                        act.wait_ge(S["pv_done"], st * UN + 2 * h + 2 + CREDIT)
                        act.activation(ot[:, 0, h, :], PO[h % 2][:, :], ACT.Copy).then_inc(S["out_hi"], 1)

                    def turn_hi(u):
                        act.wait_ge(S["turn_full"], st * UN + u + 1 + CREDIT)
                        act.wait_ge(S["pv_done"], st * UN + u - 1 + CREDIT)
                        act.activation(pt[:, u % 2, 0, :], PT[u % 2][:, :], ACT.Copy).then_inc(S["turn_hi"], 1)

                    for u in range(UN):
                        for name in UNIT_JOBS[u]:
                            if name in SPLIT:
                                job_hi((job0, JOB[name]), (qn if name[0] == "q" else kn)[:, int(name[1]) % 2, 0, :])
                        act.wait_ge(S["max_ready"], st * UN + u + 1)
                        act.wait_ge(S["turn_full"], st * UN + u - 1 + CREDIT)
                        for t in range(2):
                            i = act.activation(pr[:, u % 2, t, :], PS[u % 2][:, t * SEQ:(t + 1) * SEQ], ACT.Exp,
                                               bias=nb[:, u % 2, t:t + 1], scale=SCALE0,
                                               accum_out=sm[:, u % 2, t:t + 1])
                        i.then_inc(S["exp_ready"], 1)
                        if u >= 1:
                            turn_hi(u - 1)
                        if u >= 3 and u % 2 == 1:
                            out_hi((u - 3) // 2)
                        if u in (5, 7):
                            rot_hi(st + 1, (u - 5) // 2)
                        if last and u == 0:
                            act.wait_ge(S["w_in"], 16 * (g + 2))
                        if last and u < 2:
                            split_weights(W_ORDER[u])
                        if last and u == 5:
                            act.wait_ge(S["job_full"], job0 + JOB["k3"] + 1)
                            split_weights(W_ORDER[2])
                            split_weights(W_ORDER[3])
                    job_hi((job0, JN), kn[:, 0, 0, :])
                    job_hi((job0, JN + 1), qn[:, 1, 0, :])
                    turn_hi(UN - 1)
                    for i in range(TT):
                        if i == 2:
                            out_hi(HG - 1)
                        job_hi((job0, JV + i), v[:, 0, i, :])
                    if last:
                        act.wait_ge(S["job_full"], job0 + JO + 2)
                        split_weights(4)

                act.wait_ge(S["w_in"], 16)
                for i in W_ORDER:
                    split_weights(i)
                for i, buf in enumerate([qn[:, 0, 0, :], kn[:, 0, 0, :], qn[:, 1, 0, :]] + [v[:, 0, i, :] for i in range(TT)]):
                    job_hi((0, 5 + i), buf)
                    if i in (1, 3):
                        rot_hi(0, i // 2)
                with act.Fori(0, NG) as g:
                    with act.Fori(0, NSTEP - 1) as b:
                        step(g, b, False)
                    step(g, NSTEP - 1, True)

            @block.vector
            def _(dve):
                dve.memset(sk[DR:P, 1, :, :].bitcast(F32), 0.0)
                dve.memset(sacc[:, :, :], 0.0).then_inc(S["zeroed"], 1)
                dve.wait_ge(S["zeroed"], 1)
                dve.wait_ge(S["const_in"], 32)
                dve.sem_inc(S["job_free"], CREDIT + 1)
                dve.sem_inc(S["turn_free"], CREDIT)
                dve.sem_inc(S["out_free"], CREDIT)
                def split_weights(g, i):
                    dve.wait_ge(S["w_hi"], 5 * g + W_ORDER.index(i) + 1)
                    dve.tensor_tensor(w(1, 1024 * i, 1024 * i + 1024), raw[:, 1024 * i:1024 * i + 1024],
                                      w(0, 1024 * i, 1024 * i + 1024), ALU.subtract).then_inc(S["w_lo_d"], 1)

                def job_lo(count, j, hi, lo):
                    dve.wait_ge(S["job_hi"], count)
                    dve.tensor_tensor(lo, PJ[j % 2][:, :], hi, ALU.subtract).then_inc(S["job_free"], 1)

                def rope_half(st, job0, j, q, half):
                    if q == 0 and half == 0:
                        dve.wait_ge(S["qstack_in"], st * QSTACKS)
                    if q == 1 and half == 0:
                        for h in range(HG):
                            dve.wait_ge(kstack_in[h], st * KSTACKS)
                    dve.wait_ge(S["job_full"], job0 + j + 1)
                    for s_ in range(2):
                        slot = 2 * half + s_
                        i = dve.tensor_tensor(rot[q][:, slot, :], PJ[j % 2][:, :],
                                              tab[:, 2 * q + (s_ if half == 0 else 1 - s_), :], ALU.mult)
                    i.then_inc(S["job_free"], 1)
                    if half == 1:
                        dve.wait_ge(S["job_free"], job0 + j + 1 + CREDIT)
                        dve.sem_inc(S["rot_mul"], 1)

                def step(g, b, last):
                    st = g * NSTEP + b
                    job0, hi0 = JP + st * JS, HP + st * HI

                    def normalise(u):
                        dve.wait_ge(S["exp_ready"], st * UN + u + 1 + CREDIT)
                        dve.reciprocal(ri[:, u % 2, :], sm[:, u % 2, :]).then_inc(S["sum_inv"], 1)
                        dve.wait_ge(S["sum_inv"], st * UN + u + 1)
                        for t in range(2):
                            i = dve.tensor_scalar(pr[:, u % 2, t, :], pr[:, u % 2, t, :], ri[:, u % 2, t:t + 1],
                                                  None, ALU.mult)
                        i.then_inc(S["norm_ready"], 1)

                    def turn_lo(u):
                        dve.wait_ge(S["turn_hi"], st * UN + u + 1)
                        dve.tensor_tensor(pt[:, u % 2, 1, :], PT[u % 2][:, :], pt[:, u % 2, 0, :], ALU.subtract)\
                           .then_inc(S["turn_free"], 1)

                    def out_lo(h):
                        dve.wait_ge(S["out_hi"], st * HG + h + 1)
                        dve.tensor_tensor(ot[:, 1, h, :], PO[h % 2][:, :], ot[:, 0, h, :], ALU.subtract)\
                           .then_inc(S["out_free"], 1)

                    for u in range(UN):
                        h = u // 2
                        if u >= 1:
                            normalise(u - 1)
                        for name in UNIT_JOBS[u]:
                            if name in SPLIT:
                                buf = (qn if name[0] == "q" else kn)[:, int(name[1]) % 2]
                                job_lo(hi0 + SPLIT[name] + 1, JOB[name], buf[:, 0, :], buf[:, 1, :])
                        dve.wait_ge(S["score_full"], st * UN + u + 1)
                        dve.tensor_reduce(mx[:, u % 2, :], PS[u % 2][:, :].rearrange("p (t k) -> p t k", t=2),
                                          AX.X, ALU.max).then_inc(S["max_raw"], 1)
                        dve.wait_ge(S["max_raw"], st * UN + u + 1)
                        dve.tensor_scalar(nb[:, u % 2, :], mx[:, u % 2, :], -SCALE0, None, ALU.mult)\
                           .then_inc(S["max_ready"], 1)
                        for name in UNIT_JOBS[u]:
                            if name not in SPLIT:
                                rope_half(st + 1, job0, JOB[name], int(name[4]) // 2, int(name[4]) % 2)
                        if u >= 1:
                            turn_lo(u - 1)
                        if u >= 3 and u % 2 == 1:
                            out_lo((u - 3) // 2)
                        if last and u in (1, 5):
                            split_weights(g + 1, W_ORDER[1] if u == 1 else W_ORDER[2])
                    normalise(UN - 1)
                    job_lo(hi0 + SN + 1, JN, kn[:, 0, 0, :], kn[:, 0, 1, :])
                    job_lo(hi0 + SN + 2, JN + 1, qn[:, 1, 0, :], qn[:, 1, 1, :])
                    turn_lo(UN - 1)
                    for i in range(TT):
                        if i == 2:
                            out_lo(HG - 1)
                        job_lo(hi0 + SV + i + 1, JV + i, v[:, 0, i, :], v[:, 1, i, :])
                    for i in range(2):
                        dve.wait_ge(S["job_full"], job0 + JO + i + 1)
                        acc = sacc[:, bass.ds(b * TT + 2 * i, 2), :]
                        dve.tensor_tensor(acc, acc, PJ[i][:, :].rearrange("p (t d) -> p t d", t=2), ALU.add)\
                           .then_inc(S["job_free"], 1)
                    if last:
                        split_weights(g + 1, 4)

                for i in (2, 0, 4):
                    split_weights(0, i)
                for i in range(4):
                    rope_half(0, 0, 1 + i, i // 2, i % 2)
                for i, buf in enumerate([qn[:, 0], kn[:, 0], qn[:, 1]] + [v[:, :, i] for i in range(TT)]):
                    job_lo(i + 1, 5 + i, buf[:, 0, :], buf[:, 1, :])
                with dve.Fori(0, NG) as g:
                    with dve.Fori(0, NSTEP - 1) as b:
                        step(g, b, False)
                    step(g, NSTEP - 1, True)

            @block.tensor
            def _(pe):
                pe.wait_ge(S["const_in"], 32)
                pe.sem_inc(S["exp_ready"], CREDIT)
                pe.sem_inc(S["turn_full"], CREDIT)
                pe.sem_inc(S["pv_done"], CREDIT)
                def open_job(job0, j):
                    pe.wait_ge(S["job_free"], job0 + j - 1 + CREDIT)
                    return PJ[j % 2]

                def feature_job(x, job0, j, wcol, rows):
                    bank = open_job(job0, j)
                    for c in range(KC):
                        i = product(pe, bank[:, :], w2(wcol + c * rows, wcol + c * rows + P), x2(x, c, 0, STEP),
                                    c == 0, c == KC - 1)
                    i.then_inc(S["job_full"], 1)

                def nope(job0, j, name, x):
                    feature_job(x, job0, j, (W_Q if name[0] == "q" else W_K) + int(name[1]) * DN, HG * DN)

                def rope(job0, j, part):
                    feature_job(xr, job0, j, W_R + 512 * (part // 2) + (part % 2) * P, 2 * P)

                def value_rows(job0, j, i):
                    bank = open_job(job0, j)
                    for c in range(KC):
                        m = product(pe, bank[:, :], x2(xs, c, i * P, (i + 1) * P),
                                    w2(W_V + c * 512, W_V + (c + 1) * 512), c == 0, c == KC - 1)
                    m.then_inc(S["job_full"], 1)

                def step(g, b, last):
                    st = g * NSTEP + b
                    job0 = JP + st * JS

                    def scores(u):
                        h, bb = u // 2, u % 2
                        pe.wait_ge(S["exp_ready"], st * UN + u - 1 + CREDIT)
                        pe.wait_ge(S["job_free"], job0 + QK_DONE[h] + CREDIT)
                        if bb == 0:
                            pe.wait_ge(kstack_in[h], (st + 1) * KSTACKS)
                        if u == 0:
                            pe.wait_ge(S["qstack_in"], (st + 1) * QSTACKS)
                        for t in range(2):
                            out = PS[u % 2][:, t * SEQ:(t + 1) * SEQ]
                            a, z = bb * SEQ + t * P, bb * SEQ
                            product(pe, out, (qn[:, h % 2, 0, a:a + P], qn[:, h % 2, 1, a:a + P]),
                                    (kn[:, h % 2, 0, z:z + SEQ], kn[:, h % 2, 1, z:z + SEQ]), True, False)
                            pe.matmul(out, sq[:, h, a:a + P], sk[:, 0, h, z:z + SEQ], start=False, stop=False)
                            i = pe.matmul(out, sq[:, h, a:a + P], sk[:, 1, h, z:z + SEQ], start=False, stop=True)
                        i.then_inc(S["score_full"], 1)

                    def turn(u):
                        pe.wait_ge(S["norm_ready"], st * UN + u + 1)
                        pe.wait_ge(S["turn_free"], st * UN + u - 1 + CREDIT)
                        for kc in range(2):
                            for t in range(2):
                                i = pe.transpose(PT[u % 2][:, kc * SEQ + t * P:kc * SEQ + (t + 1) * P],
                                                 pr[:, u % 2, t, kc * P:(kc + 1) * P], ident[:, :])
                        i.then_inc(S["turn_full"], 1)

                    def values(u):
                        h, bb = u // 2, u % 2
                        pe.wait_ge(S["turn_free"], st * UN + u + 1 + CREDIT)
                        if bb == 0:
                            pe.wait_ge(S["out_free"], st * HG + h - 1 + CREDIT)
                        for kc in range(2):
                            vv = [v[:, s_, 2 * bb + kc, h * DV:(h + 1) * DV] for s_ in range(2)]
                            pp = [pt[:, u % 2, s_, kc * SEQ:(kc + 1) * SEQ] for s_ in range(2)]
                            i = product(pe, PO[h % 2][:, bb * SEQ:(bb + 1) * SEQ], vv, pp, kc == 0, kc == 1)
                        i.then_inc(S["pv_done"], 1)

                    for u in range(UN):
                        for name in UNIT_JOBS[u]:
                            if last and name == "q0+":
                                pe.wait_ge(S["w_lo_d"], 3 * (g + 1) + 2)
                            if name in SPLIT:
                                nope(job0, JOB[name], name, xr if name[-1] == "+" else xs)
                        scores(u)
                        for name in UNIT_JOBS[u]:
                            if name == "rope0":
                                pe.wait_ge(S["xr_in"], 16 * (st + 2))
                                if last:
                                    pe.wait_ge(S["w_lo_p"], 2 * (g + 1) + 1)
                            if name not in SPLIT:
                                rope(job0, JOB[name], int(name[4]))
                        if u >= 2:
                            values(u - 2)
                        if u >= 1:
                            turn(u - 1)
                    if last:
                        pe.wait_ge(S["w_lo_p"], 2 * (g + 1) + 2)
                    nope(job0, JN, "k0", xr)
                    nope(job0, JN + 1, "q1", xr)
                    values(UN - 2)
                    turn(UN - 1)
                    pe.wait_ge(S["x_in"], 16 * (st + 2))
                    for i in range(TT):
                        if i == 2:
                            values(UN - 1)
                        value_rows(job0, JV + i, i)
                    pe.wait_ge(S["w_lo_d"], 3 * (g + 1))
                    pe.wait_ge(S["out_free"], (st + 1) * HG + CREDIT)
                    for i in range(2):
                        bank = open_job(job0, JO + i)
                        for t in range(2):
                            a = (2 * i + t) * P
                            for h in range(HG):
                                m = product(pe, bank[:, t * D:(t + 1) * D],
                                            (ot[:, 0, h, a:a + P], ot[:, 1, h, a:a + P]),
                                            w2(W_O + h * D, W_O + (h + 1) * D), h == 0, h == HG - 1)
                        m.then_inc(S["job_full"], 1)

                pe.wait_ge(S["w_lo_d"], 3)
                pe.wait_ge(S["w_lo_p"], 2)
                pe.wait_ge(S["xr_in"], 16)
                pe.wait_ge(S["x_in"], 16)
                pe.sem_inc(S["job_full"], 1)
                for part in range(4):
                    rope(0, 1 + part, part)
                for i, name in enumerate(("q0", "k0", "q1")):
                    nope(0, 5 + i, name, xr)
                for i in range(TT):
                    value_rows(0, 8 + i, i)
                with pe.Fori(0, NG) as g:
                    with pe.Fori(0, NSTEP - 1) as b:
                        step(g, b, False)
                    step(g, NSTEP - 1, True)


def stage_ffn0(nc, x, wg_in, wu_in, wd_in, scale_in, scale_rest_in, sd_in, xn_dram, sacc):
    with ExitStack() as ctx:
        n = Names(nc, ctx, "f0_")
        ri = [n.sb(f"raw{i}", [P, KC, HT * P], I32) for i in range(2)] + [n.sb("raw2", [P, HT, D], I32)]
        rf = [n.sb(f"rawf{i}", [P, HT * D]) for i in range(2)]
        w = [n.sb(f"w{i}", [P, 2, HT * D], F32R) for i in range(3)]
        scale = n.sb("scale", [P, HT, 2])
        sd = n.sb("sd", [P, D])
        xs = n.sb("xs", [P, 2, 2, KC, STEP], F32R)
        xt = n.sb("x", [P, 2, TT, D])
        act_g = n.sb("act_g", [P, 2, STEP])
        hid = n.sb("hid", [P, 2, HT, STEP], F32R)
        y = n.sb("y", [P, 2, 2 * D])
        G = [n.ps(f"gate{i}") for i in range(2)]
        U = [n.ps(f"up{i}") for i in range(2)]
        Y = [n.ps(f"down{i}") for i in range(2)]
        S = {s: n.sem(s) for s in ("scale_in", "padded", "ws", "w_hi", "w_lo", "own", "up_full", "act_ready", "prod",
                                   "hid_hi", "hid_lo", "down_full", "y_ready", "y_act", "merged")}
        w_in = [n.sem(f"w_in{i}") for i in range(3)]
        x_in = [n.sem(f"x_in{i}") for i in range(NSTEP)]

        with nc.Block() as block:
            @block.sync
            def _(sp):
                for i, src in ((0, wg_in), (1, wu_in)):
                    sp.dma_start(ri[i][:, :, 0:HID], src.rearrange("(c p) n -> p c n", p=P)).then_inc(w_in[i], 16)
                sp.dma_start(ri[2][:, 0:HT - 1, :], wd_in[0:(HT - 1) * P, :].rearrange("(t p) n -> p t n", p=P)).then_inc(w_in[2], 16)
                sp.dma_start(ri[2][0:HREST, HT - 1, :], wd_in[(HT - 1) * P:HID, :]).then_inc(w_in[2], 16)
                sp.dma_start(scale[:, 0:HT - 1, :], scale_in).then_inc(S["scale_in"], 16)
                sp.dma_start(scale[0:HREST, HT - 1, :], scale_rest_in).then_inc(S["scale_in"], 16)
                sp.dma_start(sd[:, :], sd_in.rearrange("(o n) -> o n", o=1).broadcast_to([P, D])).then_inc(S["scale_in"], 16)
                for s in range(NSTEP):
                    if s >= 2:
                        sp.wait_ge(S["merged"], 2 * (s - 1))
                    sp.dma_start(xs[:, s % 2].bitcast(F32), xn_dram[s]).then_inc(x_in[s], 16)
                    sp.dma_start(xt[:, s % 2], x[STEP * s:STEP * (s + 1), :].rearrange("(t p) d -> p t d", p=P)).then_inc(x_in[s], 16)

            @block.gpsimd
            def _(pool):
                for s in range(NSTEP):
                    for t in range(HT):
                        k = HT * s + t
                        pool.wait_ge(S["hid_hi"], k + 1)
                        pool.tensor_tensor(hid[:, 1, t, :], act_g[:, k % 2, :], hid[:, 0, t, :], ALU.subtract)\
                            .then_inc(S["hid_lo"], 1)

            @block.scalar
            def _(act):
                for i in range(3):
                    act.wait_ge(S["ws"], i + 1)
                    act.activation(w[i][:, 0, :], rf[i % 2][:, :], ACT.Copy).then_inc(S["w_hi"], 1)
                act.wait_ge(S["scale_in"], 48)
                for s in range(NSTEP):
                    for t in range(HT):
                        k = HT * s + t
                        act.wait_ge(S["up_full"], k + 1)
                        if k >= 2:
                            act.wait_ge(S["hid_lo"], k - 1)
                        act.activation(act_g[:, k % 2, :], G[k % 2][:, :], ACT.Silu, scale=scale[:, t, 0:1])\
                           .then_inc(S["act_ready"], 1)
                        act.wait_ge(S["prod"], k + 1)
                        if t == 0 and s >= 1:
                            act.wait_ge(S["down_full"], 2 * s)
                        act.activation(hid[:, 0, t, :], act_g[:, k % 2, :], ACT.Copy).then_inc(S["hid_hi"], 1)
                    for i in range(2):
                        act.wait_ge(S["y_ready"], 2 * s + i + 1)
                        act.activation(y[:, i, :], y[:, i, :], ACT.Silu).then_inc(S["y_act"], 1)

            @block.vector
            def _(dve):
                dve.memset(ri[0][:, :, HID:], 128)
                dve.memset(ri[1][:, :, HID:], 128)
                dve.memset(ri[2][HREST:, HT - 1, :], 128)
                dve.memset(scale[HREST:, HT - 1, :], 0.0).then_inc(S["padded"], 1)
                dve.wait_ge(S["padded"], 1)
                for i in range(3):
                    dve.wait_ge(w_in[i], 16 if i < 2 else 32)
                    if i >= 2:
                        dve.wait_ge(S["w_lo"], i - 1)
                    dve.tensor_scalar(rf[i % 2][:, :], ri[i][:, :, :].rearrange("p a b -> p (a b)"), -128.0, None, ALU.add)\
                       .then_inc(S["ws"], 1)
                    dve.wait_ge(S["w_hi"], i + 1)
                    dve.tensor_tensor(w[i][:, 1, :], rf[i % 2][:, :], w[i][:, 0, :], ALU.subtract).then_inc(S["w_lo"], 1)
                dve.wait_ge(S["scale_in"], 48)
                for s in range(NSTEP):
                    for t in range(HT):
                        k = HT * s + t
                        dve.wait_ge(S["act_ready"], k + 1)
                        dve.scalar_tensor_tensor(out=act_g[:, k % 2, :], in0=U[k % 2][:, :], scalar=scale[:, t, 1:2],
                                                 in1=act_g[:, k % 2, :], op0=ALU.mult, op1=ALU.mult).then_inc(S["prod"], 1)
                    for i in range(2):
                        dve.wait_ge(S["down_full"], 2 * s + i + 1)
                        if s >= 1:
                            dve.wait_ge(S["merged"], 2 * (s - 1) + i + 1)
                        dve.tensor_tensor(y[:, i, :].rearrange("p (t d) -> p t d", t=2), Y[i][:, :].rearrange("p (t d) -> p t d", t=2),
                                          sd[:, :].unsqueeze(1).broadcast_to([P, 2, D]), ALU.mult).then_inc(S["y_ready"], 1)
                    dve.wait_ge(x_in[s], 32)
                    for i in range(2):
                        part = sacc[:, TT * s + 2 * i:TT * s + 2 * i + 2, :]
                        dve.wait_ge(S["y_act"], 2 * s + i + 1)
                        dve.tensor_tensor(part, part, y[:, i, :].rearrange("p (t d) -> p t d", t=2), ALU.mult).then_inc(S["own"], 1)
                        dve.wait_ge(S["own"], 2 * s + i + 1)
                        dve.tensor_tensor(part, part, xt[:, s % 2, 2 * i:2 * i + 2, :], ALU.add).then_inc(S["merged"], 1)

            @block.tensor
            def _(pe):
                pe.wait_ge(S["w_lo"], 3)
                for s in range(NSTEP):
                    pe.wait_ge(x_in[s], 32)
                    for t in range(HT):
                        k = HT * s + t
                        if k >= 2:
                            pe.wait_ge(S["prod"], k - 1)
                        for i, bank in ((0, G[k % 2]), (1, U[k % 2])):
                            for c in range(KC):
                                a = c * HT * P + t * P
                                m = product(pe, bank[:, :], (w[i][:, 0, a:a + P], w[i][:, 1, a:a + P]),
                                            (xs[:, s % 2, 0, c, :], xs[:, s % 2, 1, c, :]), c == 0, c == KC - 1)
                        m.then_inc(S["up_full"], 1)
                    pe.wait_ge(S["hid_lo"], HT * (s + 1))
                    for i in range(2):
                        if s >= 1:
                            pe.wait_ge(S["y_ready"], 2 * (s - 1) + i + 1)
                        for tt in range(2):
                            a = (2 * i + tt) * P
                            for t in range(HT):
                                m = product(pe, Y[i][:, tt * D:(tt + 1) * D], (hid[:, 0, t, a:a + P], hid[:, 1, t, a:a + P]),
                                            (w[2][:, 0, t * D:(t + 1) * D], w[2][:, 1, t * D:(t + 1) * D]),
                                            t == 0, t == HT - 1)
                        m.then_inc(S["down_full"], 1)


def stage_attention1(nc, wqkv_in, wproj_in, norm_in, bproj_in, ident_in, xn_dram, x1, s1):
    TB = SEQ // P
    QK = 2 * D
    NPAIR = H1 // 2
    BLK = 8 * 144
    SLOT_JOBS = {0: ["S7"], 4: ["V"], 5: ["P0", "P1"], 7: ["S0", "T"], 8: ["S1"], 9: ["S2", "Q0"], 10: ["S3"],
                 11: ["Q1", "S4"], 12: ["S5"], 14: ["S6"]}
    ALL = sum(SLOT_JOBS.values(), [])
    ROW_JOBS, OUT_JOBS = ["T", "Q0", "Q1"], ["P0", "P1"]
    STEP_JOBS = {
        "ahead0": ["T", "Q0", "Q1", "V"] + [f"S{p}" for p in range(NPAIR - 1)], "ahead1": ROW_JOBS,
        "first": [j for j in ALL if j not in OUT_JOBS], "middle": ALL,
        "seventh": [j for j in ALL if j not in ROW_JOBS], "last": ["S7"] + OUT_JOBS, "behind": OUT_JOBS}
    NMID = BATCH - 3
    JM = len(ALL)
    FIRST_JOB = {"ahead0": 0, "ahead1": 11, "first": 14, "middle": 26, "seventh": 26 + NMID * JM,
                 "last": 37 + NMID * JM, "behind": 40 + NMID * JM}
    BY_ACT = {0, 1, 2, 3, 5, 7}
    OWN = 2 * TB + 10
    with ExitStack() as ctx:
        n = Names(nc, ctx, "a1_")
        ident = n.sb("ident", [P, P])
        raw = n.sb("raw", [P, KC, 3 * D])
        rawp = n.sb("rawp", [P, KC, D])
        w = n.sb("w", [P, 2, KC, 3 * D], F32R)
        wp = n.sb("wp", [P, 2, KC, D], F32R)
        nw = n.sb("nw", [P, QK])
        nqk = n.sb("nqk", [P, D])
        bp = n.sb("bp", [P, D])
        mhalf = n.sb("mhalf", [P, 64])
        xt = n.sb("x", [P, TB, D])
        stats, mv = n.sb("stats", [P, TB, 6]), n.sb("mv", [P, TB, 2])
        ve, rs, tmp = n.sb("ve", [P, TB]), n.sb("rs", [P, TB]), n.sb("tmp", [P, TB])
        xs = n.sb("xs", [P, 2, KC, SEQ], F32R)
        qk = n.sb("qk", [P, TB, QK])
        sqr = n.sb("sqr", [P, TB, QK])
        ss, rq, tq = n.sb("ss", [P, 64]), n.sb("rq", [P, 64]), n.sb("tq", [P, 64])
        stq = n.sb("stq", [P, TB, H1, 4, D1])
        stk = n.sb("stk", [P, TB, H1, 4, D1])
        stack = n.sb("stack", [P, NPAIR, 2 * SEQ], F32R)
        vc = n.sb("vc", [P, 2, TB * D], F32R)
        vp = n.sb("vp", [P, 2, TB, 2, BLK], F32R)
        pr = n.sb("pr", [P, 4, 2, SEQ])
        pt = n.sb("pt", [P, 2, 2, 512], F32R)
        ot = n.sb("ot", [P, 2, 2, SEQ], F32R)
        nb, sm, ri = (n.sb(s, [P, 4, 2]) for s in ("nb", "sm", "ri"))
        PJ = [n.ps(f"job{i}") for i in range(2)]
        PS = [n.ps(f"score{i}") for i in range(2)]
        PT = [n.ps(f"turn{i}") for i in range(2)]
        PO = [n.ps(f"out{i}") for i in range(2)]
        job_free = [n.sem(f"job_free{i}") for i in range(2)]
        S = {s: n.sem(s) for s in (
            "const_in", "w_in", "w_hi", "w_lo", "mhalf_ready", "nqk_raw", "nqk_ready", "zeroed", "own", "stats_seen",
            "x_copied", "ve_ready", "rs_ready", "xn_ready", "job_full", "xs_hi", "v_hi", "sq_ready", "ms_ready", "rq_ready", "waited",
            "scaled", "weighted", "k_hi", "q_hi", "k_lo", "q_lo", "spread_hi", "spread_lo", "stored", "score_full",
            "max_ready", "exp_ready", "sum_inv", "norm_ready", "turn_full", "turn_free", "turn_hi", "pv_done", "out_hi",
            "out_free")}

        def job(kind, b, name):
            at = STEP_JOBS[kind].index(name)
            if kind == "middle":
                first = FIRST_JOB[kind] - JM
                return b * JM + (first + at + 1), b * (JM // 2) + (first // 2 + at // 2), at % 2
            at += FIRST_JOB[kind]
            return at + 1, at // 2, at % 2

        def slot_jobs(kind, u):
            return [j for j in SLOT_JOBS.get(u, []) if j in STEP_JOBS[kind]]

        def stack_job(kind, b, p):
            if p == NPAIR - 1:
                return job(kind, b, "S7")
            before = {"first": "ahead0", "middle": "middle", "seventh": "middle", "last": "seventh"}[kind]
            return job(before, b - 1, f"S{p}")

        def flow(step, engine):
            step("first", 0)
            with engine.Fori(1, 1 + NMID) as b:
                step("middle", b)
            step("seventh", BATCH - 2)
            step("last", BATCH - 1)
            step("behind", BATCH)

        def bc(ap, shape):
            return ap.broadcast_to(shape)

        def heads(buf, t, part):
            return bc(buf[:, t, part * D:(part + 1) * D].rearrange("p (h d) -> p h d", d=D1).unsqueeze(2), [P, H1, 2, D1])

        def spread(part, a):
            return (vp[:, part, :, a, :].rearrange("p t (e w) -> p t e w", w=144)[:, :, :, 0:D1],
                    vc[:, part, :].rearrange("p (t a e d) -> p t a e d", t=TB, a=2, d=D1)[:, :, a])

        with nc.Block() as block:
            @block.sync
            def _(sp):
                sp.dma_start(raw[:, :, :], wqkv_in.rearrange("(c p) n -> p c n", p=P)).then_inc(S["w_in"], 16)
                sp.dma_start(rawp[:, :, :], wproj_in.rearrange("(c p) n -> p c n", p=P)).then_inc(S["w_in"], 16)
                sp.dma_start(ident[:, :], ident_in).then_inc(S["const_in"], 16)
                sp.dma_start(nw[:, :], norm_in.broadcast_to([P, QK])).then_inc(S["const_in"], 16)
                sp.dma_start(bp[:, :], bproj_in.broadcast_to([P, D])).then_inc(S["const_in"], 16)

                def store(kind, b, batch):
                    _, before, bank = job(kind, b, "T")
                    sp.wait_ge(job_free[bank], before + 1)
                    sp.dma_start(xn_dram[bass.ds(batch, 1)].rearrange("o p s c n -> p (o s c n)"),
                                 xs[:, :, :, :].bitcast(F32).rearrange("p s c n -> p (s c n)")).then_inc(S["stored"], 16)

                store("ahead0", None, 0)
                store("ahead1", None, 1)
                store("first", 0, 2)
                with sp.Fori(1, 1 + NMID) as b:
                    store("middle", b, b + 2)
                sp.wait_ge(S["stored"], 16 * BATCH)

            @block.gpsimd
            def _(pool):
                pool.memset(mhalf[:, :], -0.5).then_inc(S["mhalf_ready"], 1)
                pool.wait_ge(S["mhalf_ready"], 1)

                def copy_x(m):
                    pool.wait_ge(S["xs_hi"], m)
                    pool.sem_inc(S["waited"], 1)
                    pool.tensor_copy(xt[:, :, :], x1[:, bass.ds(m * TB, TB), :]).then_inc(S["x_copied"], 1)

                def pow_x(m):
                    pool.wait_ge(S["ve_ready"], m + 1)
                    pool.tensor_tensor(rs[:, :], ve[:, :], mhalf[:, 0:TB], ALU.pow).then_inc(S["rs_ready"], 1)

                def pow_rms(m):
                    pool.wait_ge(S["ms_ready"], m + 1)
                    pool.tensor_tensor(rq[:, :], ss[:, :], mhalf[:, :], ALU.pow).then_inc(S["rq_ready"], 1)

                def weigh(m):
                    pool.wait_ge(S["scaled"], m + 1)
                    pool.tensor_tensor(qk[:, :, 0:D], qk[:, :, 0:D], bc(nqk[:, :].unsqueeze(1), [P, TB, D]), ALU.mult)\
                        .then_inc(S["weighted"], 1)

                def q_lo(m, t):
                    pool.wait_ge(S["q_hi"], m * TB + t + 1)
                    pool.tensor_tensor(stq[:, t, :, 1::2, :].bitcast(F32R), heads(qk, t, 0), stq[:, t, :, 0::2, :],
                                       ALU.subtract).then_inc(S["q_lo"], 1)

                def spread_lo(m, a, seen):
                    if seen is not None:
                        pool.wait_ge(S["pv_done"], seen)
                    pool.sem_inc(S["waited"], 1)
                    to, of = spread(1, a)
                    pool.tensor_copy(to, of).then_inc(S["spread_lo"], 1)

                def step(kind, b):
                    first, units = kind == "first", kind != "behind"
                    rows, nxt = "T" in STEP_JOBS[kind], "V" in STEP_JOBS[kind]
                    for u in range(H1 if units else 1):
                        if u >= 1 or not first:
                            pool.wait_ge(S["sum_inv"], b * H1 + u)
                            e = pr[:, (u - 1) % 4]
                            pool.tensor_tensor(e, e, bc(ri[:, (u - 1) % 4, :].unsqueeze(2), [P, 2, SEQ]), ALU.mult)\
                                .then_inc(S["norm_ready"], 1)
                        if nxt and u == 0:
                            weigh(b + 1)
                        if rows and u == 1:
                            copy_x(b + 2)
                        if rows and u == 3:
                            pow_x(b + 2)
                        if units and u == 4:
                            spread_lo(b, 1, None if first else b * H1)
                        if nxt and u in (3, 4):
                            q_lo(b + 1, u - 3)
                        if nxt and u == 13:
                            pool.wait_ge(job_free[job(kind, b, "V")[2]], job(kind, b, "V")[1] + 1)
                            spread_lo(b + 1, 0, b * H1 + 8)
                        if rows and u == 14:
                            pow_rms(b + 2)

                pool.tensor_copy(xt[:, :, :], x1[:, 0:TB, :]).then_inc(S["x_copied"], 1)
                pool.wait_ge(S["const_in"], 48)
                pool.tensor_tensor(nqk[:, :], nw[:, 0:D], nw[:, D:QK], ALU.mult).then_inc(S["nqk_raw"], 1)
                pool.wait_ge(S["nqk_raw"], 1)
                pool.tensor_scalar(nqk[:, :], nqk[:, :], SCALE1, None, ALU.mult).then_inc(S["nqk_ready"], 1)
                pool.wait_ge(S["nqk_ready"], 1)
                pow_x(0)
                copy_x(1)
                pow_rms(0)
                weigh(0)
                for t in range(TB):
                    q_lo(0, t)
                pool.wait_ge(job_free[job("ahead0", 0, "V")[2]], job("ahead0", 0, "V")[1] + 1)
                pool.wait_ge(S["zeroed"], 1)
                spread_lo(0, 0, None)
                pow_x(1)
                pow_rms(1)
                flow(step, pool)

            @block.scalar
            def _(act):
                act.wait_ge(S["w_in"], 32)
                act.activation(w[:, 0, :, :], raw[:, :, :], ACT.Copy).then_inc(S["w_hi"], 1)
                act.activation(wp[:, 0, :, :], rawp[:, :, :], ACT.Copy).then_inc(S["w_hi"], 1)

                def job_out(kind, b, name, m):
                    full, _, bank = job(kind, b, name)
                    act.wait_ge(S["job_full"], full)
                    if name == "T":
                        if kind != "ahead0":
                            act.wait_ge(S["stored"], m * 16)
                        act.activation(xs[:, 0, :, :].rearrange("p c n -> p (c n)"), PJ[bank][:, :], ACT.Copy)\
                           .then_inc(S["xs_hi"], 1)
                    elif name == "V":
                        if kind != "ahead0":
                            act.wait_ge(S["spread_hi"], 2 * (m - 1))
                        act.activation(vc[:, 0, :], PJ[bank][:, :], ACT.Copy).then_inc(S["v_hi"], 1)
                    elif name[0] == "Q":
                        if kind != "ahead0":
                            act.wait_ge(S["ms_ready"], m)
                        act.activation(sqr[:, int(name[1]), :], PJ[bank][:, :], ACT.Square).then_inc(S["sq_ready"], 1)
                    elif name[0] == "S" and int(name[1]) in BY_ACT:
                        act.activation(stack[:, int(name[1]), :], PJ[bank][:, :], ACT.Copy).then_inc(job_free[bank], 1)

                def k_hi(m):
                    act.wait_ge(S["scaled"], m + 1)
                    for t in range(TB):
                        act.activation(stk[:, t, :, 0:2, :].bitcast(F32R), heads(qk, t, 1), ACT.Copy).then_inc(S["k_hi"], 1)

                def q_hi(m):
                    act.wait_ge(S["weighted"], m + 1)
                    for t in range(TB):
                        act.activation(stq[:, t, :, 0::2, :].bitcast(F32R), heads(qk, t, 0), ACT.Copy).then_inc(S["q_hi"], 1)

                def spread_hi(m, a, seen):
                    act.wait_ge(S["v_hi"], m + 1)
                    if seen is not None:
                        act.wait_ge(S["pv_done"], seen)
                    to, of = spread(0, a)
                    act.activation(to, of, ACT.Copy).then_inc(S["spread_hi"], 1)

                def out_hi(seen, a):
                    act.wait_ge(S["pv_done"], seen)
                    act.activation(ot[:, 0, a, :], PO[a][:, 0:SEQ], ACT.Copy).then_inc(S["out_hi"], 1)

                def step(kind, b):
                    first, units = kind == "first", kind != "behind"
                    nxt = "V" in STEP_JOBS[kind]
                    for u in range(H1 if units else 5):
                        if units:
                            act.wait_ge(S["max_ready"], b * H1 + u + 1)
                            if u >= 4 or not first:
                                act.wait_ge(S["turn_full"], b * H1 + u - 3)
                            for t in range(2):
                                i = act.activation(pr[:, u % 4, t, :], PS[u % 2][:, t * SEQ:(t + 1) * SEQ], ACT.Exp,
                                                   bias=nb[:, u % 4, t:t + 1], accum_out=sm[:, u % 4, t:t + 1])
                            i.then_inc(S["exp_ready"], 1)
                        if u == 4:
                            if not first:
                                out_hi(b * H1, 1)
                            if units:
                                spread_hi(b, 1, None)
                        for name in slot_jobs(kind, u):
                            job_out(kind, b, name, b + 2)
                        if (u >= 2 or not first) and (units or u < 2):
                            act.wait_ge(S["turn_full"], b * H1 + u - 1)
                            if u >= 4 or not first:
                                act.wait_ge(S["pv_done"], b * H1 + u - 3)
                            act.activation(pt[:, u % 2, 0, :], PT[u % 2][:, :], ACT.Copy).then_inc(S["turn_hi"], 1)
                        if nxt and u == 1:
                            k_hi(b + 1)
                        if nxt and u == 2:
                            q_hi(b + 1)
                        if u == 12:
                            out_hi(b * H1 + 8, 0)
                            if nxt:
                                spread_hi(b + 1, 0, None)

                for name in ("T", "Q0", "Q1", "V"):
                    job_out("ahead0", 0, name, 0)
                act.wait_ge(S["zeroed"], 1)
                spread_hi(0, 0, None)
                k_hi(0)
                q_hi(0)
                for p in range(NPAIR - 1):
                    job_out("ahead0", 0, f"S{p}", 0)
                for name in ROW_JOBS:
                    job_out("ahead1", 0, name, 1)
                flow(step, act)

            @block.vector
            def _(dve):
                def stats_x(m):
                    dve.wait_ge(S["x_copied"], m + 1)
                    k = norm_stats(dve, S["own"], S["stats_seen"], m * OWN, xt, stats, mv, ve[:, :], TB, LN_EPS)
                    dve.wait_ge(S["own"], k)
                    dve.sem_inc(S["ve_ready"], 1)

                def norm_x(m):
                    dve.wait_ge(S["rs_ready"], m + 1)
                    polish_rsqrt(dve, S["own"], m * OWN + 2 * TB + 1, rs[:, :], ve[:, :], tmp[:, :])
                    for t in range(TB):
                        i = dve.tensor_scalar(xt[:, t, :], xt[:, t, :], mv[:, t, 0:1], rs[:, t:t + 1], ALU.subtract, ALU.mult)
                    i.then_inc(S["xn_ready"], 1)

                def job_out(kind, b, name, m):
                    full, _, bank = job(kind, b, name)
                    if name == "T":
                        dve.wait_ge(S["xs_hi"], m + 1)
                        dve.tensor_tensor(xs[:, 1, :, :].rearrange("p c n -> p (c n)"), PJ[bank][:, :],
                                          xs[:, 0, :, :].rearrange("p c n -> p (c n)"), ALU.subtract).then_inc(job_free[bank], 1)
                    elif name == "V":
                        dve.wait_ge(S["v_hi"], m)
                        if kind != "ahead0":
                            dve.wait_ge(S["spread_lo"], 2 * (m - 1))
                        dve.tensor_tensor(vc[:, 1, :], PJ[bank][:, :], vc[:, 0, :], ALU.subtract).then_inc(job_free[bank], 1)
                    elif name[0] == "Q":
                        t = int(name[1])
                        dve.wait_ge(S["sq_ready"], m * TB + t + 1)
                        if kind != "ahead0" and t == 0:
                            dve.wait_ge(S["q_lo"], m * TB)
                            dve.wait_ge(S["k_lo"], m * TB)
                        dve.tensor_copy(qk[:, t, :], PJ[bank][:, :]).then_inc(job_free[bank], 1)
                    elif name[0] == "S" and int(name[1]) not in BY_ACT:
                        dve.wait_ge(S["job_full"], full)
                        dve.tensor_copy(stack[:, int(name[1]), :], PJ[bank][:, :]).then_inc(job_free[bank], 1)
                    elif name[0] == "P":
                        t = int(name[1])
                        dve.wait_ge(S["job_full"], full)
                        dve.tensor_tensor(s1[:, bass.ds((b - 1) * TB + t, 1), :], PJ[bank][:, 0:D].unsqueeze(1),
                                          bp[:, :].unsqueeze(1), ALU.add).then_inc(job_free[bank], 1)

                def sum_squares(m):
                    dve.wait_ge(S["sq_ready"], (m + 1) * TB)
                    dve.tensor_reduce(ss[:, :], sqr[:, :, :].rearrange("p t (g d) -> p (t g) d", d=D1), AX.X, ALU.add)\
                       .then_inc(S["own"], 1)
                    dve.wait_ge(S["own"], m * OWN + 2 * TB + 6)
                    dve.tensor_scalar(ss[:, :], ss[:, :], 1.0 / D1, RMS_EPS, ALU.mult, ALU.add).then_inc(S["ms_ready"], 1)

                def scale_rows(kind, b, m):
                    dve.wait_ge(S["rq_ready"], m + 1)
                    polish_rsqrt(dve, S["own"], m * OWN + 2 * TB + 6, rq[:, :], ss[:, :], tq[:, :])
                    for name in ("Q0", "Q1"):
                        _, before, bank = job(kind, b, name)
                        dve.wait_ge(job_free[bank], before + 1)
                    dve.tensor_tensor(qk[:, :, :].rearrange("p t (g d) -> p (t g) d", d=D1),
                                      qk[:, :, :].rearrange("p t (g d) -> p (t g) d", d=D1),
                                      bc(rq[:, :].unsqueeze(2), [P, 64, D1]), ALU.mult).then_inc(S["scaled"], 1)

                def k_lo(m, t):
                    dve.wait_ge(S["k_hi"], m * TB + t + 1)
                    dve.tensor_tensor(stk[:, t, :, 2:4, :].bitcast(F32R), heads(qk, t, 1), stk[:, t, :, 0:2, :],
                                      ALU.subtract).then_inc(S["k_lo"], 1)

                def out_lo(count, a):
                    dve.wait_ge(S["out_hi"], count)
                    dve.tensor_tensor(ot[:, 1, a, :], PO[a][:, 0:SEQ], ot[:, 0, a, :], ALU.subtract).then_inc(S["out_free"], 1)

                def step(kind, b):
                    first, units = kind == "first", kind != "behind"
                    rows, nxt = "T" in STEP_JOBS[kind], "V" in STEP_JOBS[kind]
                    for u in range(H1 if units else 7):
                        if (u >= 1 or not first) and (units or u < 1):
                            dve.wait_ge(S["exp_ready"], b * H1 + u)
                            dve.reciprocal(ri[:, (u - 1) % 4, :], sm[:, (u - 1) % 4, :]).then_inc(S["sum_inv"], 1)
                        if units:
                            dve.wait_ge(S["score_full"], b * H1 + u + 1)
                            dve.tensor_reduce(nb[:, u % 4, :], PS[u % 2][:, :].rearrange("p (t k) -> p t k", t=2), AX.X,
                                              ALU.max, negate=True).then_inc(S["max_ready"], 1)
                        for name in slot_jobs(kind, u):
                            if name[0] == "S":
                                job_out(kind, b, name, b + 2)
                        for name in slot_jobs(kind, u - 1):
                            if name[0] != "S":
                                job_out(kind, b, name, b + 2)
                        if (u >= 3 or not first) and (units or u < 3):
                            dve.wait_ge(S["turn_hi"], b * H1 + u - 2)
                            dve.tensor_tensor(pt[:, (u - 3) % 2, 1, :], PT[(u - 3) % 2][:, :], pt[:, (u - 3) % 2, 0, :],
                                              ALU.subtract).then_inc(S["turn_free"], 1)
                        if nxt and u in (2, 3):
                            k_lo(b + 1, u - 2)
                        if rows and u == 2:
                            stats_x(b + 2)
                        if u == 4 and not first:
                            out_lo(b * 2, 1)
                        if rows and u == 4:
                            norm_x(b + 2)
                        if rows and u == 13:
                            sum_squares(b + 2)
                        if u == 13:
                            out_lo(b * 2 + 1, 0)
                        if rows and u == 15:
                            scale_rows(kind, b, b + 2)

                stats_x(0)
                dve.wait_ge(S["w_hi"], 2)
                dve.tensor_tensor(w[:, 1, :, :], raw[:, :, :], w[:, 0, :, :], ALU.subtract).then_inc(S["w_lo"], 1)
                norm_x(0)
                dve.memset(vp[:, :, :, :, :].bitcast(F32), 0.0).then_inc(S["zeroed"], 1)
                dve.tensor_tensor(wp[:, 1, :, :], rawp[:, :, :], wp[:, 0, :, :], ALU.subtract).then_inc(S["w_lo"], 1)
                dve.wait_ge(S["const_in"], 48)
                for name in ("T", "Q0", "Q1", "V"):
                    job_out("ahead0", 0, name, 1 if name == "V" else 0)
                sum_squares(0)
                scale_rows("ahead0", 0, 0)
                for t in range(TB):
                    k_lo(0, t)
                stats_x(1)
                norm_x(1)
                for p in range(NPAIR - 1):
                    job_out("ahead0", 0, f"S{p}", 0)
                for name in ROW_JOBS:
                    job_out("ahead1", 0, name, 1)
                sum_squares(1)
                scale_rows("ahead1", 0, 1)
                flow(step, dve)

            @block.tensor
            def _(pe):
                pe.wait_ge(S["const_in"], 48)

                def do_job(kind, b, name, m):
                    full, before, bank = job(kind, b, name)
                    if kind != "ahead0" or before > 0:
                        pe.wait_ge(job_free[bank], before)
                    out = PJ[bank]
                    if name == "T":
                        pe.wait_ge(S["xn_ready"], m + 1)
                        for c in range(KC):
                            for t in range(TB):
                                i = pe.transpose(out[:, c * SEQ + t * P:c * SEQ + (t + 1) * P], xt[:, t, c * P:(c + 1) * P],
                                                 ident[:, :])
                    elif name[0] == "Q":
                        t = int(name[1])
                        if t == 0:
                            _, t_before, t_bank = job(kind, b, "T")
                            pe.wait_ge(job_free[t_bank], t_before + 1)
                        for c in range(KC):
                            i = product(pe, out[:, :], [xs[:, s, c, t * P:(t + 1) * P] for s in range(2)],
                                        [w[:, s, c, 0:QK] for s in range(2)], c == 0, c == KC - 1)
                    elif name == "V":
                        for t in range(TB):
                            for c in range(KC):
                                i = product(pe, out[:, t * D:(t + 1) * D], [xs[:, s, c, t * P:(t + 1) * P] for s in range(2)],
                                            [w[:, s, c, QK:QK + D] for s in range(2)], c == 0, c == KC - 1)
                    elif name[0] == "S":
                        p = int(name[1])
                        for k, rows in enumerate((stq, stk)):
                            for t in range(TB):
                                i = pe.transpose(out[:, k * SEQ + t * P:k * SEQ + (t + 1) * P],
                                                 rows[:, t, 2 * p:2 * p + 2, :, :].rearrange("p h r d -> p (h r d)"), ident[:, :])
                    else:
                        t = int(name[1])
                        if t == 0:
                            pe.wait_ge(S["out_free"], b * 2)
                        for a in range(2):
                            i = product(pe, out[:, 0:D], [ot[:, s, a, t * P:(t + 1) * P] for s in range(2)],
                                        [wp[:, s, a, :] for s in range(2)], a == 0, a == 1)
                    i.then_inc(S["job_full"], 1)

                def step(kind, b):
                    first, units = kind == "first", kind != "behind"

                    def values(r):
                        u = r % H1
                        a, e = u // 8, u % 8
                        pe.wait_ge(S["turn_free"], b * H1 + r + 1)
                        if e == 0:
                            pe.wait_ge(S["spread_hi"], b * 2 + a + 1)
                            pe.wait_ge(S["spread_lo"], b * 2 + a + 1)
                            if not first:
                                pe.wait_ge(S["out_free"], b * 2 + a - 1)
                        for kc in range(2):
                            m = product(pe, PO[a][:, 0:SEQ], [vp[:, s, kc, a, e * P:(e + 1) * P] for s in range(2)],
                                        [pt[:, u % 2, s, kc * SEQ:(kc + 1) * SEQ] for s in range(2)],
                                        e == 0 and kc == 0, e == 7 and kc == 1)
                        m.then_inc(S["pv_done"], 1)

                    for u in range(H1 if units else 6):
                        if units:
                            p, at = u // 2, 64 * (u % 2)
                            if u >= 2 or not first:
                                pe.wait_ge(S["exp_ready"], b * H1 + u - 1)
                            if u % 2 == 0:
                                _, before, bank = stack_job(kind, b, p)
                                pe.wait_ge(job_free[bank], before + 1)
                            for t in range(2):
                                m = pe.matmul(PS[u % 2][:, t * SEQ:(t + 1) * SEQ], stack[at:at + 64, p, t * P:(t + 1) * P],
                                              stack[at:at + 64, p, SEQ:2 * SEQ], start=True, stop=True)
                            m.then_inc(S["score_full"], 1)
                        for name in slot_jobs(kind, u):
                            if name == "S0":
                                pe.wait_ge(S["q_lo"], (b + 2) * TB)
                                pe.wait_ge(S["k_lo"], (b + 2) * TB)
                            do_job(kind, b, name, b + 2)
                        if (u >= 4 or not first) and (units or u < 4):
                            values(u - 4)
                        if (u >= 2 or not first) and (units or u < 2):
                            pe.wait_ge(S["norm_ready"], b * H1 + u - 1)
                            if u >= 4 or not first:
                                pe.wait_ge(S["turn_free"], b * H1 + u - 3)
                            for kc in range(2):
                                for t in range(2):
                                    m = pe.transpose(PT[u % 2][:, kc * SEQ + t * P:kc * SEQ + (t + 1) * P],
                                                     pr[:, (u - 2) % 4, t, kc * P:(kc + 1) * P], ident[:, :])
                            m.then_inc(S["turn_full"], 1)

                do_job("ahead0", 0, "T", 0)
                pe.wait_ge(S["w_lo"], 2)
                for name in STEP_JOBS["ahead0"][1:]:
                    if name == "S0":
                        pe.wait_ge(S["q_lo"], TB)
                        pe.wait_ge(S["k_lo"], TB)
                    do_job("ahead0", 0, name, 0)
                for name in ROW_JOBS:
                    do_job("ahead1", 0, name, 1)
                flow(step, pe)


def stage_moe(nc, a, xn_dram, x1, s1, out):
    ROUT = ME * P
    OWN = 19
    with ExitStack() as ctx:
        n = Names(nc, ctx, "m_")
        ident = n.sb("ident", [P, P])
        raw = n.sb("raw", [P, MT * D])
        w = [n.sb(f"w{i}", [P, 2, MT * D], F32R) for i in range(3)]
        rr, rw = n.sb("rr", [P, KC, E]), n.sb("rw", [P, 2, KC, E], F32R)
        sel_raw, sel = n.sb("sel_raw", [2 * E, ROUT]), n.sb("sel", [2 * E, ROUT], F32R)
        rank = n.sb("rank", [P, E])
        bias = n.sb("bias", [P, MT, 2])
        db = n.sb("db", [P, D])
        xs = n.sb("xs", [P, 2, KC, STEP], F32R)
        lg, eq, oh, oh2 = (n.sb(s, [P, TT, E]) for s in ("lg", "eq", "oh", "oh2"))
        m1 = n.sb("m1", [P, TT])
        cm = n.sb("cm", [P, TT, 2, E])
        ct = n.sb("ct", [2 * E, STEP], F32R)
        g = n.sb("g", [P, 2, STEP])
        hid = n.sb("hid", [P, 2, 2, STEP], F32R)
        y = n.sb("y", [P, 2, 2 * D])
        G = [n.ps(f"gate{i}") for i in range(2)]
        U = [n.ps(f"up{i}") for i in range(2)]
        C = [n.ps(f"comb{i}") for i in range(2)]
        Y = [n.ps(f"down{i}") for i in range(2)]
        S = {s: n.sem(s) for s in ("const_in", "w_hi", "w_lo", "raw_used", "zeroed", "own", "x_in", "x_used", "logits",
                                   "lg_ready", "exp_ready", "cm_hi", "cm_ready", "ct_turned", "ct_ready", "up_full", "act_ready",
                                   "prod", "comb_read", "hid_hi", "hid_lo", "down_done", "y_ready", "y_act", "merged", "stored")}
        w_in = [n.sem(f"w_in{i}") for i in range(3)]

        def split(i):
            return w[i][:, 0, :], w[i][:, 1, :]

        with nc.Block() as block:
            @block.sync
            def _(sp):
                sp.dma_start(ident[:, :], a["ident"]).then_inc(S["const_in"], 16)
                sp.dma_start(rr[:, :, :], a["router"].rearrange("(c p) e -> p c e", p=P)).then_inc(S["const_in"], 16)
                sp.dma_start(sel_raw[:, :], a["select"]).then_inc(S["const_in"], 16)
                sp.dma_start(rank[:, :], a["rank"].broadcast_to([P, E])).then_inc(S["const_in"], 16)
                sp.dma_start(db[:, :], a["down_b"].broadcast_to([P, D])).then_inc(S["const_in"], 16)
                sp.wait_ge(S["zeroed"], 1)
                sp.dma_start(bias[:, ME:MT - 1, :], a["bias"]).then_inc(S["const_in"], 16)
                sp.dma_start(bias[0:MREST, MT - 1, :], a["bias_rest"]).then_inc(S["const_in"], 16)
                for i, name in enumerate(("gate", "up")):
                    if i:
                        sp.wait_ge(S["w_lo"], i)
                    dst = raw[:, :].rearrange("p (c n) -> p c n", c=KC)
                    sp.dma_start(dst[:, :, 0:ROUT], a[name].rearrange("(c p) n -> p c n", p=P)).then_inc(w_in[i], 16)
                    sp.dma_start(dst[:, :, ROUT:MW], a["s_" + name].rearrange("(c p) n -> p c n", p=P)).then_inc(w_in[i], 16)
                sp.wait_ge(S["raw_used"], 1)
                dst = raw[:, :].rearrange("p (t n) -> p t n", t=MT)
                sp.dma_start(dst[:, 0:ME, :], a["down"].rearrange("(t p) n -> p t n", p=P)).then_inc(w_in[2], 16)
                sp.dma_start(dst[:, ME:MT - 1, :], a["s_down"][0:(MT - 1 - ME) * P, :].rearrange("(t p) n -> p t n", p=P))\
                  .then_inc(w_in[2], 16)
                sp.dma_start(dst[0:MREST, MT - 1, :], a["s_down"][(MT - 1 - ME) * P:SI, :]).then_inc(w_in[2], 16)
                with sp.Fori(0, NSTEP) as s:
                    sp.wait_ge(S["x_used"], s)
                    for half in range(2):
                        sp.dma_start(xs[:, :, :, half * SEQ:(half + 1) * SEQ].bitcast(F32),
                                     xn_dram[bass.ds(2 * s + half, 1)].rearrange("o p s c n -> p (o s) c n")).then_inc(S["x_in"], 16)
                    sp.wait_ge(S["merged"], 2 * s + 2)
                    sp.dma_start(out[bass.ds(s, 1)].rearrange("o (t p) d -> p (o t) d", p=P),
                                 x1[:, bass.ds(s * TT, TT), :]).then_inc(S["stored"], 16)
                sp.wait_ge(S["stored"], 16 * NSTEP)

            @block.gpsimd
            def _(pool):
                with pool.Fori(0, NSTEP) as s:
                    for t in range(MT):
                        pool.wait_ge(S["hid_hi"], s * MT + t + 1)
                        pool.tensor_tensor(hid[:, t % 2, 1, :], g[:, t % 2, :], hid[:, t % 2, 0, :], ALU.subtract)\
                            .then_inc(S["hid_lo"], 1)

            @block.scalar
            def _(act):
                act.wait_ge(S["const_in"], 112)
                act.activation(rw[:, 0, :, :], rr[:, :, :], ACT.Copy).then_inc(S["w_hi"], 1)
                act.activation(sel[:, :], sel_raw[:, :], ACT.Copy).then_inc(S["w_hi"], 1)
                for i in range(3):
                    act.wait_ge(w_in[i], 32 if i < 2 else 48)
                    act.activation(w[i][:, 0, :], raw[:, :], ACT.Copy).then_inc(S["w_hi"], 1)
                with act.Fori(0, NSTEP) as s:
                    act.wait_ge(S["lg_ready"], s + 1)
                    act.activation(lg[:, :, :], lg[:, :, :], ACT.Exp).then_inc(S["exp_ready"], 1)
                    act.wait_ge(S["cm_hi"], s + 1)
                    act.activation(cm[:, :, 0, :].bitcast(F32R), oh[:, :, :], ACT.Copy).then_inc(S["cm_ready"], 1)
                    act.wait_ge(S["ct_turned"], s + 1)
                    act.activation(ct[:, :], C[1][0:2 * E, :], ACT.Copy).then_inc(S["ct_ready"], 1)
                    for t in range(MT):
                        act.wait_ge(S["up_full"], s * MT + t + 1)
                        act.wait_ge(S["hid_lo"], s * MT + t - 1 + CREDIT)
                        act.activation(g[:, t % 2, :], G[t % 2][:, :], ACT.Silu, bias=bias[:, t, 0:1]).then_inc(S["act_ready"], 1)
                        act.wait_ge(S["comb_read"], s * MT + t + 1 + CREDIT)
                        act.wait_ge(S["down_done"], s * MT + t - 1 + CREDIT)
                        act.activation(hid[:, t % 2, 0, :], g[:, t % 2, :], ACT.Copy).then_inc(S["hid_hi"], 1)
                    for i in range(2):
                        act.wait_ge(S["y_ready"], 2 * s + i + 1 + CREDIT)
                        act.activation(y[:, i, :], y[:, i, :], ACT.Silu).then_inc(S["y_act"], 1)

            @block.vector
            def _(dve):
                pad = raw[:, :].rearrange("p (c n) -> p c n", c=KC)
                dve.memset(pad[:, :, MW:], 0.0)
                dve.memset(bias[:, :, :], 0.0).then_inc(S["zeroed"], 1)
                dve.wait_ge(S["w_hi"], 1)
                dve.tensor_tensor(rw[:, 1, :, :], rr[:, :, :], rw[:, 0, :, :], ALU.subtract).then_inc(S["own"], 1)
                for i in range(3):
                    dve.wait_ge(S["w_hi"], i + 3)
                    dve.tensor_tensor(w[i][:, 1, :], raw[:, :], w[i][:, 0, :], ALU.subtract).then_inc(S["w_lo"], 1)
                    if i == 1:
                        dve.wait_ge(S["w_lo"], 2)
                        dve.memset(raw[96:P, (MT - 1) * D:], 0.0).then_inc(S["raw_used"], 1)
                dve.wait_ge(S["const_in"], 112)
                for s_ in ("hid_lo", "comb_read", "y_ready"):
                    dve.sem_inc(S[s_], CREDIT)
                with dve.Fori(0, NSTEP) as s:
                    k0 = s * OWN + 1

                    def own(k, i):
                        i.then_inc(S["own"], 1)
                        dve.wait_ge(S["own"], k0 + k)

                    def rows(ap):
                        return ap.unsqueeze(2).broadcast_to([P, TT, E])

                    ranks = rank[:, :].unsqueeze(1).broadcast_to([P, TT, E])
                    dve.wait_ge(S["logits"], s + 1)
                    own(1, dve.tensor_reduce(m1[:, :], C[0][:, 0:TT * E].rearrange("p (t e) -> p t e", e=E), AX.X, ALU.max))
                    dve.tensor_tensor(lg[:, :, :], C[0][:, 0:TT * E].rearrange("p (t e) -> p t e", e=E), rows(m1[:, :]), ALU.subtract)\
                       .then_inc(S["lg_ready"], 1)
                    dve.wait_ge(S["exp_ready"], s + 1)
                    own(2, dve.tensor_reduce(m1[:, :], lg[:, :, :], AX.X, ALU.max))
                    own(3, dve.tensor_tensor(eq[:, :, :], lg[:, :, :], rows(m1[:, :]), ALU.is_equal))
                    own(4, dve.tensor_tensor(eq[:, :, :], eq[:, :, :], ranks, ALU.mult))
                    own(5, dve.tensor_reduce(m1[:, :], eq[:, :, :], AX.X, ALU.max))
                    own(6, dve.tensor_tensor(oh[:, :, :], eq[:, :, :], rows(m1[:, :]), ALU.is_equal))
                    own(7, dve.scalar_tensor_tensor(out=eq[:, :, :], in0=oh[:, :, :], scalar=-2.0, in1=lg[:, :, :],
                                                    op0=ALU.mult, op1=ALU.add))
                    own(8, dve.tensor_reduce(m1[:, :], eq[:, :, :], AX.X, ALU.max))
                    own(9, dve.tensor_tensor(eq[:, :, :], eq[:, :, :], rows(m1[:, :]), ALU.is_equal))
                    own(10, dve.tensor_tensor(eq[:, :, :], eq[:, :, :], ranks, ALU.mult))
                    own(11, dve.tensor_reduce(m1[:, :], eq[:, :, :], AX.X, ALU.max))
                    own(12, dve.tensor_tensor(oh2[:, :, :], eq[:, :, :], rows(m1[:, :]), ALU.is_equal))
                    own(13, dve.tensor_tensor(oh2[:, :, :], oh2[:, :, :], oh[:, :, :], ALU.add))
                    own(14, dve.tensor_tensor(oh2[:, :, :], oh2[:, :, :], lg[:, :, :], ALU.mult))
                    own(15, dve.tensor_reduce(m1[:, :], oh2[:, :, :], AX.X, ALU.add))
                    own(16, dve.reciprocal(m1[:, :], m1[:, :]))
                    dve.tensor_tensor(oh[:, :, :], oh2[:, :, :], rows(m1[:, :]), ALU.mult).then_inc(S["cm_hi"], 1)
                    dve.wait_ge(S["cm_ready"], s + 1)
                    own(17, dve.tensor_tensor(cm[:, :, 1, :].bitcast(F32R), oh[:, :, :], cm[:, :, 0, :], ALU.subtract))
                    dve.sem_inc(S["raw_used"], 1)
                    for t in range(MT):
                        dve.wait_ge(S["act_ready"], s * MT + t + 1)
                        i = dve.scalar_tensor_tensor(out=g[:, t % 2, :], in0=U[t % 2][:, :], scalar=bias[:, t, 1:2],
                                                     in1=g[:, t % 2, :], op0=ALU.add, op1=ALU.mult)
                        if t < ME:
                            i.then_inc(S["prod"], 1)
                            dve.wait_ge(S["prod"], s * ME + t + 1)
                            i = dve.tensor_tensor(g[:, t % 2, :], g[:, t % 2, :], C[t % 2][:, :], ALU.mult)
                        i.then_inc(S["comb_read"], 1)
                    for i in range(2):
                        dve.wait_ge(S["down_done"], (s + 1) * MT + CREDIT)
                        dve.tensor_tensor(y[:, i, :].rearrange("p (t d) -> p t d", t=2), Y[i][:, :].rearrange("p (t d) -> p t d", t=2),
                                          db[:, :].unsqueeze(1).broadcast_to([P, 2, D]), ALU.add).then_inc(S["y_ready"], 1)
                    for i in range(2):
                        dve.wait_ge(S["y_act"], 2 * s + i + 1)
                        yy = y[:, i, :].rearrange("p (t d) -> p t d", t=2)
                        own(18 + i, dve.tensor_tensor(yy, yy, s1[:, bass.ds(s * TT + 2 * i, 2), :], ALU.mult))
                        part = x1[:, bass.ds(s * TT + 2 * i, 2), :]
                        dve.tensor_tensor(part, part, yy, ALU.add).then_inc(S["merged"], 1)

            @block.tensor
            def _(pe):
                pe.wait_ge(S["const_in"], 112)
                pe.wait_ge(S["w_lo"], 3)
                pe.wait_ge(S["own"], 1)
                pe.wait_ge(S["w_hi"], 5)
                pe.sem_inc(S["down_done"], CREDIT)
                with pe.Fori(0, NSTEP) as s:
                    pe.wait_ge(S["x_in"], 32 * (s + 1))
                    pe.wait_ge(S["comb_read"], s * MT + CREDIT)
                    for t in range(TT):
                        for c in range(KC):
                            m = product(pe, C[0][:, t * E:(t + 1) * E], [xs[:, i, c, t * P:(t + 1) * P] for i in range(2)],
                                        [rw[:, i, c, :] for i in range(2)], c == 0, c == KC - 1)
                    m.then_inc(S["logits"], 1)

                    def up(t):
                        pe.wait_ge(S["comb_read"], s * MT + t - 1 + CREDIT)
                        for i, bank in ((0, G[t % 2]), (1, U[t % 2])):
                            for c in range(KC):
                                a_ = c * (MT * P) + t * P
                                m = product(pe, bank[:, :], [w[i][:, q, a_:a_ + P] for q in range(2)],
                                            [xs[:, q, c, :] for q in range(2)], c == 0, c == KC - 1)
                        return m

                    def combine(t):
                        return pe.matmul(C[t % 2][:, :], sel[:, t * P:(t + 1) * P], ct[:, :], start=True, stop=True)

                    def down(t):
                        pe.wait_ge(S["hid_lo"], s * MT + t + 1 + CREDIT)
                        if t == 0:
                            pe.wait_ge(S["y_ready"], 2 * s + CREDIT)
                        for tt in range(TT):
                            o = Y[tt // 2][:, (tt % 2) * D:(tt % 2 + 1) * D]
                            hh, hl = (hid[:, t % 2, q, tt * P:(tt + 1) * P] for q in range(2))
                            wh, wl = (w[2][:, q, t * D:(t + 1) * D] for q in range(2))
                            pe.matmul(o, hh, wh, start=(t == 0 and tt % 2 == 0), stop=False, skip_group_check=True)
                            pe.matmul(o, hh, wl, start=False, stop=False, skip_group_check=True)
                            m = pe.matmul(o, hl, wh, start=False, stop=(t == MT - 1), skip_group_check=True)
                        m.then_inc(S["down_done"], 1)

                    up(0)
                    pe.wait_ge(S["raw_used"], s + 2)
                    for t in range(TT):
                        m = pe.transpose(C[1][0:2 * E, t * P:(t + 1) * P], cm[:, t, :, :].rearrange("p s e -> p (s e)"), ident[:, :])
                    m.then_inc(S["ct_turned"], 1)
                    pe.wait_ge(S["ct_ready"], s + 1)
                    combine(0).then_inc(S["up_full"], 1)
                    for t in range(1, MT):
                        m = up(t)
                        if t == MT - 1:
                            m.then_inc(S["x_used"], 1)
                            pe.wait_ge(S["x_used"], s + 1)
                            pe.sem_inc(S["up_full"], 1)
                        else:
                            (combine(t) if t < ME else m).then_inc(S["up_full"], 1)
                        down(t - 1)
                    down(MT - 1)


def program(nc, a, out):
    xn0 = nc.dram_tensor("xn0_scratch", [NSTEP, P, 2, KC, STEP], F32, kind="Internal").ap()
    xn1 = nc.dram_tensor("xn1_scratch", [BATCH, P, 2, KC, SEQ], F32, kind="Internal").ap()
    stage_norm0(nc, a["x"], a["ident"], xn0)
    with nc.sbuf_tensor("x1", [P, NT, D], F32) as x1:
        stage_attention0(nc, a["w0"], a["rope"], a["ident"], xn0, x1)
        stage_ffn0(nc, a["x"], a["wg"], a["wu"], a["wd"], a["scale"], a["scale_rest"], a["sd"], xn0, x1)
        with nc.sbuf_tensor("s1", [P, NT, D], F32) as s1:
            stage_attention1(nc, a["w_qkv"], a["w_proj"], a["norm_w"], a["b_proj"], a["ident"], xn1, x1, s1)
            stage_moe(nc, a, xn1, x1, s1, out)


def rope_tables():
    import numpy as np
    freq = (np.float32(1.0) / np.float32(10000.0) ** (np.arange(0, DR, 2, dtype=np.float32) / np.float32(DR))).astype(np.float32)
    angle = (np.arange(SEQ, dtype=np.float32)[None, :] * freq[:, None]).astype(np.float32)
    cos, sin = (np.tile(f(angle.astype(np.float64)), (HG, 2)) for f in (np.cos, np.sin))
    more = math.sqrt(DN / DR)
    return np.ascontiguousarray(np.stack([cos * more, sin * more, cos, sin], axis=1).astype(np.float32))


def group_weights(wq, wk, wv, wo):
    import numpy as np
    groups = []
    for g in range(NG):
        cols = []
        for w in (wq, wk, wv):
            rows = w[g * HG * DN:(g + 1) * HG * DN]
            cols.append(rows.T.reshape(KC, P, HG * DN).transpose(1, 0, 2).reshape(P, -1))
        for w in (wq, wk):
            rows = w[H * DN + g * HG * DR:H * DN + (g + 1) * HG * DR].reshape(HG, 2, HALF, D)
            rows = rows.transpose(1, 0, 2, 3).reshape(2 * HG * HALF, D)
            cols.append(rows.T.reshape(KC, P, 2 * P).transpose(1, 0, 2).reshape(P, -1))
        cols.append(wo[:, g * HG * DV:(g + 1) * HG * DV].T.reshape(HG, DV, D).transpose(1, 0, 2).reshape(P, -1))
        groups.append(np.concatenate(cols, axis=1))
    return np.ascontiguousarray(np.stack(groups))


def kernel(**inputs):
    import numpy as _np
    import concourse.bacc as _bacc
    from concourse import mybir as _mybir
    from concourse.bass_utils import run_bass_kernel_spmd as _run

    i = {k: _np.asarray(v) for k, v in inputs.items()}
    scales = _np.stack([i["L0_ffn_s_gate"], i["L0_ffn_s_up"]], axis=1)
    shared = _np.stack([i["L1_ffn_s_gate_b"], i["L1_ffn_s_up_b"]], axis=1)
    data = {
        "x": i["L0_attn_hidden_states"].reshape(NTOK, D),
        "ident": _np.eye(P, dtype=_np.float32),
        "rope": rope_tables(),
        "w0": group_weights(i["L0_attn_Wq"], i["L0_attn_Wk"], i["L0_attn_Wv"], i["L0_attn_Wo"]),
        "wg": i["L0_ffn_wq_gate"].T, "wu": i["L0_ffn_wq_up"].T, "wd": i["L0_ffn_wq_down"].T,
        "scale": scales[0:(HT - 1) * P].reshape(HT - 1, P, 2).transpose(1, 0, 2), "scale_rest": scales[(HT - 1) * P:],
        "sd": i["L0_ffn_s_down"],
        "w_qkv": i["L1_attn_w_qkv"].T, "w_proj": i["L1_attn_w_proj"].T,
        "norm_w": _np.concatenate([_np.tile(i["L1_attn_q_norm_w"], H1), _np.tile(i["L1_attn_k_norm_w"], H1)])[None],
        "b_proj": i["L1_attn_b_proj"][None],
        "router": i["L1_ffn_router_w"].T,
        "gate": i["L1_ffn_gate_w"].transpose(1, 0, 2).reshape(D, E * I1),
        "up": i["L1_ffn_up_w"].transpose(1, 0, 2).reshape(D, E * I1),
        "down": i["L1_ffn_down_w"].reshape(E * I1, D),
        "s_gate": i["L1_ffn_s_gate_w"], "s_up": i["L1_ffn_s_up_w"], "s_down": i["L1_ffn_s_down_w"],
        "bias": shared[0:2 * P].reshape(2, P, 2).transpose(1, 0, 2), "bias_rest": shared[2 * P:],
        "down_b": i["L1_ffn_s_down_b"][None],
        "rank": (E - _np.arange(E, dtype=_np.float32))[None],
        "select": _np.tile(_np.repeat(_np.eye(E, dtype=_np.float32), I1, axis=1), (2, 1)),
    }
    nc = _bacc.Bacc("TRN2", target_bir_lowering=False, num_devices=1)
    arrays, args = {}, {}
    for name, value in data.items():
        arrays["in_" + name] = _np.ascontiguousarray(value)
        args[name] = nc.dram_tensor("in_" + name, value.shape, _mybir.dt.from_np(value.dtype), kind="ExternalInput").ap()
    out = nc.dram_tensor("out_x", (NSTEP, STEP, D), F32, kind="ExternalOutput").ap()
    program(nc, args, out)
    r = _run(nc, [arrays], core_ids=[0])
    return r.results[0]["out_x"].reshape(BATCH, SEQ, D)
```

```python
from contextlib import ExitStack
import math

import concourse.bass as bass
from concourse import mybir

F32 = mybir.dt.float32
F32R = mybir.dt.float32r
I32 = mybir.dt.int32
ALU = mybir.AluOpType
ACT = mybir.ActivationFunctionType
AX = mybir.AxisListType

P = 128
D = 256
KC = D // P
NTOK, SEQ, BATCH = 2048, 256, 8
NT = NTOK // P
STEP = 512
NSTEP = NTOK // STEP
TT = STEP // P
H, DN, DR, DV = 16, 128, 64, 128
HG = 4
NG = H // HG
HALF = DR // 2
HID = 704
HT = 6
HREST = HID - (HT - 1) * P
H1, D1 = 16, 16
E, I1 = 8, 176
SI = 2 * I1
MW = E * I1 + SI
MT = 14
ME = E * I1 // P
MREST = MW - (MT - 1) * P
LN_EPS, RMS_EPS = 1e-5, 1e-6
SCALE0 = 1.0 / math.sqrt(DN)
SCALE1 = D1 ** -0.5
CREDIT = 2

W_Q, W_K, W_V, W_R, W_O, W_END = 0, 1024, 2048, 3072, 4096, 5120


def product(pe, out, lhs, rhs, first, last):
    (lh, ll), (rh, rl) = lhs, rhs
    pe.matmul(out, lh, rh, start=first, stop=False)
    pe.matmul(out, lh, rl, start=False, stop=False)
    return pe.matmul(out, ll, rh, start=False, stop=last)


class Names:

    def __init__(self, nc, ctx, prefix):
        self.nc, self.ctx, self.prefix = nc, ctx, prefix

    def sb(self, name, shape, dt=F32):
        return self.ctx.enter_context(self.nc.sbuf_tensor(self.prefix + name, shape, dt))

    def ps(self, name, shape=(P, 512)):
        return self.ctx.enter_context(self.nc.psum_tensor(self.prefix + name, list(shape), F32))

    def sem(self, name):
        return self.ctx.enter_context(self.nc.semaphore(self.prefix + name))


def norm_stats(dve, own, seen, k, xt, stats, mv, var_eps, tiles, eps):
    for t in range(tiles):
        dve.bn_stats(stats[:, t, :], xt[:, t, :]).then_inc(own, 1)
    dve.wait_ge(own, k + tiles)
    dve.sem_inc(seen, 1)
    for t in range(tiles):
        dve.bn_aggr(mv[:, t, :], stats[:, t, :]).then_inc(own, 1)
    dve.wait_ge(own, k + 2 * tiles)
    dve.tensor_scalar(var_eps, mv[:, 0:tiles, 1], eps, None, ALU.add).then_inc(own, 1)
    return k + 2 * tiles + 1


def polish_rsqrt(dve, own, k, r, v, tmp):
    dve.tensor_tensor(tmp, r, r, ALU.mult).then_inc(own, 1)
    dve.wait_ge(own, k + 1)
    dve.tensor_tensor(tmp, tmp, v, ALU.mult).then_inc(own, 1)
    dve.wait_ge(own, k + 2)
    dve.tensor_scalar(tmp, tmp, -0.5, 1.5, ALU.mult, ALU.add).then_inc(own, 1)
    dve.wait_ge(own, k + 3)
    dve.tensor_tensor(r, r, tmp, ALU.mult).then_inc(own, 1)
    dve.wait_ge(own, k + 4)
    return k + 4


class Shared0:

    def __init__(self, nc, ctx):
        n = Names(nc, ctx, "s0_")
        self.ident = n.sb("ident", [P, P])
        self.tab = n.sb("tab", [P, 4, STEP])
        self.raw = n.sb("raw", [P, W_END])
        self.wh, self.wl = n.sb("wh", [P, W_END], F32R), n.sb("wl", [P, W_END], F32R)


def stage_norm0(nc, x, ident_in, weights, tables, shared, xn_dram):
    with ExitStack() as ctx:
        n = Names(nc, ctx, "n0_")
        xt = n.sb("x", [P, NT, D])
        xn = n.sb("xn", [P, 2, TT, D])
        ident = shared.ident
        stats = n.sb("stats", [P, NT, 6])
        mv = n.sb("mv", [P, NT, 2])
        ve = n.sb("ve", [P, NSTEP, TT])
        rs = n.sb("rs", [P, NSTEP, TT])
        tmp = n.sb("tmp", [P, TT])
        mhalf = n.sb("mhalf", [P, TT])
        xs = n.sb("xs", [P, 2, 2, KC, STEP], F32R)
        bank = [n.ps(f"bank{i}") for i in range(2)]
        x_in = [n.sem(f"x_in{s}") for s in range(NSTEP)]
        id_in, own, stats_seen, ve_ready, rs_ready, mhalf_ready = (n.sem(s) for s in ("id_in", "own", "stats_seen", "ve_ready", "rs_ready", "mhalf_ready"))
        xn_ready, turned, hi_ready, lo_ready = (n.sem(s) for s in ("xn_ready", "turned", "hi_ready", "lo_ready"))
        w_in, w_hi, w_lo, tab_in = (n.sem(s) for s in ("w_in", "w_hi", "w_lo", "tab_in"))
        stored = [n.sem(f"stored{i}") for i in range(2)]
        W_PART = 1024

        with nc.Block() as block:
            @block.sync
            def _(sp):
                for s in range(NSTEP):
                    sp.dma_start(xt[:, TT * s:TT * (s + 1), :],
                                 x[STEP * s:STEP * (s + 1), :].rearrange("(t p) d -> p t d", p=P)).then_inc(x_in[s], 16)
                    if s == 0:
                        sp.dma_start(ident[:, :], ident_in).then_inc(id_in, 16)
                sp.dma_start(shared.raw[:, :], weights[0]).then_inc(w_in, 16)
                sp.dma_start(shared.tab[:, :, :], tables).then_inc(tab_in, 16)
                for s in range(NSTEP):
                    sp.wait_ge(lo_ready, 2 * s + 2)
                    sp.dma_start(xn_dram[s], xs[:, s % 2].bitcast(F32)).then_inc(stored[s % 2], 16)
                for i in range(2):
                    sp.wait_ge(stored[i], 16 * NSTEP // 2)
                sp.wait_ge(tab_in, 16)

            @block.gpsimd
            def _(pool):
                pool.memset(mhalf[:, :], -0.5).then_inc(mhalf_ready, 1)
                pool.wait_ge(mhalf_ready, 1)
                for s in range(NSTEP):
                    pool.wait_ge(ve_ready, s + 1)
                    pool.tensor_tensor(rs[:, s, :], ve[:, s, :], mhalf[:, :], ALU.pow).then_inc(rs_ready, 1)
                for a in range(0, W_END, W_PART):
                    pool.wait_ge(w_hi, a // W_PART + 1)
                    pool.tensor_tensor(shared.wl[:, a:a + W_PART], shared.raw[:, a:a + W_PART], shared.wh[:, a:a + W_PART],
                                       ALU.subtract).then_inc(w_lo, 1)

            @block.vector
            def _(dve):
                def variances(s, k):
                    tiles = slice(TT * s, TT * (s + 1))
                    dve.wait_ge(x_in[s], 16)
                    k = norm_stats(dve, own, stats_seen, k, xt[:, tiles, :], stats[:, tiles], mv[:, tiles], ve[:, s, :], TT, LN_EPS)
                    dve.wait_ge(own, k)
                    dve.sem_inc(ve_ready, 1)
                    return k

                def low_parts(s):
                    for c in range(KC):
                        dve.wait_ge(hi_ready, 2 * s + c + 1)
                        dve.tensor_tensor(xs[:, s % 2, 1, c, :], bank[c][:, :], xs[:, s % 2, 0, c, :], ALU.subtract)\
                           .then_inc(lo_ready, 1)

                k = variances(0, 0)
                for s in range(NSTEP):
                    if s + 1 < NSTEP:
                        k = variances(s + 1, k)
                    dve.wait_ge(rs_ready, s + 1)
                    k = polish_rsqrt(dve, own, k, rs[:, s, :], ve[:, s, :], tmp[:, :])
                    if s >= 2:
                        dve.wait_ge(turned, 2 * (s - 1))
                    for t in range(TT):
                        i = dve.tensor_scalar(xn[:, s % 2, t, :], xt[:, TT * s + t, :], mv[:, TT * s + t, 0:1],
                                              rs[:, s, t:t + 1], ALU.subtract, ALU.mult)
                    i.then_inc(xn_ready, 1)
                    if s >= 1:
                        low_parts(s - 1)
                low_parts(NSTEP - 1)

            @block.tensor
            def _(pe):
                pe.wait_ge(id_in, 16)
                for s in range(NSTEP):
                    pe.wait_ge(xn_ready, s + 1)
                    for c in range(KC):
                        if s >= 1:
                            pe.wait_ge(lo_ready, 2 * (s - 1) + c + 1)
                        for t in range(TT):
                            i = pe.transpose(bank[c][:, t * P:(t + 1) * P], xn[:, s % 2, t, c * P:(c + 1) * P], ident[:, :])
                        i.then_inc(turned, 1)

            @block.scalar
            def _(act):
                for s in range(NSTEP):
                    if s >= 2:
                        act.wait_ge(stored[s % 2], 16 * (s // 2))
                    for c in range(KC):
                        act.wait_ge(turned, 2 * s + c + 1)
                        act.activation(xs[:, s % 2, 0, c, :], bank[c][:, :], ACT.Copy).then_inc(hi_ready, 1)
                    if s == 1:
                        act.wait_ge(w_in, 16)
                    for a in ([], [0, 1], [2, 3], [4])[s]:
                        cols = slice(a * W_PART, (a + 1) * W_PART)
                        act.activation(shared.wh[:, cols], shared.raw[:, cols], ACT.Copy).then_inc(w_hi, 1)


def stage_attention0(nc, weights, shared, xn_dram, sacc):
    UN = 2 * HG
    UNIT_JOBS = [[], ["k1"], ["q2"], ["k2", "rope0"], ["q3", "rope1"], ["k3", "rope2"], ["q0+", "rope3"], []]
    JOB = {name: i for i, name in enumerate(sum(UNIT_JOBS, []))}
    JN, JV, JO, JS, JP = 10, 12, 16, 18, 12
    HI, HP = 12, 7
    SPLIT = {name: i for i, name in enumerate(x for x in JOB if not x.startswith("rope"))}
    SN, SV = 6, 8
    FINAL = {name: i for i, name in enumerate(["k1", "q2", "k2", "q3", "k3", "out"])}

    def unit_jobs(u, final):
        return [name for name in UNIT_JOBS[u] if not final or name in FINAL]

    def job_no(name, final):
        return (FINAL if final else JOB)[name]

    def out_no(final):
        return FINAL["out"] if final else JO

    def qk_done(h, final):
        return job_no(f"k{h}", final) + 1 if h else -2

    W_ORDER = [3, 2, 0, 1, 4]
    with ExitStack() as ctx:
        n = Names(nc, ctx, "a0_")
        ident, tab, raw, wh, wl = shared.ident, shared.tab, shared.raw, shared.wh, shared.wl
        xs = n.sb("xs", [P, 2, KC, STEP], F32R)
        xr = n.sb("xr", [P, 2, KC, STEP], F32R)
        rot = [n.sb("rotq", [P, 4, STEP]), n.sb("rotk", [P, 4, STEP])]
        sq = n.sb("sq", [P, HG, STEP], F32R)
        sk = n.sb("sk", [P, 2, HG, STEP], F32R)
        qn = n.sb("qn", [P, 2, 2, STEP], F32R)
        kn = n.sb("kn", [P, 2, 2, STEP], F32R)
        v = n.sb("v", [P, 2, TT, HG * DV], F32R)
        pr = n.sb("pr", [P, 2, 2, SEQ])
        pt = n.sb("pt", [P, 2, 2, 512], F32R)
        ot = n.sb("ot", [P, 2, HG, STEP], F32R)
        mx = n.sb("mx", [P, 2, 2])
        nb = n.sb("nb", [P, 2, 2])
        sm = n.sb("sm", [P, 2, 2])
        ri = n.sb("ri", [P, 2, 2])
        PJ = [n.ps(f"job{i}") for i in range(2)]
        PS = [n.ps(f"score{i}") for i in range(2)]
        PT = [n.ps(f"turn{i}") for i in range(2)]
        PO = [n.ps(f"out{i}") for i in range(2)]
        QSTACKS, KSTACKS = 16 * 4 * HG, 16 * 6
        kstack_in = [n.sem(f"kstack_in{j}") for j in range(HG)]
        S = {s: n.sem(s) for s in (
            "w_in", "w_hi", "w_lo_d", "w_lo_p", "x_in", "xr_in", "qstack_in", "job_full", "job_free", "job_hi", "rot_mul",
            "rot_add", "rot_hi", "rot_lo", "score_full", "score_free", "max_raw", "max_ready", "exp_ready",
            "sum_inv", "norm_ready", "turn_full", "turn_free", "turn_hi", "pv_done", "out_hi", "out_free", "zeroed", "wl_p")}

        def w(part, a, b):
            return (wh, wl)[part][:, a:b]

        def w2(a, b):
            return w(0, a, b), w(1, a, b)

        def x2(x, c, a, b):
            return x[:, 0, c, a:b], x[:, 1, c, a:b]

        with nc.Block() as block:
            @block.sync
            def _(sp):
                def load_x(x, b, loaded):
                    sp.dma_start(x[:, :, :, :].bitcast(F32).rearrange("p s c n -> p (s c n)"),
                                 xn_dram[bass.ds(b, 1)].rearrange("o p s c n -> p (o s c n)")).then_inc(S[loaded], 16)

                def load_weights(g):
                    sp.dma_start(raw[:, :], weights[bass.ds(g, 1)].rearrange("o p n -> p (o n)")).then_inc(S["w_in"], 16)

                def stack_q(st, before):
                    sp.wait_ge(S["rot_lo"], st * 2 + 1)
                    for j in range(HG):
                        if before is not None:
                            sp.wait_ge(S["score_full"], before * UN + 2 * j + 2)
                        for part in range(2):
                            for r in range(2):
                                at = HALF * (2 * part + r)
                                sp.dma_start(sq[at:at + HALF, j, :].bitcast(F32),
                                             rot[0][HALF * j:HALF * (j + 1), 2 * (1 - part) + r, :]).then_inc(S["qstack_in"], 16)

                def stack_k(st):
                    sp.wait_ge(S["rot_lo"], st * 2 + 2)
                    for j in range(HG):
                        for part, copies in ((0, 2), (1, 1)):
                            for r in range(2):
                                for copy in range(copies):
                                    at = HALF * (2 * copy + r)
                                    sp.dma_start(sk[at:at + HALF, part, j, :].bitcast(F32),
                                                 rot[1][HALF * j:HALF * (j + 1), 2 * (1 - part) + r, :]).then_inc(kstack_in[j], 16)

                def step(g, b, next_b):
                    st = g * NSTEP + b
                    job0 = JP + st * JS
                    sp.wait_ge(S["job_full"], job0 + JOB["k3"] + 1)
                    load_x(xs, next_b, "x_in")
                    stack_q(st + 1, st)
                    sp.wait_ge(S["job_full"], job0 + JN + 2)
                    load_x(xr, (b + 2) % NSTEP, "xr_in")
                    stack_k(st + 1)

                load_x(xr, 0, "xr_in")
                load_x(xs, 0, "x_in")
                sp.wait_ge(S["job_full"], 8)
                load_x(xr, 1, "xr_in")
                stack_q(0, None)
                stack_k(0)
                with sp.Fori(0, NG - 1) as g:
                    sp.wait_ge(S["w_lo_d"], (g + 1) * 3)
                    load_weights(g + 1)
                    with sp.Fori(0, NSTEP - 1) as b:
                        step(g, b, b + 1)
                    step(g, NSTEP - 1, 0)
                with sp.Fori(0, NSTEP - 1) as b:
                    step(NG - 1, b, b + 1)
                sp.wait_ge(S["xr_in"], 16 * (NG * NSTEP + 1))

            @block.gpsimd
            def _(pool):
                def split_weights(g, i):
                    pool.wait_ge(S["w_hi"], 5 * g + W_ORDER.index(i) + 1)
                    pool.tensor_tensor(w(1, 1024 * i, 1024 * i + 1024), raw[:, 1024 * i:1024 * i + 1024],
                                       w(0, 1024 * i, 1024 * i + 1024), ALU.subtract).then_inc(S["w_lo_p"], 1)

                def rotate(st, q):
                    r = rot[q]
                    pool.wait_ge(S["rot_mul"], st * 2 + q + 1)
                    pool.tensor_tensor(r[:, 0, :], r[:, 0, :], r[:, 2, :], ALU.subtract).then_inc(S["rot_add"], 1)
                    pool.tensor_tensor(r[:, 1, :], r[:, 1, :], r[:, 3, :], ALU.add).then_inc(S["rot_add"], 1)
                    pool.wait_ge(S["rot_hi"], st * 2 + q + 1)
                    pool.tensor_tensor(r[:, 0:2, :].bitcast(F32R), r[:, 0:2, :], r[:, 2:4, :],
                                       ALU.subtract).then_inc(S["rot_lo"], 1)

                pool.sem_inc(S["w_lo_p"], 2)
                rotate(0, 0)
                rotate(0, 1)
                def steps(g):
                    with pool.Fori(0, NSTEP - 1) as b:
                        rotate(g * NSTEP + b + 1, 0)
                        rotate(g * NSTEP + b + 1, 1)

                with pool.Fori(0, NG - 1) as g:
                    steps(g)
                    split_weights(g + 1, 3)
                    rotate((g + 1) * NSTEP, 0)
                    split_weights(g + 1, 1)
                    rotate((g + 1) * NSTEP, 1)
                steps(NG - 1)

            @block.scalar
            def _(act):
                def split_weights(i):
                    act.activation(w(0, 1024 * i, 1024 * i + 1024), raw[:, 1024 * i:1024 * i + 1024], ACT.Copy)\
                       .then_inc(S["w_hi"], 1)

                def job_hi(count, out):
                    act.wait_ge(S["job_full"], count[0] + count[1] + 1)
                    act.activation(out, PJ[count[1] % 2][:, :], ACT.Copy).then_inc(S["job_hi"], 1)

                def rot_hi(st, q):
                    act.wait_ge(S["rot_add"], st * 4 + 2 * q + 2)
                    act.activation(rot[q][:, 2:4, :].bitcast(F32R), rot[q][:, 0:2, :], ACT.Copy).then_inc(S["rot_hi"], 1)

                def step(g, b, last, final=False):
                    st = g * NSTEP + b
                    job0 = JP + st * JS

                    def out_hi(h):
                        act.wait_ge(S["pv_done"], st * UN + 2 * h + 2 + CREDIT)
                        act.activation(ot[:, 0, h, :], PO[h % 2][:, :], ACT.Copy).then_inc(S["out_hi"], 1)

                    def turn_hi(u):
                        act.wait_ge(S["turn_full"], st * UN + u + 1 + CREDIT)
                        act.wait_ge(S["pv_done"], st * UN + u - 1 + CREDIT)
                        act.activation(pt[:, u % 2, 0, :], PT[u % 2][:, :], ACT.Copy).then_inc(S["turn_hi"], 1)

                    for u in range(UN):
                        for name in unit_jobs(u, final):
                            if name in SPLIT:
                                job_hi((job0, job_no(name, final)), (qn if name[0] == "q" else kn)[:, int(name[1]) % 2, 0, :])
                        act.wait_ge(S["max_ready"], st * UN + u + 1)
                        act.wait_ge(S["turn_full"], st * UN + u - 1 + CREDIT)
                        for t in range(2):
                            i = act.activation(pr[:, u % 2, t, :], PS[u % 2][:, t * SEQ:(t + 1) * SEQ], ACT.Exp,
                                               bias=nb[:, u % 2, t:t + 1], scale=SCALE0,
                                               accum_out=sm[:, u % 2, t:t + 1])
                        i.then_inc(S["exp_ready"], 1)
                        if u >= 1:
                            turn_hi(u - 1)
                        if u >= 3 and u % 2 == 1:
                            out_hi((u - 3) // 2)
                        if u in (5, 7) and not final:
                            rot_hi(st + 1, (u - 5) // 2)
                        if last and u == 0:
                            act.wait_ge(S["w_in"], 16 * (g + 1))
                        if last and u < 2:
                            split_weights(W_ORDER[u])
                        if last and u == 5:
                            act.wait_ge(S["job_full"], job0 + JOB["k3"] + 1)
                            split_weights(W_ORDER[2])
                            split_weights(W_ORDER[3])
                    if not final:
                        job_hi((job0, JN), kn[:, 0, 0, :])
                        job_hi((job0, JN + 1), qn[:, 1, 0, :])
                    turn_hi(UN - 1)
                    for i in range(TT):
                        if i == 2:
                            out_hi(HG - 1)
                        if not final:
                            job_hi((job0, JV + i), v[:, 0, i, :])
                    if last:
                        act.wait_ge(S["job_full"], job0 + JO + 2)
                        split_weights(4)

                act.sem_inc(S["w_hi"], 5)
                rot_hi(0, 0)
                for i, buf in enumerate([qn[:, 0, 0, :], kn[:, 0, 0, :], qn[:, 1, 0, :]] + [v[:, 0, i, :] for i in range(TT)]):
                    job_hi((0, 5 + i), buf)
                    if i == 1:
                        rot_hi(0, 1)
                with act.Fori(0, NG - 1) as g:
                    with act.Fori(0, NSTEP - 1) as b:
                        step(g, b, False)
                    step(g, NSTEP - 1, True)
                with act.Fori(0, NSTEP - 1) as b:
                    step(NG - 1, b, False)
                step(NG - 1, NSTEP - 1, False, final=True)

            @block.vector
            def _(dve):
                dve.sem_inc(S["w_lo_d"], 3)
                dve.memset(sk[DR:P, 1, :, :].bitcast(F32), 0.0)
                dve.memset(sacc[:, :, :], 0.0).then_inc(S["zeroed"], 1)
                dve.wait_ge(S["zeroed"], 1)
                dve.sem_inc(S["job_free"], CREDIT + 1)
                dve.sem_inc(S["turn_free"], CREDIT)
                dve.sem_inc(S["out_free"], CREDIT)
                def split_weights(g, i):
                    dve.wait_ge(S["w_hi"], 5 * g + W_ORDER.index(i) + 1)
                    dve.tensor_tensor(w(1, 1024 * i, 1024 * i + 1024), raw[:, 1024 * i:1024 * i + 1024],
                                      w(0, 1024 * i, 1024 * i + 1024), ALU.subtract).then_inc(S["w_lo_d"], 1)

                def job_lo(count, j, hi, lo):
                    dve.wait_ge(S["job_hi"], count)
                    dve.tensor_tensor(lo, PJ[j % 2][:, :], hi, ALU.subtract).then_inc(S["job_free"], 1)

                def rope_half(st, job0, j, q, half):
                    if q == 0 and half == 0:
                        dve.wait_ge(S["qstack_in"], st * QSTACKS)
                    if q == 1 and half == 0:
                        for h in range(HG):
                            dve.wait_ge(kstack_in[h], st * KSTACKS)
                    dve.wait_ge(S["job_full"], job0 + j + 1)
                    for s_ in range(2):
                        slot = 2 * half + s_
                        i = dve.tensor_tensor(rot[q][:, slot, :], PJ[j % 2][:, :],
                                              tab[:, 2 * q + (s_ if half == 0 else 1 - s_), :], ALU.mult)
                    i.then_inc(S["job_free"], 1)
                    if half == 1:
                        dve.wait_ge(S["job_free"], job0 + j + 1 + CREDIT)
                        dve.sem_inc(S["rot_mul"], 1)

                def step(g, b, last, final=False):
                    st = g * NSTEP + b
                    job0, hi0 = JP + st * JS, HP + st * HI

                    def normalise(u):
                        dve.wait_ge(S["exp_ready"], st * UN + u + 1 + CREDIT)
                        dve.reciprocal(ri[:, u % 2, :], sm[:, u % 2, :]).then_inc(S["sum_inv"], 1)
                        dve.wait_ge(S["sum_inv"], st * UN + u + 1)
                        for t in range(2):
                            i = dve.tensor_scalar(pr[:, u % 2, t, :], pr[:, u % 2, t, :], ri[:, u % 2, t:t + 1],
                                                  None, ALU.mult)
                        i.then_inc(S["norm_ready"], 1)

                    def turn_lo(u):
                        dve.wait_ge(S["turn_hi"], st * UN + u + 1)
                        dve.tensor_tensor(pt[:, u % 2, 1, :], PT[u % 2][:, :], pt[:, u % 2, 0, :], ALU.subtract)\
                           .then_inc(S["turn_free"], 1)

                    def out_lo(h):
                        dve.wait_ge(S["out_hi"], st * HG + h + 1)
                        dve.tensor_tensor(ot[:, 1, h, :], PO[h % 2][:, :], ot[:, 0, h, :], ALU.subtract)\
                           .then_inc(S["out_free"], 1)

                    for u in range(UN):
                        h = u // 2
                        if u >= 1:
                            normalise(u - 1)
                        for name in unit_jobs(u, final):
                            if name in SPLIT:
                                buf = (qn if name[0] == "q" else kn)[:, int(name[1]) % 2]
                                job_lo(hi0 + SPLIT[name] + 1, job_no(name, final), buf[:, 0, :], buf[:, 1, :])
                        dve.wait_ge(S["score_full"], st * UN + u + 1)
                        dve.tensor_reduce(mx[:, u % 2, :], PS[u % 2][:, :].rearrange("p (t k) -> p t k", t=2),
                                          AX.X, ALU.max).then_inc(S["max_raw"], 1)
                        dve.wait_ge(S["max_raw"], st * UN + u + 1)
                        dve.tensor_scalar(nb[:, u % 2, :], mx[:, u % 2, :], -SCALE0, None, ALU.mult)\
                           .then_inc(S["max_ready"], 1)
                        for name in unit_jobs(u, final):
                            if name not in SPLIT:
                                rope_half(st + 1, job0, JOB[name], int(name[4]) // 2, int(name[4]) % 2)
                        if u >= 1:
                            turn_lo(u - 1)
                        if u >= 3 and u % 2 == 1:
                            out_lo((u - 3) // 2)
                        if last and u in (1, 5):
                            split_weights(g + 1, W_ORDER[1] if u == 1 else W_ORDER[2])
                    normalise(UN - 1)
                    if not final:
                        job_lo(hi0 + SN + 1, JN, kn[:, 0, 0, :], kn[:, 0, 1, :])
                        job_lo(hi0 + SN + 2, JN + 1, qn[:, 1, 0, :], qn[:, 1, 1, :])
                    turn_lo(UN - 1)
                    for i in range(TT):
                        if i == 2:
                            out_lo(HG - 1)
                        if not final:
                            job_lo(hi0 + SV + i + 1, JV + i, v[:, 0, i, :], v[:, 1, i, :])
                    for i in range(2):
                        j = out_no(final) + i
                        dve.wait_ge(S["job_full"], job0 + j + 1)
                        acc = sacc[:, bass.ds(b * TT + 2 * i, 2), :]
                        dve.tensor_tensor(acc, acc, PJ[j % 2][:, :].rearrange("p (t d) -> p t d", t=2), ALU.add)\
                           .then_inc(S["job_free"], 1)
                    if last:
                        split_weights(g + 1, 4)

                for i in range(4):
                    rope_half(0, 0, 1 + i, i // 2, i % 2)
                for i, buf in enumerate([qn[:, 0], kn[:, 0], qn[:, 1]] + [v[:, :, i] for i in range(TT)]):
                    job_lo(i + 1, 5 + i, buf[:, 0, :], buf[:, 1, :])
                with dve.Fori(0, NG - 1) as g:
                    with dve.Fori(0, NSTEP - 1) as b:
                        step(g, b, False)
                    step(g, NSTEP - 1, True)
                with dve.Fori(0, NSTEP - 1) as b:
                    step(NG - 1, b, False)
                step(NG - 1, NSTEP - 1, False, final=True)

            @block.tensor
            def _(pe):
                pe.sem_inc(S["exp_ready"], CREDIT)
                pe.sem_inc(S["turn_full"], CREDIT)
                pe.sem_inc(S["pv_done"], CREDIT)
                def open_job(job0, j):
                    pe.wait_ge(S["job_free"], job0 + j - 1 + CREDIT)
                    return PJ[j % 2]

                def feature_job(x, job0, j, wcol, rows):
                    bank = open_job(job0, j)
                    for c in range(KC):
                        i = product(pe, bank[:, :], w2(wcol + c * rows, wcol + c * rows + P), x2(x, c, 0, STEP),
                                    c == 0, c == KC - 1)
                    i.then_inc(S["job_full"], 1)

                def nope(job0, j, name, x):
                    feature_job(x, job0, j, (W_Q if name[0] == "q" else W_K) + int(name[1]) * DN, HG * DN)

                def rope(job0, j, part):
                    feature_job(xr, job0, j, W_R + 512 * (part // 2) + (part % 2) * P, 2 * P)

                def value_rows(job0, j, i):
                    bank = open_job(job0, j)
                    for c in range(KC):
                        m = product(pe, bank[:, :], x2(xs, c, i * P, (i + 1) * P),
                                    w2(W_V + c * 512, W_V + (c + 1) * 512), c == 0, c == KC - 1)
                    m.then_inc(S["job_full"], 1)

                def step(g, b, last, final=False):
                    st = g * NSTEP + b
                    job0 = JP + st * JS

                    def scores(u):
                        h, bb = u // 2, u % 2
                        pe.wait_ge(S["exp_ready"], st * UN + u - 1 + CREDIT)
                        pe.wait_ge(S["job_free"], job0 + qk_done(h, final) + CREDIT)
                        if bb == 0:
                            pe.wait_ge(kstack_in[h], (st + 1) * KSTACKS)
                        if u == 0:
                            pe.wait_ge(S["qstack_in"], (st + 1) * QSTACKS)
                        for t in range(2):
                            out = PS[u % 2][:, t * SEQ:(t + 1) * SEQ]
                            a, z = bb * SEQ + t * P, bb * SEQ
                            product(pe, out, (qn[:, h % 2, 0, a:a + P], qn[:, h % 2, 1, a:a + P]),
                                    (kn[:, h % 2, 0, z:z + SEQ], kn[:, h % 2, 1, z:z + SEQ]), True, False)
                            pe.matmul(out, sq[:, h, a:a + P], sk[:, 0, h, z:z + SEQ], start=False, stop=False)
                            i = pe.matmul(out, sq[:, h, a:a + P], sk[:, 1, h, z:z + SEQ], start=False, stop=True)
                        i.then_inc(S["score_full"], 1)

                    def turn(u):
                        pe.wait_ge(S["norm_ready"], st * UN + u + 1)
                        pe.wait_ge(S["turn_free"], st * UN + u - 1 + CREDIT)
                        for kc in range(2):
                            for t in range(2):
                                i = pe.transpose(PT[u % 2][:, kc * SEQ + t * P:kc * SEQ + (t + 1) * P],
                                                 pr[:, u % 2, t, kc * P:(kc + 1) * P], ident[:, :])
                        i.then_inc(S["turn_full"], 1)

                    def values(u):
                        h, bb = u // 2, u % 2
                        pe.wait_ge(S["turn_free"], st * UN + u + 1 + CREDIT)
                        if bb == 0:
                            pe.wait_ge(S["out_free"], st * HG + h - 1 + CREDIT)
                        for kc in range(2):
                            vv = [v[:, s_, 2 * bb + kc, h * DV:(h + 1) * DV] for s_ in range(2)]
                            pp = [pt[:, u % 2, s_, kc * SEQ:(kc + 1) * SEQ] for s_ in range(2)]
                            i = product(pe, PO[h % 2][:, bb * SEQ:(bb + 1) * SEQ], vv, pp, kc == 0, kc == 1)
                        i.then_inc(S["pv_done"], 1)

                    for u in range(UN):
                        for name in unit_jobs(u, final):
                            if last and name == "q0+":
                                pe.wait_ge(S["w_lo_d"], 3 * (g + 1) + 2)
                            if name in SPLIT:
                                nope(job0, job_no(name, final), name, xr if name[-1] == "+" else xs)
                        scores(u)
                        for name in unit_jobs(u, final):
                            if name == "rope0":
                                pe.wait_ge(S["xr_in"], 16 * (st + 2))
                                if last:
                                    pe.wait_ge(S["w_lo_p"], 2 * (g + 1) + 1)
                            if name not in SPLIT:
                                rope(job0, JOB[name], int(name[4]))
                        if u >= 2:
                            values(u - 2)
                        if u >= 1:
                            turn(u - 1)
                    if last:
                        pe.wait_ge(S["w_lo_p"], 2 * (g + 1) + 2)
                    if not final:
                        nope(job0, JN, "k0", xr)
                        nope(job0, JN + 1, "q1", xr)
                    values(UN - 2)
                    turn(UN - 1)
                    if not final:
                        pe.wait_ge(S["x_in"], 16 * (st + 2))
                    for i in range(TT):
                        if i == 2:
                            values(UN - 1)
                        if not final:
                            value_rows(job0, JV + i, i)
                    pe.wait_ge(S["w_lo_d"], 3 * (g + 1))
                    pe.wait_ge(S["out_free"], (st + 1) * HG + CREDIT)
                    for i in range(2):
                        bank = open_job(job0, out_no(final) + i)
                        for t in range(2):
                            a = (2 * i + t) * P
                            for h in range(HG):
                                m = product(pe, bank[:, t * D:(t + 1) * D],
                                            (ot[:, 0, h, a:a + P], ot[:, 1, h, a:a + P]),
                                            w2(W_O + h * D, W_O + (h + 1) * D), h == 0, h == HG - 1)
                        m.then_inc(S["job_full"], 1)

                pe.wait_ge(S["xr_in"], 16)
                pe.wait_ge(S["x_in"], 16)
                pe.sem_inc(S["job_full"], 1)
                for part in range(4):
                    rope(0, 1 + part, part)
                for i, name in enumerate(("q0", "k0", "q1")):
                    nope(0, 5 + i, name, xr)
                for i in range(TT):
                    value_rows(0, 8 + i, i)
                with pe.Fori(0, NG - 1) as g:
                    with pe.Fori(0, NSTEP - 1) as b:
                        step(g, b, False)
                    step(g, NSTEP - 1, True)
                with pe.Fori(0, NSTEP - 1) as b:
                    step(NG - 1, b, False)
                step(NG - 1, NSTEP - 1, False, final=True)


def stage_ffn0(nc, x, wg_in, wu_in, wd_in, scale_in, scale_rest_in, sd_in, xn_dram, sacc):
    with ExitStack() as ctx:
        n = Names(nc, ctx, "f0_")
        raw = [n.sb(f"raw{i}", [P, HT * D], I32) for i in range(3)]
        rf = [n.sb(f"rawf{i}", [P, HT * D]) for i in range(3)]
        w = [n.sb(f"w{i}", [P, 2, HT * D], F32R) for i in range(3)]
        scale = n.sb("scale", [P, HT, 2])
        sd = n.sb("sd", [P, D])
        xs = n.sb("xs", [P, 2, 2, KC, STEP], F32R)
        xt = n.sb("x", [P, 2, TT, D])
        act_g = n.sb("act_g", [P, 2, STEP])
        hid = n.sb("hid", [P, 2, 2, STEP], F32R)
        y = n.sb("y", [P, 2, 2 * D])
        G = [n.ps(f"gate{i}") for i in range(2)]
        U = [n.ps(f"up{i}") for i in range(2)]
        Y = [n.ps(f"down{i}") for i in range(2)]
        S = {s: n.sem(s) for s in ("scale_in", "padded", "converted", "w_hi", "w_lo", "gated", "up_full", "act_ready",
                                   "prod", "hid_hi", "hid_lo", "down_done", "y_ready", "y_act", "merged")}
        w_in = [n.sem(f"w_in{i}") for i in range(3)]
        x_in, xt_in = ([n.sem(f"{name}{i}") for i in range(NSTEP)] for name in ("xn_in", "x_in"))

        def part(i, row, t):
            if i == 2:
                return row[:, t * D:(t + 1) * D]
            return row.rearrange("p (c n) -> p c n", c=KC)[:, :, t * P:(t + 1) * P]

        with nc.Block() as block:
            @block.sync
            def _(sp):
                def load_x(s):
                    sp.dma_start(xs[:, s % 2].bitcast(F32), xn_dram[s]).then_inc(x_in[s], 16)

                def load_rest(s):
                    sp.dma_start(xt[:, s % 2], x[STEP * s:STEP * (s + 1), :].rearrange("(t p) d -> p t d", p=P)).then_inc(xt_in[s], 16)

                load_x(0)
                for i, src in ((0, wg_in), (1, wu_in)):
                    dst = raw[i][:, :].rearrange("p (c n) -> p c n", c=KC)
                    sp.dma_start(dst[:, :, 0:HID], src.rearrange("(c p) n -> p c n", p=P)).then_inc(w_in[i], 16)
                dst = raw[2][:, :].rearrange("p (t n) -> p t n", t=HT)
                sp.dma_start(dst[:, 0:HT - 1, :], wd_in[0:(HT - 1) * P, :].rearrange("(t p) n -> p t n", p=P)).then_inc(w_in[2], 16)
                sp.dma_start(dst[0:HREST, HT - 1, :], wd_in[(HT - 1) * P:HID, :]).then_inc(w_in[2], 16)
                sp.dma_start(scale[:, 0:HT - 1, :], scale_in).then_inc(S["scale_in"], 16)
                sp.dma_start(scale[0:HREST, HT - 1, :], scale_rest_in).then_inc(S["scale_in"], 16)
                sp.dma_start(sd[:, :], sd_in.rearrange("(o n) -> o n", o=1).broadcast_to([P, D])).then_inc(S["scale_in"], 16)
                load_rest(0)
                for s in range(1, NSTEP):
                    if s >= 2:
                        sp.wait_ge(S["merged"], 2 * (s - 1))
                    load_x(s)
                    load_rest(s)

            @block.gpsimd
            def _(pool):
                def merge(s):
                    pool.wait_ge(xt_in[s], 16)
                    for i in range(2):
                        tiles = sacc[:, TT * s + 2 * i:TT * s + 2 * i + 2, :]
                        pool.wait_ge(S["y_act"], 2 * s + i + 1)
                        pool.tensor_tensor(tiles, tiles, y[:, i, :].rearrange("p (t d) -> p t d", t=2), ALU.mult)\
                            .then_inc(S["gated"], 1)
                        pool.wait_ge(S["gated"], 2 * s + i + 1)
                        pool.tensor_tensor(tiles, tiles, xt[:, s % 2, 2 * i:2 * i + 2, :], ALU.add).then_inc(S["merged"], 1)

                for s in range(NSTEP):
                    for k in range(HT):
                        K = HT * s + k
                        pool.wait_ge(S["hid_hi"], K + 1)
                        pool.tensor_tensor(hid[:, k % 2, 1, :], act_g[:, k % 2, :], hid[:, k % 2, 0, :], ALU.subtract)\
                            .then_inc(S["hid_lo"], 1)
                        if s >= 1 and k == 2:
                            merge(s - 1)
                merge(NSTEP - 1)

            @block.scalar
            def _(act):
                def weights_hi(k):
                    for i in range(3):
                        act.wait_ge(S["converted"], 3 * k + i + 1)
                        act.activation(part(i, w[i][:, 0, :], k), part(i, rf[i][:, :], k), ACT.Copy).then_inc(S["w_hi"], 1)

                def sums(s):
                    for i in range(2):
                        act.wait_ge(S["y_ready"], 2 * s + i + 1)
                        act.activation(y[:, i, :], y[:, i, :], ACT.Silu).then_inc(S["y_act"], 1)

                weights_hi(0)
                weights_hi(1)
                act.wait_ge(S["scale_in"], 48)
                for s in range(NSTEP):
                    for k in range(HT):
                        K = HT * s + k
                        act.wait_ge(S["up_full"], K + 1)
                        if K >= 2:
                            act.wait_ge(S["hid_lo"], K - 1)
                        act.activation(act_g[:, k % 2, :], G[k % 2][:, :], ACT.Silu, scale=scale[:, k, 0:1])\
                           .then_inc(S["act_ready"], 1)
                        act.wait_ge(S["prod"], K + 1)
                        if K >= 2:
                            act.wait_ge(S["down_done"], K - 1)
                        act.activation(hid[:, k % 2, 0, :], act_g[:, k % 2, :], ACT.Copy).then_inc(S["hid_hi"], 1)
                        if s == 0 and k + 2 < HT:
                            weights_hi(k + 2)
                        if k == 0 and s >= 1:
                            sums(s - 1)
                sums(NSTEP - 1)

            @block.vector
            def _(dve):
                for i in range(2):
                    dve.memset(raw[i][:, :].rearrange("p (c n) -> p c n", c=KC)[:, :, HID:], 128)
                dve.memset(raw[2][HREST:, (HT - 1) * D:], 128)
                dve.memset(scale[HREST:, HT - 1, :], 0.0).then_inc(S["padded"], 1)
                dve.wait_ge(S["padded"], 1)

                def convert(k):
                    for i in range(3):
                        if k == 0:
                            dve.wait_ge(w_in[i], 16 if i < 2 else 32)
                        dve.tensor_scalar(part(i, rf[i][:, :], k), part(i, raw[i][:, :], k), -128.0, None, ALU.add)\
                           .then_inc(S["converted"], 1)

                def weights_lo(k):
                    for i in range(3):
                        dve.wait_ge(S["w_hi"], 3 * k + i + 1)
                        dve.tensor_tensor(part(i, w[i][:, 1, :], k), part(i, rf[i][:, :], k), part(i, w[i][:, 0, :], k),
                                          ALU.subtract).then_inc(S["w_lo"], 1)

                def sums(s):
                    dve.wait_ge(S["down_done"], (s + 1) * HT)
                    if s >= 1:
                        dve.wait_ge(S["merged"], 2 * s)
                    for i in range(2):
                        dve.tensor_tensor(y[:, i, :].rearrange("p (t d) -> p t d", t=2), Y[i][:, :].rearrange("p (t d) -> p t d", t=2),
                                          sd[:, :].unsqueeze(1).broadcast_to([P, 2, D]), ALU.mult).then_inc(S["y_ready"], 1)

                convert(0)
                convert(1)
                weights_lo(0)
                convert(2)
                weights_lo(1)
                dve.wait_ge(S["scale_in"], 48)
                for s in range(NSTEP):
                    for k in range(HT):
                        K = HT * s + k
                        dve.wait_ge(S["act_ready"], K + 1)
                        dve.scalar_tensor_tensor(out=act_g[:, k % 2, :], in0=U[k % 2][:, :], scalar=scale[:, k, 1:2],
                                                 in1=act_g[:, k % 2, :], op0=ALU.mult, op1=ALU.mult).then_inc(S["prod"], 1)
                        if s == 0 and k + 3 < HT:
                            convert(k + 3)
                        if s == 0 and k + 2 < HT:
                            weights_lo(k + 2)
                        if k == 0 and s >= 1:
                            sums(s - 1)
                sums(NSTEP - 1)

            @block.tensor
            def _(pe):
                def up(s, k):
                    K = HT * s + k
                    if K >= 2:
                        pe.wait_ge(S["prod"], K - 1)
                    if s == 0:
                        pe.wait_ge(S["w_lo"], 3 * k + 2)
                    for i, bank in ((0, G[k % 2]), (1, U[k % 2])):
                        for c in range(KC):
                            a = c * HT * P + k * P
                            m = product(pe, bank[:, :], (w[i][:, 0, a:a + P], w[i][:, 1, a:a + P]),
                                        (xs[:, s % 2, 0, c, :], xs[:, s % 2, 1, c, :]), c == 0, c == KC - 1)
                    m.then_inc(S["up_full"], 1)

                def down(s, k):
                    pe.wait_ge(S["hid_lo"], HT * s + k + 1)
                    if s == 0:
                        pe.wait_ge(S["w_lo"], 3 * k + 3)
                    if k == 0 and s >= 1:
                        pe.wait_ge(S["y_ready"], 2 * s)
                    for tt in range(TT):
                        o = Y[tt // 2][:, (tt % 2) * D:(tt % 2 + 1) * D]
                        hh, hl = (hid[:, k % 2, q, tt * P:(tt + 1) * P] for q in range(2))
                        wh, wl = (w[2][:, q, k * D:(k + 1) * D] for q in range(2))
                        pe.matmul(o, hh, wh, start=(k == 0 and tt % 2 == 0), stop=False, skip_group_check=True)
                        pe.matmul(o, hh, wl, start=False, stop=False, skip_group_check=True)
                        m = pe.matmul(o, hl, wh, start=False, stop=(k == HT - 1), skip_group_check=True)
                    m.then_inc(S["down_done"], 1)

                for s in range(NSTEP):
                    pe.wait_ge(x_in[s], 16)
                    for k in range(HT):
                        up(s, k)
                        if k >= 1:
                            down(s, k - 1)
                        elif s >= 1:
                            down(s - 1, HT - 1)
                down(NSTEP - 1, HT - 1)


def stage_attention1(nc, wqkv_in, wproj_in, norm_in, bproj_in, ident_in, xn_dram, x1, s1):
    TB = SEQ // P
    QK = 2 * D
    NPAIR = H1 // 2
    BLK = 8 * 144
    SLOT_JOBS = {0: ["S7"], 4: ["V"], 5: ["P0", "P1"], 7: ["S0", "T"], 8: ["S1"], 9: ["S2", "Q0"], 10: ["S3"],
                 11: ["Q1", "S4"], 12: ["S5"], 14: ["S6"]}
    ALL = sum(SLOT_JOBS.values(), [])
    ROW_JOBS, OUT_JOBS = ["T", "Q0", "Q1"], ["P0", "P1"]
    STEP_JOBS = {
        "ahead0": ["T", "Q0", "Q1", "V"] + [f"S{p}" for p in range(NPAIR - 1)], "ahead1": ROW_JOBS,
        "first": [j for j in ALL if j not in OUT_JOBS], "middle": ALL,
        "seventh": [j for j in ALL if j not in ROW_JOBS], "last": ["S7"] + OUT_JOBS, "behind": OUT_JOBS}
    NMID = BATCH - 3
    JM = len(ALL)
    FIRST_JOB = {"ahead0": 0, "ahead1": 11, "first": 14, "middle": 26, "seventh": 26 + NMID * JM,
                 "last": 37 + NMID * JM, "behind": 40 + NMID * JM}
    OWN = 2 * TB + 7
    with ExitStack() as ctx:
        n = Names(nc, ctx, "a1_")
        ident = n.sb("ident", [P, P])
        raw = n.sb("raw", [P, KC, 3 * D])
        rawp = n.sb("rawp", [P, KC, D])
        w = n.sb("w", [P, 2, KC, 3 * D], F32R)
        wp = n.sb("wp", [P, 2, KC, D], F32R)
        nw = n.sb("nw", [P, QK])
        nqk = n.sb("nqk", [P, D])
        bp = n.sb("bp", [P, D])
        mhalf = n.sb("mhalf", [P, TB])
        three_halves = n.sb("three_halves", [P, 64])
        xt = n.sb("x", [P, TB, D])
        stats, mv = n.sb("stats", [P, TB, 6]), n.sb("mv", [P, TB, 2])
        ve, rs, tmp = n.sb("ve", [P, TB]), n.sb("rs", [P, TB]), n.sb("tmp", [P, TB])
        xs = n.sb("xs", [P, 2, KC, SEQ], F32R)
        qk = n.sb("qk", [P, TB, QK])
        sqr = n.sb("sqr", [P, TB, QK])
        ss, rq, tq = n.sb("ss", [P, 64]), n.sb("rq", [P, 64]), n.sb("tq", [P, 64])
        stq = n.sb("stq", [P, TB, H1, 4, D1])
        stk = n.sb("stk", [P, TB, H1, 4, D1])
        stack = n.sb("stack", [P, NPAIR, 2 * SEQ], F32R)
        vc = n.sb("vc", [P, 2, TB * D], F32R)
        vp = n.sb("vp", [P, 2, TB, 2, BLK], F32R)
        pr = n.sb("pr", [P, 4, 2, SEQ])
        pt = n.sb("pt", [P, 2, 2, 512], F32R)
        ot = n.sb("ot", [P, 2, 2, SEQ], F32R)
        ROOT_BITS = float(0x5F3759DF - (1 << 22))
        nb, sm, ri = (n.sb(s, [P, 4, 2]) for s in ("nb", "sm", "ri"))
        PJ = [n.ps(f"job{i}") for i in range(2)]
        PS = [n.ps(f"score{i}") for i in range(2)]
        PT = [n.ps(f"turn{i}") for i in range(2)]
        PO = [n.ps(f"out{i}") for i in range(2)]
        job_free = [n.sem(f"job_free{i}") for i in range(2)]
        S = {s: n.sem(s) for s in (
            "const_in", "w_in", "w_hi", "w_lo", "mhalf_ready", "nqk_raw", "nqk_ready", "zeroed", "own", "stats_seen",
            "x_copied", "ve_ready", "rs_ready", "xn_ready", "job_full", "xs_hi", "v_hi", "sq_ready", "ms_ready", "rq_ready", "waited", "newton",
            "scaled", "weighted", "k_hi", "q_hi", "k_lo", "q_lo", "spread_hi", "spread_lo", "stored", "score_full",
            "max_ready", "exp_ready", "sum_inv", "norm_ready", "turn_full", "turn_free", "turn_hi", "pv_done", "out_hi",
            "out_free")}

        def job(kind, b, name):
            at = STEP_JOBS[kind].index(name)
            if kind == "middle":
                first = FIRST_JOB[kind] - JM
                return b * JM + (first + at + 1), b * (JM // 2) + (first // 2 + at // 2), at % 2
            at += FIRST_JOB[kind]
            return at + 1, at // 2, at % 2

        def slot_jobs(kind, u):
            return [j for j in SLOT_JOBS.get(u, []) if j in STEP_JOBS[kind]]

        def stack_job(kind, b, p):
            if p == NPAIR - 1:
                return job(kind, b, "S7")
            before = {"first": "ahead0", "middle": "middle", "seventh": "middle", "last": "seventh"}[kind]
            return job(before, b - 1, f"S{p}")

        def flow(step, engine):
            step("first", 0)
            with engine.Fori(1, 1 + NMID) as b:
                step("middle", b)
            step("seventh", BATCH - 2)
            step("last", BATCH - 1)
            step("behind", BATCH)

        def bc(ap, shape):
            return ap.broadcast_to(shape)

        def heads(buf, t, part):
            return bc(buf[:, t, part * D:(part + 1) * D].rearrange("p (h d) -> p h d", d=D1).unsqueeze(2), [P, H1, 2, D1])

        def spread(part, a):
            return (vp[:, part, :, a, :].rearrange("p t (e w) -> p t e w", w=144)[:, :, :, 0:D1],
                    vc[:, part, :].rearrange("p (t a e d) -> p t a e d", t=TB, a=2, d=D1)[:, :, a])

        with nc.Block() as block:
            @block.sync
            def _(sp):
                sp.dma_start(raw[:, :, :], wqkv_in.rearrange("(c p) n -> p c n", p=P)).then_inc(S["w_in"], 16)
                sp.dma_start(rawp[:, :, :], wproj_in.rearrange("(c p) n -> p c n", p=P)).then_inc(S["w_in"], 16)
                sp.dma_start(ident[:, :], ident_in).then_inc(S["const_in"], 16)
                sp.dma_start(nw[:, :], norm_in.broadcast_to([P, QK])).then_inc(S["const_in"], 16)
                sp.dma_start(bp[:, :], bproj_in.broadcast_to([P, D])).then_inc(S["const_in"], 16)

                def store(kind, b, batch):
                    _, before, bank = job(kind, b, "T")
                    sp.wait_ge(job_free[bank], before + 1)
                    sp.dma_start(xn_dram[bass.ds(batch, 1)].rearrange("o p s c n -> p (o s c n)"),
                                 xs[:, :, :, :].bitcast(F32).rearrange("p s c n -> p (s c n)")).then_inc(S["stored"], 16)

                store("ahead0", None, 0)
                store("ahead1", None, 1)
                store("first", 0, 2)
                with sp.Fori(1, 1 + NMID) as b:
                    store("middle", b, b + 2)
                sp.wait_ge(S["stored"], 16 * BATCH)

            @block.gpsimd
            def _(pool):
                pool.memset(mhalf[:, :], -0.5).then_inc(S["mhalf_ready"], 1)
                pool.memset(three_halves[:, :], 1.5).then_inc(S["mhalf_ready"], 1)
                pool.wait_ge(S["mhalf_ready"], 2)

                def copy_x(m):
                    pool.wait_ge(S["xs_hi"], m)
                    pool.sem_inc(S["waited"], 1)
                    pool.tensor_copy(xt[:, :, :], x1[:, bass.ds(m * TB, TB), :]).then_inc(S["x_copied"], 1)

                def pow_x(m):
                    pool.wait_ge(S["ve_ready"], m + 1)
                    pool.tensor_tensor(rs[:, :], ve[:, :], mhalf[:, :], ALU.pow).then_inc(S["rs_ready"], 1)

                def root_rms(m, i):
                    if i == 0:
                        pool.wait_ge(S["ms_ready"], m + 1)
                    k = m * 12 + 4 * i
                    pool.tensor_tensor(tq[:, :], rq[:, :], rq[:, :], ALU.mult).then_inc(S["newton"], 1)
                    pool.wait_ge(S["newton"], k + 1)
                    pool.tensor_tensor(tq[:, :], tq[:, :], ss[:, :], ALU.mult).then_inc(S["newton"], 1)
                    pool.wait_ge(S["newton"], k + 2)
                    pool.tensor_tensor(tq[:, :], three_halves[:, :], tq[:, :], ALU.subtract).then_inc(S["newton"], 1)
                    pool.wait_ge(S["newton"], k + 3)
                    pool.tensor_tensor(rq[:, :], rq[:, :], tq[:, :], ALU.mult).then_inc(S["newton"], 1)
                    pool.wait_ge(S["newton"], k + 4)
                    if i == 2:
                        pool.sem_inc(S["rq_ready"], 1)

                def weigh(m):
                    pool.wait_ge(S["scaled"], m + 1)
                    pool.tensor_tensor(qk[:, :, 0:D], qk[:, :, 0:D], bc(nqk[:, :].unsqueeze(1), [P, TB, D]), ALU.mult)\
                        .then_inc(S["weighted"], 1)

                def q_lo(m, t):
                    pool.wait_ge(S["q_hi"], m * TB + t + 1)
                    pool.tensor_tensor(stq[:, t, :, 1::2, :].bitcast(F32R), heads(qk, t, 0), stq[:, t, :, 0::2, :],
                                       ALU.subtract).then_inc(S["q_lo"], 1)

                def spread_lo(m, a, seen):
                    if seen is not None:
                        pool.wait_ge(S["pv_done"], seen)
                    pool.sem_inc(S["waited"], 1)
                    to, of = spread(1, a)
                    pool.tensor_copy(to, of).then_inc(S["spread_lo"], 1)

                def step(kind, b):
                    first, units = kind == "first", kind != "behind"
                    rows, nxt = "T" in STEP_JOBS[kind], "V" in STEP_JOBS[kind]
                    for u in range(H1 if units else 1):
                        if u >= 1 or not first:
                            pool.wait_ge(S["sum_inv"], b * H1 + u)
                            e = pr[:, (u - 1) % 4]
                            pool.tensor_tensor(e, e, bc(ri[:, (u - 1) % 4, :].unsqueeze(2), [P, 2, SEQ]), ALU.mult)\
                                .then_inc(S["norm_ready"], 1)
                        if nxt and u == 0:
                            root_rms(b + 1, 2)
                        if nxt and u == 2:
                            weigh(b + 1)
                        if rows and u == 1:
                            copy_x(b + 2)
                        if rows and u == 3:
                            pow_x(b + 2)
                        if units and u == 4:
                            spread_lo(b, 1, None if first else b * H1)
                        if nxt and u in (4, 5):
                            q_lo(b + 1, u - 4)
                        if nxt and u == 13:
                            pool.wait_ge(job_free[job(kind, b, "V")[2]], job(kind, b, "V")[1] + 1)
                            spread_lo(b + 1, 0, b * H1 + 8)
                        if rows and u == 14:
                            root_rms(b + 2, 0)
                        if rows and u == 15:
                            root_rms(b + 2, 1)

                pool.tensor_copy(xt[:, :, :], x1[:, 0:TB, :]).then_inc(S["x_copied"], 1)
                pow_x(0)
                pool.memset(vp[:, :, :, :, :].bitcast(F32), 0.0).then_inc(S["zeroed"], 1)
                copy_x(1)
                pool.wait_ge(S["const_in"], 48)
                pool.tensor_tensor(nqk[:, :], nw[:, 0:D], nw[:, D:QK], ALU.mult).then_inc(S["nqk_raw"], 1)
                pool.wait_ge(S["nqk_raw"], 1)
                pool.tensor_scalar(nqk[:, :], nqk[:, :], SCALE1, None, ALU.mult).then_inc(S["nqk_ready"], 1)
                pool.wait_ge(S["nqk_ready"], 1)
                for i in range(3):
                    root_rms(0, i)
                pow_x(1)
                weigh(0)
                for t in range(TB):
                    q_lo(0, t)
                pool.wait_ge(job_free[job("ahead0", 0, "V")[2]], job("ahead0", 0, "V")[1] + 1)
                pool.wait_ge(S["zeroed"], 1)
                spread_lo(0, 0, None)
                for i in range(2):
                    root_rms(1, i)
                flow(step, pool)

            @block.scalar
            def _(act):
                act.wait_ge(S["w_in"], 32)
                act.activation(w[:, 0, :, :], raw[:, :, :], ACT.Copy).then_inc(S["w_hi"], 1)
                act.activation(wp[:, 0, :, :], rawp[:, :, :], ACT.Copy).then_inc(S["w_hi"], 1)

                def job_out(kind, b, name, m):
                    full, _, bank = job(kind, b, name)
                    act.wait_ge(S["job_full"], full)
                    if name == "T":
                        if kind != "ahead0":
                            act.wait_ge(S["stored"], m * 16)
                        act.activation(xs[:, 0, :, :].rearrange("p c n -> p (c n)"), PJ[bank][:, :], ACT.Copy)\
                           .then_inc(S["xs_hi"], 1)
                    elif name == "V":
                        if kind != "ahead0":
                            act.wait_ge(S["spread_hi"], 2 * (m - 1))
                        act.activation(vc[:, 0, :], PJ[bank][:, :], ACT.Copy).then_inc(S["v_hi"], 1)
                    elif name[0] == "Q":
                        if kind != "ahead0":
                            act.wait_ge(S["ms_ready"], m)
                        act.activation(sqr[:, int(name[1]), :], PJ[bank][:, :], ACT.Square).then_inc(S["sq_ready"], 1)
                    elif name[0] == "S":
                        act.activation(stack[:, int(name[1]), :], PJ[bank][:, :], ACT.Copy).then_inc(job_free[bank], 1)

                def k_hi(m):
                    act.wait_ge(S["scaled"], m + 1)
                    for t in range(TB):
                        act.activation(stk[:, t, :, 0:2, :].bitcast(F32R), heads(qk, t, 1), ACT.Copy).then_inc(S["k_hi"], 1)

                def q_hi(m):
                    act.wait_ge(S["weighted"], m + 1)
                    for t in range(TB):
                        act.activation(stq[:, t, :, 0::2, :].bitcast(F32R), heads(qk, t, 0), ACT.Copy).then_inc(S["q_hi"], 1)

                def spread_hi(m, a, seen):
                    act.wait_ge(S["v_hi"], m + 1)
                    if seen is not None:
                        act.wait_ge(S["pv_done"], seen)
                    to, of = spread(0, a)
                    act.activation(to, of, ACT.Copy).then_inc(S["spread_hi"], 1)

                def out_hi(seen, a):
                    act.wait_ge(S["pv_done"], seen)
                    act.activation(ot[:, 0, a, :], PO[a][:, 0:SEQ], ACT.Copy).then_inc(S["out_hi"], 1)

                def step(kind, b):
                    first, units = kind == "first", kind != "behind"
                    nxt = "V" in STEP_JOBS[kind]
                    for u in range(H1 if units else 5):
                        if units:
                            act.wait_ge(S["max_ready"], b * H1 + u + 1)
                            if u >= 4 or not first:
                                act.wait_ge(S["turn_full"], b * H1 + u - 3)
                            for t in range(2):
                                i = act.activation(pr[:, u % 4, t, :], PS[u % 2][:, t * SEQ:(t + 1) * SEQ], ACT.Exp,
                                                   bias=nb[:, u % 4, t:t + 1], accum_out=sm[:, u % 4, t:t + 1])
                            i.then_inc(S["exp_ready"], 1)
                        if u == 4:
                            if not first:
                                out_hi(b * H1, 1)
                            if units:
                                spread_hi(b, 1, None)
                        for name in slot_jobs(kind, u):
                            job_out(kind, b, name, b + 2)
                        if (u >= 2 or not first) and (units or u < 2):
                            act.wait_ge(S["turn_full"], b * H1 + u - 1)
                            if u >= 4 or not first:
                                act.wait_ge(S["pv_done"], b * H1 + u - 3)
                            act.activation(pt[:, u % 2, 0, :], PT[u % 2][:, :], ACT.Copy).then_inc(S["turn_hi"], 1)
                        if nxt and u == 2:
                            k_hi(b + 1)
                        if nxt and u == 3:
                            q_hi(b + 1)
                        if u == 12:
                            out_hi(b * H1 + 8, 0)
                            if nxt:
                                spread_hi(b + 1, 0, None)

                for name in ("T", "Q0", "Q1", "V"):
                    job_out("ahead0", 0, name, 0)
                act.wait_ge(S["zeroed"], 1)
                spread_hi(0, 0, None)
                k_hi(0)
                q_hi(0)
                for p in range(NPAIR - 1):
                    job_out("ahead0", 0, f"S{p}", 0)
                for name in ROW_JOBS:
                    job_out("ahead1", 0, name, 1)
                flow(step, act)

            @block.vector
            def _(dve):
                def stats_x(m):
                    dve.wait_ge(S["x_copied"], m + 1)
                    k = norm_stats(dve, S["own"], S["stats_seen"], m * OWN, xt, stats, mv, ve[:, :], TB, LN_EPS)
                    dve.wait_ge(S["own"], k)
                    dve.sem_inc(S["ve_ready"], 1)

                def norm_x(m):
                    dve.wait_ge(S["rs_ready"], m + 1)
                    polish_rsqrt(dve, S["own"], m * OWN + 2 * TB + 1, rs[:, :], ve[:, :], tmp[:, :])
                    for t in range(TB):
                        i = dve.tensor_scalar(xt[:, t, :], xt[:, t, :], mv[:, t, 0:1], rs[:, t:t + 1], ALU.subtract, ALU.mult)
                    i.then_inc(S["xn_ready"], 1)

                def job_out(kind, b, name, m):
                    full, _, bank = job(kind, b, name)
                    if name == "T":
                        dve.wait_ge(S["xs_hi"], m + 1)
                        dve.tensor_tensor(xs[:, 1, :, :].rearrange("p c n -> p (c n)"), PJ[bank][:, :],
                                          xs[:, 0, :, :].rearrange("p c n -> p (c n)"), ALU.subtract).then_inc(job_free[bank], 1)
                    elif name == "V":
                        dve.wait_ge(S["v_hi"], m)
                        if kind != "ahead0":
                            dve.wait_ge(S["spread_lo"], 2 * (m - 1))
                        dve.tensor_tensor(vc[:, 1, :], PJ[bank][:, :], vc[:, 0, :], ALU.subtract).then_inc(job_free[bank], 1)
                    elif name[0] == "Q":
                        t = int(name[1])
                        dve.wait_ge(S["sq_ready"], m * TB + t + 1)
                        if kind != "ahead0" and t == 0:
                            dve.wait_ge(S["q_lo"], m * TB)
                            dve.wait_ge(S["k_lo"], m * TB)
                        dve.tensor_copy(qk[:, t, :], PJ[bank][:, :]).then_inc(job_free[bank], 1)
                    elif name[0] == "P":
                        t = int(name[1])
                        dve.wait_ge(S["job_full"], full)
                        dve.tensor_tensor(s1[:, bass.ds((b - 1) * TB + t, 1), :], PJ[bank][:, 0:D].unsqueeze(1),
                                          bp[:, :].unsqueeze(1), ALU.add).then_inc(job_free[bank], 1)

                def sum_squares(kind, b, m):
                    for name in ("Q0", "Q1"):
                        _, before, bank = job(kind, b, name)
                        dve.wait_ge(job_free[bank], before + 1)
                    dve.wait_ge(S["sq_ready"], (m + 1) * TB)
                    dve.tensor_reduce(ss[:, :], sqr[:, :, :].rearrange("p t (g d) -> p (t g) d", d=D1), AX.X, ALU.add)\
                       .then_inc(S["own"], 1)
                    dve.wait_ge(S["own"], m * OWN + 2 * TB + 6)
                    dve.tensor_scalar(ss[:, :], ss[:, :], 0.5 / D1, RMS_EPS / 2, ALU.mult, ALU.add).then_inc(S["own"], 1)
                    dve.wait_ge(S["own"], m * OWN + 2 * TB + 7)
                    dve.tensor_scalar(rq[:, :].bitcast(I32), ss[:, :].bitcast(I32), -0.5, ROOT_BITS, ALU.mult, ALU.add)\
                       .then_inc(S["ms_ready"], 1)

                def scale_rows(m):
                    dve.wait_ge(S["rq_ready"], m + 1)
                    dve.tensor_tensor(qk[:, :, :].rearrange("p t (g d) -> p (t g) d", d=D1),
                                      qk[:, :, :].rearrange("p t (g d) -> p (t g) d", d=D1),
                                      bc(rq[:, :].unsqueeze(2), [P, 64, D1]), ALU.mult).then_inc(S["scaled"], 1)

                def k_lo(m, t):
                    dve.wait_ge(S["k_hi"], m * TB + t + 1)
                    dve.tensor_tensor(stk[:, t, :, 2:4, :].bitcast(F32R), heads(qk, t, 1), stk[:, t, :, 0:2, :],
                                      ALU.subtract).then_inc(S["k_lo"], 1)

                def out_lo(count, a):
                    dve.wait_ge(S["out_hi"], count)
                    dve.tensor_tensor(ot[:, 1, a, :], PO[a][:, 0:SEQ], ot[:, 0, a, :], ALU.subtract).then_inc(S["out_free"], 1)

                def step(kind, b):
                    first, units = kind == "first", kind != "behind"
                    rows, nxt = "T" in STEP_JOBS[kind], "V" in STEP_JOBS[kind]
                    for u in range(H1 if units else 7):
                        if (u >= 1 or not first) and (units or u < 1):
                            dve.wait_ge(S["exp_ready"], b * H1 + u)
                            dve.reciprocal(ri[:, (u - 1) % 4, :], sm[:, (u - 1) % 4, :]).then_inc(S["sum_inv"], 1)
                        if units:
                            dve.wait_ge(S["score_full"], b * H1 + u + 1)
                            dve.tensor_reduce(nb[:, u % 4, :], PS[u % 2][:, :].rearrange("p (t k) -> p t k", t=2), AX.X,
                                              ALU.max, negate=True).then_inc(S["max_ready"], 1)
                        for name in slot_jobs(kind, u - 1):
                            job_out(kind, b, name, b + 2)
                        if (u >= 3 or not first) and (units or u < 3):
                            dve.wait_ge(S["turn_hi"], b * H1 + u - 2)
                            dve.tensor_tensor(pt[:, (u - 3) % 2, 1, :], PT[(u - 3) % 2][:, :], pt[:, (u - 3) % 2, 0, :],
                                              ALU.subtract).then_inc(S["turn_free"], 1)
                        if nxt and u in (3, 4):
                            k_lo(b + 1, u - 3)
                        if rows and u == 2:
                            stats_x(b + 2)
                        if u == 4 and not first:
                            out_lo(b * 2, 1)
                        if rows and u == 4:
                            norm_x(b + 2)
                        if rows and u == 13:
                            sum_squares(kind, b, b + 2)
                        if u == 13:
                            out_lo(b * 2 + 1, 0)
                        if nxt and u == 1:
                            scale_rows(b + 1)

                stats_x(0)
                dve.wait_ge(S["w_hi"], 2)
                dve.tensor_tensor(w[:, 1, :, :], raw[:, :, :], w[:, 0, :, :], ALU.subtract).then_inc(S["w_lo"], 1)
                norm_x(0)
                dve.tensor_tensor(wp[:, 1, :, :], rawp[:, :, :], wp[:, 0, :, :], ALU.subtract).then_inc(S["w_lo"], 1)
                dve.wait_ge(S["const_in"], 48)
                for name in ("T", "Q0", "Q1", "V"):
                    job_out("ahead0", 0, name, 1 if name == "V" else 0)
                sum_squares("ahead0", 0, 0)
                stats_x(1)
                scale_rows(0)
                for t in range(TB):
                    k_lo(0, t)
                norm_x(1)
                for name in ROW_JOBS:
                    job_out("ahead1", 0, name, 1)
                sum_squares("ahead1", 0, 1)
                flow(step, dve)

            @block.tensor
            def _(pe):
                pe.wait_ge(S["const_in"], 48)

                def do_job(kind, b, name, m):
                    full, before, bank = job(kind, b, name)
                    if kind != "ahead0" or before > 0:
                        pe.wait_ge(job_free[bank], before)
                    out = PJ[bank]
                    if name == "T":
                        pe.wait_ge(S["xn_ready"], m + 1)
                        for c in range(KC):
                            for t in range(TB):
                                i = pe.transpose(out[:, c * SEQ + t * P:c * SEQ + (t + 1) * P], xt[:, t, c * P:(c + 1) * P],
                                                 ident[:, :])
                    elif name[0] == "Q":
                        t = int(name[1])
                        if t == 0:
                            _, t_before, t_bank = job(kind, b, "T")
                            pe.wait_ge(job_free[t_bank], t_before + 1)
                        for c in range(KC):
                            i = product(pe, out[:, :], [xs[:, s, c, t * P:(t + 1) * P] for s in range(2)],
                                        [w[:, s, c, 0:QK] for s in range(2)], c == 0, c == KC - 1)
                    elif name == "V":
                        for t in range(TB):
                            for c in range(KC):
                                i = product(pe, out[:, t * D:(t + 1) * D], [xs[:, s, c, t * P:(t + 1) * P] for s in range(2)],
                                            [w[:, s, c, QK:QK + D] for s in range(2)], c == 0, c == KC - 1)
                    elif name[0] == "S":
                        p = int(name[1])
                        for k, rows in enumerate((stq, stk)):
                            for t in range(TB):
                                i = pe.transpose(out[:, k * SEQ + t * P:k * SEQ + (t + 1) * P],
                                                 rows[:, t, 2 * p:2 * p + 2, :, :].rearrange("p h r d -> p (h r d)"), ident[:, :])
                    else:
                        t = int(name[1])
                        if t == 0:
                            pe.wait_ge(S["out_free"], b * 2)
                        for a in range(2):
                            i = product(pe, out[:, 0:D], [ot[:, s, a, t * P:(t + 1) * P] for s in range(2)],
                                        [wp[:, s, a, :] for s in range(2)], a == 0, a == 1)
                    i.then_inc(S["job_full"], 1)

                def step(kind, b):
                    first, units = kind == "first", kind != "behind"

                    def values(r):
                        u = r % H1
                        a, e = u // 8, u % 8
                        pe.wait_ge(S["turn_free"], b * H1 + r + 1)
                        if e == 0:
                            pe.wait_ge(S["spread_hi"], b * 2 + a + 1)
                            pe.wait_ge(S["spread_lo"], b * 2 + a + 1)
                            if not first:
                                pe.wait_ge(S["out_free"], b * 2 + a - 1)
                        for kc in range(2):
                            m = product(pe, PO[a][:, 0:SEQ], [vp[:, s, kc, a, e * P:(e + 1) * P] for s in range(2)],
                                        [pt[:, u % 2, s, kc * SEQ:(kc + 1) * SEQ] for s in range(2)],
                                        e == 0 and kc == 0, e == 7 and kc == 1)
                        m.then_inc(S["pv_done"], 1)

                    def scores(r):
                        u = r % H1
                        p, at = u // 2, 64 * (u % 2)
                        if r >= 2 or not first:
                            pe.wait_ge(S["exp_ready"], b * H1 + r - 1)
                        if u % 2 == 0:
                            _, before, bank = job(kind, b, "S0") if r == H1 else stack_job(kind, b, p)
                            pe.wait_ge(job_free[bank], before + 1)
                        for t in range(2):
                            m = pe.matmul(PS[u % 2][:, t * SEQ:(t + 1) * SEQ], stack[at:at + 64, p, t * P:(t + 1) * P],
                                          stack[at:at + 64, p, SEQ:2 * SEQ], start=True, stop=True)
                        m.then_inc(S["score_full"], 1)

                    if first:
                        scores(0)
                    for u in range(H1 if units else 6):
                        if units and (u + 1 < H1 or "S0" in STEP_JOBS[kind]):
                            scores(u + 1)
                        for name in slot_jobs(kind, u):
                            if name == "S0":
                                pe.wait_ge(S["q_lo"], (b + 2) * TB)
                                pe.wait_ge(S["k_lo"], (b + 2) * TB)
                            if name[0] != "P":
                                do_job(kind, b, name, b + 2)
                        if (u >= 4 or not first) and (units or u < 4):
                            values(u - 4)
                        if (u >= 2 or not first) and (units or u < 2):
                            pe.wait_ge(S["norm_ready"], b * H1 + u - 1)
                            if u >= 4 or not first:
                                pe.wait_ge(S["turn_free"], b * H1 + u - 3)
                            for kc in range(2):
                                for t in range(2):
                                    m = pe.transpose(PT[u % 2][:, kc * SEQ + t * P:kc * SEQ + (t + 1) * P],
                                                     pr[:, (u - 2) % 4, t, kc * P:(kc + 1) * P], ident[:, :])
                            m.then_inc(S["turn_full"], 1)
                        for name in slot_jobs(kind, u):
                            if name[0] == "P":
                                do_job(kind, b, name, b + 2)

                do_job("ahead0", 0, "T", 0)
                pe.wait_ge(S["w_lo"], 2)
                for name in STEP_JOBS["ahead0"][1:]:
                    if name == "S0":
                        pe.wait_ge(S["q_lo"], TB)
                        pe.wait_ge(S["k_lo"], TB)
                    do_job("ahead0", 0, name, 0)
                for name in ROW_JOBS:
                    do_job("ahead1", 0, name, 1)
                flow(step, pe)


def stage_moe(nc, a, xn_dram, x1, s1, out):
    ROUT = ME * P
    NSH = MT - ME
    ORDER = list(range(ME, MT)) + list(range(ME))
    OWN = 17
    with ExitStack() as ctx:
        n = Names(nc, ctx, "m_")
        ident = n.sb("ident", [P, P])
        raw = [n.sb(f"raw{i}", [P, MT * D]) for i in range(3)]
        w = [n.sb(f"w{i}", [P, 2, MT * D], F32R) for i in range(3)]
        rr, rw = n.sb("rr", [P, KC, E]), n.sb("rw", [P, 2, KC, E], F32R)
        sel_raw, sel = n.sb("sel_raw", [2 * E, ROUT]), n.sb("sel", [2 * E, ROUT], F32R)
        rank = n.sb("rank", [P, E])
        bias = n.sb("bias", [P, MT, 2])
        db = n.sb("db", [P, D])
        xs = n.sb("xs", [P, 2, 2, KC, STEP], F32R)
        lt = n.sb("lt", [E, STEP])
        lg, eq, oh, oh2 = (n.sb(s, [P, TT, E]) for s in ("lg", "eq", "oh", "oh2"))
        m1 = n.sb("m1", [P, TT])
        cm = n.sb("cm", [P, TT, 2, E])
        ct = n.sb("ct", [2 * E, STEP], F32R)
        g = n.sb("g", [P, 2, STEP])
        hid = n.sb("hid", [P, 2, 2, STEP], F32R)
        y = n.sb("y", [P, 2, 2 * D])
        G = [n.ps(f"gate{i}") for i in range(2)]
        U = [n.ps(f"up{i}") for i in range(2)]
        C = [n.ps(f"comb{i}") for i in range(2)]
        Y = [n.ps(f"down{i}") for i in range(2)]
        S = {s: n.sem(s) for s in ("const_in", "shared_in", "routed_in", "w_hi", "w_lo", "rw_hi", "rw_lo", "sel_ready", "zeroed", "own",
                                   "x_in0", "x_in1", "logits", "lt_ready", "lt_turned", "lg_ready", "exp_ready", "cm_hi",
                                   "cm_ready", "cm_lo", "ct_turned", "ct_ready", "up_full", "act_ready", "prod", "comb_read",
                                   "hid_hi", "hid_lo", "down_done", "y_ready", "y_act", "gated", "merged", "stored")}

        def tile_of(i, k):
            t = ORDER[k]
            if i == 2:
                return lambda row: row[:, t * D:(t + 1) * D]
            return lambda row: row.rearrange("p (c n) -> p c n", c=KC)[:, :, t * P:(t + 1) * P]

        with nc.Block() as block:
            @block.sync
            def _(sp):
                def load_x(s):
                    for half in range(2):
                        sp.dma_start(xs[:, s % 2, :, :, half * SEQ:(half + 1) * SEQ].bitcast(F32),
                                     xn_dram[2 * s + half]).then_inc(S[f"x_in{s % 2}"], 16)

                gate, up = (raw[i][:, :].rearrange("p (c n) -> p c n", c=KC) for i in range(2))
                down = raw[2][:, :].rearrange("p (t n) -> p t n", t=MT)
                sp.dma_start(gate[:, :, ROUT:MW], a["s_gate"].rearrange("(c p) n -> p c n", p=P)).then_inc(S["shared_in"], 16)
                sp.dma_start(up[:, :, ROUT:MW], a["s_up"].rearrange("(c p) n -> p c n", p=P)).then_inc(S["shared_in"], 16)
                sp.dma_start(down[:, ME:MT - 1, :], a["s_down"][0:(NSH - 1) * P, :].rearrange("(t p) n -> p t n", p=P))\
                  .then_inc(S["shared_in"], 16)
                sp.dma_start(down[0:MREST, MT - 1, :], a["s_down"][(NSH - 1) * P:SI, :]).then_inc(S["shared_in"], 16)
                load_x(0)
                sp.wait_ge(S["zeroed"], 1)
                sp.dma_start(bias[:, ME:MT - 1, :], a["bias"]).then_inc(S["const_in"], 16)
                sp.dma_start(bias[0:MREST, MT - 1, :], a["bias_rest"]).then_inc(S["const_in"], 16)
                sp.dma_start(ident[:, :], a["ident"]).then_inc(S["const_in"], 16)
                sp.dma_start(rr[:, :, :], a["router"].rearrange("(c p) e -> p c e", p=P)).then_inc(S["const_in"], 16)
                sp.dma_start(sel_raw[:, :], a["select"]).then_inc(S["const_in"], 16)
                sp.dma_start(rank[:, :], a["rank"].broadcast_to([P, E])).then_inc(S["const_in"], 16)
                sp.dma_start(db[:, :], a["down_b"].broadcast_to([P, D])).then_inc(S["const_in"], 16)
                sp.dma_start(gate[:, :, 0:ROUT], a["gate"].rearrange("(c p) n -> p c n", p=P)).then_inc(S["routed_in"], 16)
                sp.dma_start(up[:, :, 0:ROUT], a["up"].rearrange("(c p) n -> p c n", p=P)).then_inc(S["routed_in"], 16)
                sp.dma_start(down[:, 0:ME, :], a["down"].rearrange("(t p) n -> p t n", p=P)).then_inc(S["routed_in"], 16)
                load_x(1)
                for s in range(NSTEP):
                    if s + 2 < NSTEP:
                        sp.wait_ge(S["up_full"], (s + 1) * MT)
                        load_x(s + 2)
                for s in range(NSTEP):
                    sp.wait_ge(S["merged"], 2 * s + 2)
                    sp.dma_start(out[s].rearrange("(t p) d -> p t d", p=P), x1[:, s * TT:(s + 1) * TT, :]).then_inc(S["stored"], 16)
                sp.wait_ge(S["stored"], 16 * NSTEP)

            @block.gpsimd
            def _(pool):
                def merge(s):
                    for i in range(2):
                        pool.wait_ge(S["y_act"], 2 * s + i + 1)
                        yy = y[:, i, :].rearrange("p (t d) -> p t d", t=2)
                        tiles = slice(s * TT + 2 * i, s * TT + 2 * i + 2)
                        pool.tensor_tensor(yy, yy, s1[:, tiles, :], ALU.mult).then_inc(S["gated"], 1)
                        pool.wait_ge(S["gated"], 2 * s + i + 1)
                        pool.tensor_tensor(x1[:, tiles, :], x1[:, tiles, :], yy, ALU.add).then_inc(S["merged"], 1)

                for s in range(NSTEP):
                    for k in range(MT):
                        pool.wait_ge(S["hid_hi"], s * MT + k + 1)
                        pool.tensor_tensor(hid[:, k % 2, 1, :], g[:, k % 2, :], hid[:, k % 2, 0, :], ALU.subtract)\
                            .then_inc(S["hid_lo"], 1)
                        if s >= 1 and k == 2:
                            merge(s - 1)
                merge(NSTEP - 1)

            @block.scalar
            def _(act):
                def weights_hi(k):
                    if k in (0, NSH):
                        act.wait_ge(S["shared_in" if k == 0 else "routed_in"], 64 if k == 0 else 48)
                    if k == 0:
                        act.wait_ge(S["zeroed"], 2)
                    for i in range(3):
                        part = tile_of(i, k)
                        act.activation(part(w[i][:, 0, :]), part(raw[i][:, :]), ACT.Copy).then_inc(S["w_hi"], 1)

                weights_hi(0)
                act.wait_ge(S["const_in"], 112)
                act.activation(rw[:, 0, :, :], rr[:, :, :], ACT.Copy).then_inc(S["rw_hi"], 1)
                weights_hi(1)
                act.activation(sel[:, :], sel_raw[:, :], ACT.Copy).then_inc(S["sel_ready"], 1)

                def sums(s):
                    for i in range(2):
                        act.wait_ge(S["y_ready"], 2 * s + i + 1)
                        act.activation(y[:, i, :], y[:, i, :], ACT.Silu).then_inc(S["y_act"], 1)

                for s in range(NSTEP):
                    for k in range(MT):
                        K = s * MT + k
                        if k == NSH:
                            act.wait_ge(S["ct_turned"], s + 1)
                            act.activation(ct[:, :], C[0][0:2 * E, :], ACT.Copy).then_inc(S["ct_ready"], 1)
                        act.wait_ge(S["up_full"], K + 1)
                        if K >= 2:
                            act.wait_ge(S["hid_lo"], K - 1)
                        act.activation(g[:, k % 2, :], G[k % 2][:, :], ACT.Silu, bias=bias[:, ORDER[k], 0:1])\
                           .then_inc(S["act_ready"], 1)
                        if k == 0:
                            act.wait_ge(S["logits"], s + 1)
                            act.activation(lt[:, :], C[1][0:E, :], ACT.Copy).then_inc(S["lt_ready"], 1)
                        act.wait_ge(S["comb_read"], K + 1)
                        if K >= 2:
                            act.wait_ge(S["down_done"], K - 1)
                        act.activation(hid[:, k % 2, 0, :], g[:, k % 2, :], ACT.Copy).then_inc(S["hid_hi"], 1)
                        if s == 0 and k + 2 < MT:
                            weights_hi(k + 2)
                        if k == 0 and s >= 1:
                            sums(s - 1)
                        if k == 1:
                            act.wait_ge(S["lg_ready"], s + 1)
                            act.activation(lg[:, :, :], lg[:, :, :], ACT.Exp).then_inc(S["exp_ready"], 1)
                        if k == NSH - 1:
                            act.wait_ge(S["cm_hi"], s + 1)
                            act.activation(cm[:, :, 0, :].bitcast(F32R), oh[:, :, :], ACT.Copy).then_inc(S["cm_ready"], 1)
                sums(NSTEP - 1)

            @block.vector
            def _(dve):
                dve.memset(bias[:, :, :], 0.0).then_inc(S["zeroed"], 1)
                for i in range(2):
                    dve.memset(raw[i][:, :].rearrange("p (c n) -> p c n", c=KC)[:, :, MW:], 0.0)
                dve.memset(raw[2][MREST:P, (MT - 1) * D:], 0.0).then_inc(S["zeroed"], 1)

                def weights_lo(k):
                    for i in range(3):
                        dve.wait_ge(S["w_hi"], 3 * k + i + 1)
                        part = tile_of(i, k)
                        dve.tensor_tensor(part(w[i][:, 1, :]), part(raw[i][:, :]), part(w[i][:, 0, :]), ALU.subtract)\
                           .then_inc(S["w_lo"], 1)

                weights_lo(0)
                dve.wait_ge(S["rw_hi"], 1)
                dve.tensor_tensor(rw[:, 1, :, :], rr[:, :, :], rw[:, 0, :, :], ALU.subtract).then_inc(S["rw_lo"], 1)
                weights_lo(1)
                dve.wait_ge(S["const_in"], 112)

                def rows(ap):
                    return ap.unsqueeze(2).broadcast_to([P, TT, E])

                ranks = rank[:, :].unsqueeze(1).broadcast_to([P, TT, E])

                def routing(s, part):
                    def own(k, i):
                        i.then_inc(S["own"], 1)
                        dve.wait_ge(S["own"], s * OWN + k)

                    logits = C[0][:, 0:TT * E].rearrange("p (t e) -> p t e", e=E)
                    if part == 0:
                        dve.wait_ge(S["lt_turned"], s + 1)
                        own(1, dve.tensor_reduce(m1[:, :], logits, AX.X, ALU.max))
                        dve.tensor_tensor(lg[:, :, :], logits, rows(m1[:, :]), ALU.subtract).then_inc(S["lg_ready"], 1)
                    elif part == 1:
                        dve.wait_ge(S["exp_ready"], s + 1)
                        own(2, dve.tensor_reduce(m1[:, :], lg[:, :, :], AX.X, ALU.max))
                        own(3, dve.tensor_tensor(eq[:, :, :], lg[:, :, :], rows(m1[:, :]), ALU.is_equal))
                        own(4, dve.tensor_tensor(eq[:, :, :], eq[:, :, :], ranks, ALU.mult))
                        own(5, dve.tensor_reduce(m1[:, :], eq[:, :, :], AX.X, ALU.max))
                        own(6, dve.tensor_tensor(oh[:, :, :], eq[:, :, :], rows(m1[:, :]), ALU.is_equal))
                        own(7, dve.scalar_tensor_tensor(out=eq[:, :, :], in0=oh[:, :, :], scalar=-2.0, in1=lg[:, :, :],
                                                        op0=ALU.mult, op1=ALU.add))
                        own(8, dve.tensor_reduce(m1[:, :], eq[:, :, :], AX.X, ALU.max))
                        own(9, dve.tensor_tensor(eq[:, :, :], eq[:, :, :], rows(m1[:, :]), ALU.is_equal))
                    elif part == 2:
                        own(10, dve.tensor_tensor(eq[:, :, :], eq[:, :, :], ranks, ALU.mult))
                        own(11, dve.tensor_reduce(m1[:, :], eq[:, :, :], AX.X, ALU.max))
                        own(12, dve.tensor_tensor(oh2[:, :, :], eq[:, :, :], rows(m1[:, :]), ALU.is_equal))
                        own(13, dve.tensor_tensor(oh2[:, :, :], oh2[:, :, :], oh[:, :, :], ALU.add))
                        own(14, dve.tensor_tensor(oh2[:, :, :], oh2[:, :, :], lg[:, :, :], ALU.mult))
                        own(15, dve.tensor_reduce(m1[:, :], oh2[:, :, :], AX.X, ALU.add))
                        own(16, dve.reciprocal(m1[:, :], m1[:, :]))
                        dve.tensor_tensor(oh[:, :, :], oh2[:, :, :], rows(m1[:, :]), ALU.mult).then_inc(S["cm_hi"], 1)
                    else:
                        dve.wait_ge(S["cm_ready"], s + 1)
                        dve.tensor_tensor(cm[:, :, 1, :].bitcast(F32R), oh[:, :, :], cm[:, :, 0, :], ALU.subtract)\
                           .then_inc(S["cm_lo"], 1)
                        dve.wait_ge(S["cm_lo"], s + 1)
                        dve.sem_inc(S["own"], 1)

                def sums(s):
                    dve.wait_ge(S["down_done"], (s + 1) * MT)
                    if s >= 1:
                        dve.wait_ge(S["merged"], 2 * s)
                    for i in range(2):
                        dve.tensor_tensor(y[:, i, :].rearrange("p (t d) -> p t d", t=2), Y[i][:, :].rearrange("p (t d) -> p t d", t=2),
                                          db[:, :].unsqueeze(1).broadcast_to([P, 2, D]), ALU.add).then_inc(S["y_ready"], 1)

                for s in range(NSTEP):
                    for k in range(MT):
                        K = s * MT + k
                        if k == NSH - 1:
                            routing(s, 1)
                        dve.wait_ge(S["act_ready"], K + 1)
                        i = dve.scalar_tensor_tensor(out=g[:, k % 2, :], in0=U[k % 2][:, :], scalar=bias[:, ORDER[k], 1:2],
                                                     in1=g[:, k % 2, :], op0=ALU.add, op1=ALU.mult)
                        if k >= NSH:
                            i.then_inc(S["prod"], 1)
                            dve.wait_ge(S["prod"], s * ME + k - NSH + 1)
                            i = dve.tensor_tensor(g[:, k % 2, :], g[:, k % 2, :], C[k % 2][:, :], ALU.mult)
                        i.then_inc(S["comb_read"], 1)
                        if s == 0 and k + 2 < MT:
                            weights_lo(k + 2)
                        if k == 0 and s >= 1:
                            sums(s - 1)
                        if k == 1:
                            routing(s, 0)
                        if k == NSH - 1:
                            routing(s, 2)
                            routing(s, 3)
                sums(NSTEP - 1)

            @block.tensor
            def _(pe):
                def up(s, k):
                    K = s * MT + k
                    if K >= 2:
                        pe.wait_ge(S["comb_read"], K - 1)
                    if s == 0:
                        pe.wait_ge(S["w_lo"], 3 * k + 2)
                    for i, bank in ((0, G[k % 2]), (1, U[k % 2])):
                        for c in range(KC):
                            a_ = c * (MT * P) + ORDER[k] * P
                            m = product(pe, bank[:, :], [w[i][:, q, a_:a_ + P] for q in range(2)],
                                        [xs[:, s % 2, q, c, :] for q in range(2)], c == 0, c == KC - 1)
                    return m

                def combine(k):
                    return pe.matmul(C[k % 2][:, :], sel[:, ORDER[k] * P:(ORDER[k] + 1) * P], ct[:, :], start=True, stop=True)

                def down(s, k):
                    K = s * MT + k
                    pe.wait_ge(S["hid_lo"], K + 1)
                    if s == 0:
                        pe.wait_ge(S["w_lo"], 3 * k + 3)
                    if k == 0 and s >= 1:
                        pe.wait_ge(S["y_ready"], 2 * s)
                    for tt in range(TT):
                        o = Y[tt // 2][:, (tt % 2) * D:(tt % 2 + 1) * D]
                        hh, hl = (hid[:, k % 2, q, tt * P:(tt + 1) * P] for q in range(2))
                        wh, wl = (w[2][:, q, ORDER[k] * D:(ORDER[k] + 1) * D] for q in range(2))
                        pe.matmul(o, hh, wh, start=(k == 0 and tt % 2 == 0), stop=False, skip_group_check=True)
                        pe.matmul(o, hh, wl, start=False, stop=False, skip_group_check=True)
                        m = pe.matmul(o, hl, wh, start=False, stop=(k == MT - 1), skip_group_check=True)
                    m.then_inc(S["down_done"], 1)

                def down_before(s, k):
                    if k >= 1:
                        down(s, k - 1)
                    elif s >= 1:
                        down(s - 1, MT - 1)

                for s in range(NSTEP):
                    pe.wait_ge(S[f"x_in{s % 2}"], 32 * (s // 2 + 1))
                    for k in range(MT):
                        m = up(s, k)
                        if k < NSH:
                            m.then_inc(S["up_full"], 1)
                        if k == 0:
                            if s == 0:
                                pe.wait_ge(S["const_in"], 112)
                                pe.wait_ge(S["rw_lo"], 1)
                            else:
                                pe.wait_ge(S["comb_read"], s * MT)
                            for c in range(KC):
                                m = product(pe, C[1][0:E, :], [rw[:, q, c, :] for q in range(2)],
                                            [xs[:, s % 2, q, c, :] for q in range(2)], c == 0, c == KC - 1)
                            m.then_inc(S["logits"], 1)
                        if k == 1:
                            pe.wait_ge(S["lt_ready"], s + 1)
                            for t in range(TT):
                                m = pe.transpose(C[0][:, t * E:(t + 1) * E], lt[:, t * P:(t + 1) * P], ident[0:E, 0:E])
                            m.then_inc(S["lt_turned"], 1)
                        if k == NSH:
                            pe.wait_ge(S["cm_lo"], s + 1)
                            for t in range(TT):
                                m = pe.transpose(C[0][0:2 * E, t * P:(t + 1) * P], cm[:, t, :, :].rearrange("p s e -> p (s e)"), ident[:, :])
                            m.then_inc(S["ct_turned"], 1)
                            down_before(s, k)
                            pe.wait_ge(S["ct_ready"], s + 1)
                            if s == 0:
                                pe.wait_ge(S["sel_ready"], 1)
                        if k >= NSH:
                            combine(k).then_inc(S["up_full"], 1)
                        if k != NSH:
                            down_before(s, k)
                down(NSTEP - 1, MT - 1)




def program(nc, a, out):
    xn0 = nc.dram_tensor("xn0_scratch", [NSTEP, P, 2, KC, STEP], F32, kind="Internal").ap()
    xn1 = nc.dram_tensor("xn1_scratch", [BATCH, P, 2, KC, SEQ], F32, kind="Internal").ap()
    with nc.sbuf_tensor("x1", [P, NT, D], F32) as x1:
        with ExitStack() as ctx:
            shared = Shared0(nc, ctx)
            stage_norm0(nc, a["x"], a["ident"], a["w0"], a["rope"], shared, xn0)
            stage_attention0(nc, a["w0"], shared, xn0, x1)
        stage_ffn0(nc, a["x"], a["wg"], a["wu"], a["wd"], a["scale"], a["scale_rest"], a["sd"], xn0, x1)
        with nc.sbuf_tensor("s1", [P, NT, D], F32) as s1:
            stage_attention1(nc, a["w_qkv"], a["w_proj"], a["norm_w"], a["b_proj"], a["ident"], xn1, x1, s1)
            stage_moe(nc, a, xn1, x1, s1, out)


def rope_tables():
    import numpy as np
    freq = (np.float32(1.0) / np.float32(10000.0) ** (np.arange(0, DR, 2, dtype=np.float32) / np.float32(DR))).astype(np.float32)
    angle = (np.arange(SEQ, dtype=np.float32)[None, :] * freq[:, None]).astype(np.float32)
    cos, sin = (np.tile(f(angle.astype(np.float64)), (HG, 2)) for f in (np.cos, np.sin))
    more = math.sqrt(DN / DR)
    return np.ascontiguousarray(np.stack([cos * more, sin * more, cos, sin], axis=1).astype(np.float32))


def group_weights(wq, wk, wv, wo):
    import numpy as np
    groups = []
    for g in range(NG):
        cols = []
        for w in (wq, wk, wv):
            rows = w[g * HG * DN:(g + 1) * HG * DN]
            cols.append(rows.T.reshape(KC, P, HG * DN).transpose(1, 0, 2).reshape(P, -1))
        for w in (wq, wk):
            rows = w[H * DN + g * HG * DR:H * DN + (g + 1) * HG * DR].reshape(HG, 2, HALF, D)
            rows = rows.transpose(1, 0, 2, 3).reshape(2 * HG * HALF, D)
            cols.append(rows.T.reshape(KC, P, 2 * P).transpose(1, 0, 2).reshape(P, -1))
        cols.append(wo[:, g * HG * DV:(g + 1) * HG * DV].T.reshape(HG, DV, D).transpose(1, 0, 2).reshape(P, -1))
        groups.append(np.concatenate(cols, axis=1))
    return np.ascontiguousarray(np.stack(groups))


def kernel(**inputs):
    import numpy as _np
    import concourse.bacc as _bacc
    from concourse import mybir as _mybir
    from concourse.bass_utils import run_bass_kernel_spmd as _run

    i = {k: _np.asarray(v) for k, v in inputs.items()}
    scales = _np.stack([i["L0_ffn_s_gate"], i["L0_ffn_s_up"]], axis=1)
    shared = _np.stack([i["L1_ffn_s_gate_b"], i["L1_ffn_s_up_b"]], axis=1)
    data = {
        "x": i["L0_attn_hidden_states"].reshape(NTOK, D),
        "ident": _np.eye(P, dtype=_np.float32),
        "rope": rope_tables(),
        "w0": group_weights(i["L0_attn_Wq"], i["L0_attn_Wk"], i["L0_attn_Wv"], i["L0_attn_Wo"]),
        "wg": i["L0_ffn_wq_gate"].T, "wu": i["L0_ffn_wq_up"].T, "wd": i["L0_ffn_wq_down"].T,
        "scale": scales[0:(HT - 1) * P].reshape(HT - 1, P, 2).transpose(1, 0, 2), "scale_rest": scales[(HT - 1) * P:],
        "sd": i["L0_ffn_s_down"],
        "w_qkv": i["L1_attn_w_qkv"].T, "w_proj": i["L1_attn_w_proj"].T,
        "norm_w": _np.concatenate([_np.tile(i["L1_attn_q_norm_w"], H1), _np.tile(i["L1_attn_k_norm_w"], H1)])[None],
        "b_proj": i["L1_attn_b_proj"][None],
        "router": i["L1_ffn_router_w"].T,
        "gate": i["L1_ffn_gate_w"].transpose(1, 0, 2).reshape(D, E * I1),
        "up": i["L1_ffn_up_w"].transpose(1, 0, 2).reshape(D, E * I1),
        "down": i["L1_ffn_down_w"].reshape(E * I1, D),
        "s_gate": i["L1_ffn_s_gate_w"], "s_up": i["L1_ffn_s_up_w"], "s_down": i["L1_ffn_s_down_w"],
        "bias": shared[0:2 * P].reshape(2, P, 2).transpose(1, 0, 2), "bias_rest": shared[2 * P:],
        "down_b": i["L1_ffn_s_down_b"][None],
        "rank": (E - _np.arange(E, dtype=_np.float32))[None],
        "select": _np.tile(_np.repeat(_np.eye(E, dtype=_np.float32), I1, axis=1), (2, 1)),
    }
    nc = _bacc.Bacc("TRN2", target_bir_lowering=False, num_devices=1)
    arrays, args = {}, {}
    for name, value in data.items():
        arrays["in_" + name] = _np.ascontiguousarray(value)
        args[name] = nc.dram_tensor("in_" + name, value.shape, _mybir.dt.from_np(value.dtype), kind="ExternalInput").ap()
    out = nc.dram_tensor("out_x", (NSTEP, STEP, D), F32, kind="ExternalOutput").ap()
    program(nc, args, out)
    r = _run(nc, [arrays], core_ids=[0])
    return r.results[0]["out_x"].reshape(BATCH, SEQ, D)
```
